# Optimizing a Trainium2 kernel written in Bass

```python
import numpy as np
import jax
import jax.numpy as jnp

def _softmax(x, axis=-1):
    return jax.nn.softmax(x, axis=axis)

def _gelu(x):
    return jax.nn.gelu(x, approximate=True)

def _silu(x):
    return jax.nn.silu(x)

def _sigmoid(x):
    return jax.nn.sigmoid(x)

def _layernorm(x, axis=-1, eps=1e-05):
    m = jnp.mean(x, axis=axis, keepdims=True)
    v = jnp.var(x, axis=axis, keepdims=True)
    return (x - m) / jnp.sqrt(v + eps)

def _scatter_add(tgt, idx, src, axis=0):
    return tgt.at[idx].add(src)

def _segment_sum(src, seg, n):
    return jax.ops.segment_sum(src, seg, n)
kernel_name = 'mk_perceiver_d2_seqx_r4_f095db'

def setup_inputs(seed: int=0):
    np.random.seed(seed)
    _w = jnp.asarray

    def _rec_inputs():
        import jax
        import jax.numpy as jnp
        _rk = jax.random.key(seed)
        x = -0.0002928 + 1 * jax.random.normal(jax.random.fold_in(_rk, 1), (64, 64, 256), jnp.float32)
        _lenS = 64 - jax.random.randint(jax.random.fold_in(_rk, 7), (64,), 0, max(1, 64 // 4) + 1, jnp.int32)
        _lenS2 = 256 - jax.random.randint(jax.random.fold_in(_rk, 8), (64,), 0, max(1, 256 // 4) + 1, jnp.int32)
        _ctx_1024P = jax.random.normal(jax.random.fold_in(_rk, 11), (64, 16, 256), jnp.float32)
        _ctx_1024c = jax.random.dirichlet(jax.random.fold_in(_rk, 511), 0.3 * jnp.ones((16,), jnp.float32), (64, 256))
        _ctx_1024t = jnp.einsum('bsk,bkd->bsd', _ctx_1024c, _ctx_1024P)
        _ctx_1024t = _ctx_1024t * jax.lax.rsqrt(jnp.mean(jnp.square(_ctx_1024t)) + 1e-12) * 0.953939
        ctx_1024 = -1.39393e-06 + 0.999914 * (_ctx_1024t + 0.3 * jax.random.normal(jax.random.fold_in(_rk, 611), (64, 256, 256), jnp.float32))
        fside_Bx16xSxS2_0 = 9.80324e-06 + 0.100009 * jax.random.normal(jax.random.fold_in(_rk, 12), (64, 16, 64, 256), jnp.float32)
        fside_SxS2_0 = -2.64403e-05 + 0.100002 * jax.random.normal(jax.random.fold_in(_rk, 14), (64, 256), jnp.float32)
        _validS = jnp.arange(64)[None, :] < _lenS[:, None]
        _validS2 = jnp.arange(256)[None, :] < _lenS2[:, None]
        _causal = jnp.tril(jnp.ones((64, 64), dtype=bool))
        mask_BxS2_bf0 = jnp.logical_not(jnp.ones((64, 256), dtype=bool))
        return (x, ctx_1024, fside_Bx16xSxS2_0, fside_SxS2_0, mask_BxS2_bf0)
    x, ctx_1024, fside_Bx16xSxS2_0, fside_SxS2_0, mask_BxS2_bf0 = _rec_inputs()

    def _L0_xattn_setup():
        import jax, jax.numpy as jnp
        import numpy as np
        E = 256
        H = 16
        D = E // H
        key = jax.random.key(seed)
        ks = jax.random.split(key, 12)
        B, T, S = (2, 512, 512)
        inp = {'query': jax.random.normal(ks[0], (B, T, E), jnp.float32), 'key': jax.random.normal(ks[1], (B, S, E), jnp.float32), 'value': jax.random.normal(ks[2], (B, S, E), jnp.float32), 'spatial_bias': jax.random.normal(ks[3], (B, H, T, S), jnp.float32) * 0.1, 'directional_bias': jax.random.normal(ks[4], (B, H, T, S), jnp.float32) * 0.1, 'key_padding_mask': jnp.zeros((B, S), dtype=bool), 'attn_mask': jax.random.normal(ks[5], (T, S), jnp.float32) * 0.1, 'Wq': jax.random.normal(ks[6], (E, E), jnp.float32) / np.sqrt(E), 'bq': jnp.zeros((E,), jnp.float32), 'Wk': jax.random.normal(ks[7], (E, E), jnp.float32) / np.sqrt(E), 'bk': jnp.zeros((E,), jnp.float32), 'Wv': jax.random.normal(ks[8], (E, E), jnp.float32) / np.sqrt(E), 'bv': jnp.zeros((E,), jnp.float32), 'Wo': jax.random.normal(ks[9], (E, E), jnp.float32) / np.sqrt(E), 'bo': jnp.zeros((E,), jnp.float32)}
        return inp
    _L0_xattn_all = _L0_xattn_setup()
    _L0_xattn_in = {k: v for k, v in _L0_xattn_all.items() if k in ('Wq', 'bq', 'Wk', 'bk', 'Wv', 'bv', 'Wo', 'bo')}
    del _L0_xattn_all

    def _L0_attn_setup():
        import jax, jax.numpy as jnp
        import numpy as np
        HEADS = 16
        EPS = 1e-06
        key = jax.random.key(seed)
        k0, k1, k2, k3, k4 = jax.random.split(key, 5)
        b, t, dim = (2, 512, 256)
        scale = 0.02
        return {'hidden_states': jax.random.normal(k0, (b, t, dim), dtype=jnp.float32), 'Wq': jax.random.normal(k1, (dim, dim), dtype=jnp.float32) * scale, 'Wk': jax.random.normal(k2, (dim, dim), dtype=jnp.float32) * scale, 'Wv': jax.random.normal(k3, (dim, dim), dtype=jnp.float32) * scale, 'Wo': jax.random.normal(k4, (dim, dim), dtype=jnp.float32) * scale}
    _L0_attn_all = _L0_attn_setup()
    _L0_attn_in = {k: v for k, v in _L0_attn_all.items() if k in ('Wq', 'Wk', 'Wv', 'Wo')}
    del _L0_attn_all

    def _L0_ffn_setup():
        import jax, jax.numpy as jnp
        import numpy as np
        B, S, D = (1, 512, 256)
        E, F = (16, 256)
        NG, TKG, K = (4, 2, 4)
        NSH = 2
        SCALE = 2.5
        STD = 0.02
        EPG = E // NG

        def _route(x_flat, router_w, bias):
            logits = x_flat.astype(jnp.float32) @ router_w.T
            scores = jax.nn.sigmoid(logits)
            s = scores + bias[None, :]
            sg = s.reshape(-1, NG, EPG)
            group_score = jax.lax.top_k(sg, 2)[0].sum(-1)
            gidx = jax.lax.top_k(group_score, TKG)[1]
            gmask = jnp.sum(jax.nn.one_hot(gidx, NG, dtype=jnp.float32), axis=1) > 0
            emask = jnp.repeat(gmask, EPG, axis=1)
            masked = jnp.where(emask, s, -1.0)
            topk_idx = jax.lax.top_k(masked, K)[1]
            tw = jnp.take_along_axis(scores, topk_idx, axis=1)
            tw = tw / (tw.sum(-1, keepdims=True) + 1e-20)
            tw = tw * SCALE
            return (topk_idx, tw)
        key = jax.random.key(seed)
        ks = jax.random.split(key, 8)
        return {'hidden_states': jax.random.normal(ks[0], (B, S, D), jnp.float32), 'router_w': jax.random.normal(ks[1], (E, D), jnp.float32) * STD, 'bias': jnp.zeros((E,), jnp.float32), 'gate_w': jax.random.normal(ks[2], (E, D, F), jnp.float32) * STD, 'up_w': jax.random.normal(ks[3], (E, D, F), jnp.float32) * STD, 'down_w': jax.random.normal(ks[4], (E, F, D), jnp.float32) * STD, 'sh_gate_w': jax.random.normal(ks[5], (D, NSH * F), jnp.float32) * STD, 'sh_up_w': jax.random.normal(ks[6], (D, NSH * F), jnp.float32) * STD, 'sh_down_w': jax.random.normal(ks[7], (NSH * F, D), jnp.float32) * STD}
    _L0_ffn_all = _L0_ffn_setup()
    _L0_ffn_in = {k: v for k, v in _L0_ffn_all.items() if k in ('router_w', 'bias', 'gate_w', 'up_w', 'down_w', 'sh_gate_w', 'sh_up_w', 'sh_down_w')}
    del _L0_ffn_all

    def _L1_xattn_setup():
        import jax, jax.numpy as jnp
        import numpy as np
        B, S, D = (8, 512, 256)
        key = jax.random.key(seed)
        kq, kk, kv = jax.random.split(key, 3)
        qm = jax.random.normal(kq, (B, S, D), dtype=jnp.float32)
        km = jax.random.normal(kk, (B, S, D), dtype=jnp.float32)
        vm = jax.random.normal(kv, (B, S, D), dtype=jnp.float32)
        return {'qm': qm, 'km': km, 'vm': vm}
    _L1_xattn_all = _L1_xattn_setup()
    _L1_xattn_in = {k: v for k, v in _L1_xattn_all.items() if k in ()}
    del _L1_xattn_all

    def _L1_attn_setup():
        import jax, jax.numpy as jnp
        import numpy as np
        B, T, D, H = (2, 512, 256, 16)
        key = jax.random.key(seed)
        k0, k1, k2, k3 = jax.random.split(key, 4)
        s = 0.02
        return {'x': jax.random.normal(k0, (B, T, D), dtype=jnp.float32), 'Wqkv': jax.random.normal(k1, (3 * D, D), dtype=jnp.float32) * s, 'Wout': jax.random.normal(k2, (D, D), dtype=jnp.float32) * s, 'bout': jax.random.normal(k3, (D,), dtype=jnp.float32) * s}
    _L1_attn_all = _L1_attn_setup()
    _L1_attn_in = {k: v for k, v in _L1_attn_all.items() if k in ('Wqkv', 'Wout', 'bout')}
    del _L1_attn_all

    def _L1_ffn_setup():
        import jax, jax.numpy as jnp
        import numpy as np
        B, S, D_MODEL, D_HIDDEN = (4, 512, 256, 1024)

        def act_quant(x):
            scale = 127.0 / jnp.clip(jnp.max(jnp.abs(x), axis=-1, keepdims=True), 1e-05)
            return jnp.clip(jnp.round(x * scale), -128, 127) / scale

        def weight_quant(w):
            scale = 1.0 / jnp.clip(jnp.mean(jnp.abs(w)), 1e-05)
            return jnp.clip(jnp.round(w * scale), -1, 1) / scale

        def bit_linear(x, w):
            xq = x + jax.lax.stop_gradient(act_quant(x) - x)
            wq = w + jax.lax.stop_gradient(weight_quant(w) - w)
            return jnp.einsum('bsd,hd->bsh', xq, wq)

        def depthwise_conv1d(x_bcl, w, b):
            y = jax.lax.conv_general_dilated(x_bcl, w, window_strides=(1,), padding=[(1, 1)], dimension_numbers=('NCH', 'OIH', 'NCH'), feature_group_count=x_bcl.shape[1])
            return y + b[None, :, None]
        key = jax.random.key(seed)
        ks = jax.random.split(key, 5)
        lim1 = 1.0 / np.sqrt(D_MODEL)
        lim2 = 1.0 / np.sqrt(D_HIDDEN)
        limc = 1.0 / np.sqrt(3.0)
        return {'x': jax.random.normal(ks[0], (B, S, D_MODEL), dtype=jnp.float32), 'w1': jax.random.uniform(ks[1], (D_HIDDEN, D_MODEL), jnp.float32, -lim1, lim1), 'conv_w': jax.random.uniform(ks[2], (D_HIDDEN, 1, 3), jnp.float32, -limc, limc), 'conv_b': jax.random.uniform(ks[3], (D_HIDDEN,), jnp.float32, -limc, limc), 'w2': jax.random.uniform(ks[4], (D_MODEL, D_HIDDEN), jnp.float32, -lim2, lim2)}
    _L1_ffn_all = _L1_ffn_setup()
    _L1_ffn_in = {k: v for k, v in _L1_ffn_all.items() if k in ('w1', 'conv_w', 'conv_b', 'w2')}
    del _L1_ffn_all
    return {'x': x, 'ctx_1024': ctx_1024, 'fside_Bx16xSxS2_0': fside_Bx16xSxS2_0, 'fside_SxS2_0': fside_SxS2_0, 'mask_BxS2_bf0': mask_BxS2_bf0, 'L0_xattn_Wq': _L0_xattn_in['Wq'], 'L0_xattn_bq': _L0_xattn_in['bq'], 'L0_xattn_Wk': _L0_xattn_in['Wk'], 'L0_xattn_bk': _L0_xattn_in['bk'], 'L0_xattn_Wv': _L0_xattn_in['Wv'], 'L0_xattn_bv': _L0_xattn_in['bv'], 'L0_xattn_Wo': _L0_xattn_in['Wo'], 'L0_xattn_bo': _L0_xattn_in['bo'], 'L0_attn_Wq': _L0_attn_in['Wq'], 'L0_attn_Wk': _L0_attn_in['Wk'], 'L0_attn_Wv': _L0_attn_in['Wv'], 'L0_attn_Wo': _L0_attn_in['Wo'], 'L0_ffn_router_w': _L0_ffn_in['router_w'], 'L0_ffn_bias': _L0_ffn_in['bias'], 'L0_ffn_gate_w': _L0_ffn_in['gate_w'], 'L0_ffn_up_w': _L0_ffn_in['up_w'], 'L0_ffn_down_w': _L0_ffn_in['down_w'], 'L0_ffn_sh_gate_w': _L0_ffn_in['sh_gate_w'], 'L0_ffn_sh_up_w': _L0_ffn_in['sh_up_w'], 'L0_ffn_sh_down_w': _L0_ffn_in['sh_down_w'], 'L1_attn_Wqkv': _L1_attn_in['Wqkv'], 'L1_attn_Wout': _L1_attn_in['Wout'], 'L1_attn_bout': _L1_attn_in['bout'], 'L1_ffn_w1': _L1_ffn_in['w1'], 'L1_ffn_conv_w': _L1_ffn_in['conv_w'], 'L1_ffn_conv_b': _L1_ffn_in['conv_b'], 'L1_ffn_w2': _L1_ffn_in['w2']}

def reference(x, ctx_1024, fside_Bx16xSxS2_0, fside_SxS2_0, mask_BxS2_bf0, L0_xattn_Wq, L0_xattn_bq, L0_xattn_Wk, L0_xattn_bk, L0_xattn_Wv, L0_xattn_bv, L0_xattn_Wo, L0_xattn_bo, L0_attn_Wq, L0_attn_Wk, L0_attn_Wv, L0_attn_Wo, L0_ffn_router_w, L0_ffn_bias, L0_ffn_gate_w, L0_ffn_up_w, L0_ffn_down_w, L0_ffn_sh_gate_w, L0_ffn_sh_up_w, L0_ffn_sh_down_w, L1_attn_Wqkv, L1_attn_Wout, L1_attn_bout, L1_ffn_w1, L1_ffn_conv_w, L1_ffn_conv_b, L1_ffn_w2):
    import jax
    import jax.numpy as jnp

    def _L0_xattn_ref(query, key, value, spatial_bias, directional_bias, key_padding_mask, attn_mask, Wq, bq, Wk, bk, Wv, bv, Wo, bo):
        import jax, jax.numpy as jnp
        import numpy as np
        E = 256
        H = 16
        D = E // H
        B, T, _ = query.shape
        S = key.shape[1]
        scale = D ** (-0.5)
        q = (query @ Wq.T + bq).reshape(B, T, H, D).transpose(0, 2, 1, 3)
        k = (key @ Wk.T + bk).reshape(B, S, H, D).transpose(0, 2, 1, 3)
        v = (value @ Wv.T + bv).reshape(B, S, H, D).transpose(0, 2, 1, 3)
        scores = jnp.einsum('bhtd,bhsd->bhts', q, k) * scale
        scores = scores + attn_mask[None, None, :, :]
        pad = key_padding_mask[:, None, None, :]
        scores = jnp.where(pad, -jnp.inf, scores)
        if T == S:
            scores = scores + spatial_bias + directional_bias
        probs = jax.nn.softmax(scores, axis=-1)
        out = jnp.einsum('bhts,bhsd->bhtd', probs, v)
        out = out.transpose(0, 2, 1, 3).reshape(B, T, E)
        return out @ Wo.T + bo

    def _L0_attn_ref(hidden_states, Wq, Wk, Wv, Wo):
        import jax, jax.numpy as jnp
        import numpy as np
        HEADS = 16
        EPS = 1e-06
        b, t, dim = hidden_states.shape
        h = HEADS
        d = dim // h

        def proj(W):
            return (hidden_states @ W.T).reshape(b, t, h, d).transpose(0, 2, 1, 3)
        q = proj(Wq) * d ** (-0.5)
        k = proj(Wk)
        v = proj(Wv)
        s = jnp.einsum('bhqd,bhkd->bhqk', q, k)
        attn = 1.0 + s + 0.5 * s * s
        causal = jnp.tril(jnp.ones((t, t), dtype=bool))
        attn = jnp.where(causal, attn, 0.0)
        o = jnp.einsum('bhqk,bhkd->bhqd', attn, v)
        z = jnp.sum(attn, axis=-1, keepdims=True) + EPS
        o = o / z
        y = o.transpose(0, 2, 1, 3).reshape(b, t, dim)
        return y @ Wo.T

    def _L0_ffn_ref(hidden_states, router_w, bias, gate_w, up_w, down_w, sh_gate_w, sh_up_w, sh_down_w):
        import jax, jax.numpy as jnp
        import numpy as np
        B, S, D = (1, 512, 256)
        E, F = (16, 256)
        NG, TKG, K = (4, 2, 4)
        NSH = 2
        SCALE = 2.5
        STD = 0.02
        EPG = E // NG

        def _route(x_flat, router_w, bias):
            logits = x_flat.astype(jnp.float32) @ router_w.T
            scores = jax.nn.sigmoid(logits)
            s = scores + bias[None, :]
            sg = s.reshape(-1, NG, EPG)
            group_score = jax.lax.top_k(sg, 2)[0].sum(-1)
            gidx = jax.lax.top_k(group_score, TKG)[1]
            gmask = jnp.sum(jax.nn.one_hot(gidx, NG, dtype=jnp.float32), axis=1) > 0
            emask = jnp.repeat(gmask, EPG, axis=1)
            masked = jnp.where(emask, s, -1.0)
            topk_idx = jax.lax.top_k(masked, K)[1]
            tw = jnp.take_along_axis(scores, topk_idx, axis=1)
            tw = tw / (tw.sum(-1, keepdims=True) + 1e-20)
            tw = tw * SCALE
            return (topk_idx, tw)
        x = hidden_states.reshape(-1, D)
        topk_idx, tw = _route(x, router_w, bias)
        combine = (jax.nn.one_hot(topk_idx, E, dtype=tw.dtype) * tw[..., None]).sum(1)
        h = jnp.einsum('td,edf->etf', x, gate_w)
        u = jnp.einsum('td,edf->etf', x, up_w)
        y = jnp.einsum('etf,efd->etd', jax.nn.silu(h) * u, down_w)
        routed = jnp.einsum('etd,te->td', y, combine)
        sh = jax.nn.silu(x @ sh_gate_w) * (x @ sh_up_w) @ sh_down_w
        return (routed + sh).reshape(hidden_states.shape)

    def _L1_xattn_ref(qm, km, vm):
        import jax, jax.numpy as jnp
        import numpy as np
        B, S, D = (8, 512, 256)
        scale = 1.0 / jnp.sqrt(jnp.asarray(qm.shape[-1], dtype=qm.dtype))
        qkm = jnp.einsum('bqd,bkd->bqk', qm, km) * scale
        out = jnp.einsum('bqk,bkd->bqd', qkm, vm)
        return jax.nn.softmax(out, axis=-1)

    def _L1_attn_ref(x, Wqkv, Wout, bout):
        import jax, jax.numpy as jnp
        import numpy as np
        B, T, D, H = (2, 512, 256, 16)
        b, t, d = x.shape
        h = H
        dh = d // h
        qkv = x @ Wqkv.T
        q, k, v = jnp.split(qkv, 3, axis=-1)

        def merge_heads(z):
            return z.reshape(b, t, h, dh).transpose(0, 2, 1, 3)
        q, k, v = map(merge_heads, (q, k, v))
        scale = dh ** (-0.5)
        dots = jnp.einsum('bhid,bhjd->bhij', q, k) * scale
        causal_mask = jnp.triu(jnp.ones((t, t), dtype=bool), 1)
        dots = jnp.where(causal_mask, -jnp.inf, dots)
        attn = jax.nn.softmax(dots, axis=-1)
        out = jnp.einsum('bhij,bhjd->bhid', attn, v)
        out = out.transpose(0, 2, 1, 3).reshape(b, t, d)
        return out @ Wout.T + bout

    def _L1_ffn_ref(x, w1, conv_w, conv_b, w2):
        import jax, jax.numpy as jnp
        import numpy as np
        B, S, D_MODEL, D_HIDDEN = (4, 512, 256, 1024)

        def act_quant(x):
            scale = 127.0 / jnp.clip(jnp.max(jnp.abs(x), axis=-1, keepdims=True), 1e-05)
            return jnp.clip(jnp.round(x * scale), -128, 127) / scale

        def weight_quant(w):
            scale = 1.0 / jnp.clip(jnp.mean(jnp.abs(w)), 1e-05)
            return jnp.clip(jnp.round(w * scale), -1, 1) / scale

        def bit_linear(x, w):
            xq = x + jax.lax.stop_gradient(act_quant(x) - x)
            wq = w + jax.lax.stop_gradient(weight_quant(w) - w)
            return jnp.einsum('bsd,hd->bsh', xq, wq)

        def depthwise_conv1d(x_bcl, w, b):
            y = jax.lax.conv_general_dilated(x_bcl, w, window_strides=(1,), padding=[(1, 1)], dimension_numbers=('NCH', 'OIH', 'NCH'), feature_group_count=x_bcl.shape[1])
            return y + b[None, :, None]
        h = bit_linear(x, w1)
        h = depthwise_conv1d(h.transpose(0, 2, 1), conv_w, conv_b)
        h = h.transpose(0, 2, 1)
        h = jax.nn.silu(h)
        return bit_linear(h, w2)
    x = x + _L0_xattn_ref(_layernorm(x, axis=-1), ctx_1024, ctx_1024, fside_Bx16xSxS2_0, fside_Bx16xSxS2_0, mask_BxS2_bf0, fside_SxS2_0, L0_xattn_Wq, L0_xattn_bq, L0_xattn_Wk, L0_xattn_bk, L0_xattn_Wv, L0_xattn_bv, L0_xattn_Wo, L0_xattn_bo)
    x = x + _L0_attn_ref(_layernorm(x, axis=-1), L0_attn_Wq, L0_attn_Wk, L0_attn_Wv, L0_attn_Wo)
    x = x + _L0_ffn_ref(_layernorm(x, axis=-1), L0_ffn_router_w, L0_ffn_bias, L0_ffn_gate_w, L0_ffn_up_w, L0_ffn_down_w, L0_ffn_sh_gate_w, L0_ffn_sh_up_w, L0_ffn_sh_down_w)
    x = x + _L1_xattn_ref(_layernorm(x, axis=-1), ctx_1024, ctx_1024)
    x = x + _L1_attn_ref(_layernorm(x, axis=-1), L1_attn_Wqkv, L1_attn_Wout, L1_attn_bout)
    x = x + _L1_ffn_ref(_layernorm(x, axis=-1), L1_ffn_w1, L1_ffn_conv_w, L1_ffn_conv_b, L1_ffn_w2)
    return x

_drawn_inputs = setup_inputs


def setup_inputs(seed=0):
    import zlib

    import numpy as np

    out = dict(_drawn_inputs(seed))
    spreads = {'L0_xattn_bq': (0.0, 0.354),
     'L0_xattn_bk': (0.0, 2.0),
     'L0_xattn_bv': (0.0, 0.1),
     'L0_xattn_bo': (0.0, 0.1),
     'L0_ffn_bias': (0.0, 0.412)}
    factors = {'fside_SxS2_0': 6.817,
     'L0_attn_Wq': 8.0,
     'L0_attn_Wk': 8.0,
     'L0_ffn_router_w': 3.853,
     'L0_ffn_gate_w': 2.886,
     'L0_ffn_up_w': 2.849,
     'L0_ffn_down_w': 2.843,
     'L1_attn_bout': 3.543,
     'L0_ffn_sh_gate_w': 2.916,
     'L0_ffn_sh_up_w': 2.87,
     'L0_ffn_sh_down_w': 2.882}
    for name, (base, spread) in spreads.items():
        noise = np.random.default_rng([zlib.crc32(name.encode()), seed]).standard_normal(out[name].shape)
        drawn = base * np.exp(spread * noise) if base else spread * noise
        out[name] = jnp.asarray(drawn.astype(out[name].dtype))
    for name, factor in factors.items():
        out[name] = (out[name] * factor).astype(out[name].dtype)
    return out
```

```python
from contextlib import ExitStack

import numpy as np

import concourse.bass as bass
from concourse import mybir

F32 = mybir.dt.float32
BF16 = mybir.dt.bfloat16
I32 = mybir.dt.int32
U8 = mybir.dt.uint8
ALU = mybir.AluOpType
ACT = mybir.ActivationFunctionType
AX = mybir.AxisListType

P = 128
B, T, S, E = 64, 64, 256, 256
H, D = 16, 16
NT = B * T // P
KC = E // P
SC = 2 * S // P
HG = H // KC
D1 = D + 1
MASKED = -1e30
NE, NG, TOP, TOP_GROUPS = 16, 4, 4, 2
NS = (B * T * TOP + NE * (P - 1)) // P + 1
NS += -NS % 4
ROUND = 1.5 * 2.0 ** 23
LN_EPS = 1e-5


class Phase:

    def __init__(self, nc, ctx, name):
        self.nc, self.ctx, self.name, self.sems = nc, ctx, name, []

    def sb(self, name, shape, dt=F32):
        return self.ctx.enter_context(self.nc.sbuf_tensor(f"{self.name}_{name}", shape, dt))

    def ps(self, name, dt=F32):
        return self.ctx.enter_context(self.nc.psum_tensor(f"{self.name}_ps_{name}", [P, 512], dt))

    def sem(self, name):
        s = self.ctx.enter_context(self.nc.semaphore(f"{self.name}_{name}"))
        self.sems.append(s)
        return s

    def block(self):
        self.ctx.callback(self.clear_semaphores)
        return self.ctx.enter_context(self.nc.Block())

    def clear_semaphores(self):
        numbers = sorted(s.num for s in self.sems)
        with self.nc.Block() as block:
            @block.gpsimd
            def _(pool):
                first = last = numbers[0]
                for number in numbers[1:] + [None]:
                    if number != last + 1:
                        pool.sem_clear(range(first, last + 1))
                        first = number
                    last = number


def wait(eng, sem, value):
    if isinstance(value, int) and value <= 0:
        return
    eng.wait_ge(sem, value)


def wait_apart(eng, sem, value, passed):
    eng.wait_ge(sem, value)
    if not isinstance(value, int):
        eng.sem_inc(passed)


def live(t, n=NT):
    return not isinstance(t, int) or 0 <= t < n


def tile_steps(eng, step, n=NT, lag=2, peel=4, turn=2):
    for s in range(peel):
        step(s, s % turn)
    with eng.Fori(0, (n - peel) // turn) as i:
        for u in range(turn):
            step(i * turn + (peel + u), u)
    for s in range(n, n + lag):
        step(s, s % turn)


class LayerNorm:

    def __init__(self, ph, c, x):
        self.c, self.x = c, x
        self.stats = ph.sb("ln_stats", [P, 2, 6])
        self.mv = ph.sb("ln_mv", [P, 2, 2])
        self.rstd = ph.sb("ln_rstd", [P, 2, 2])
        self.xn = ph.sb("xn", [P, 2, E])
        self.stats_done = ph.sem("ln_stats_done")
        self.var_ready = ph.sem("ln_var_ready")
        self.eps_added = ph.sem("ln_eps_added")
        self.rstd_ready = ph.sem("ln_rstd_ready")
        self.xn_ready = ph.sem("xn_ready")

    def statistics(self, dve, nc, t, par):
        wait(dve, self.xn_ready, t - 1)
        nc.vector.bn_stats(self.stats[:, par, :], self.x[:, t, :]).then_inc(self.stats_done, 1)
        wait_apart(dve, self.stats_done, t + 1, self.c.passed_dve)
        nc.vector.bn_aggr(self.mv[:, par, :], self.stats[:, par, :]).then_inc(self.var_ready, 1)

    def inverse_std(self, pool, nc, t, par):
        wait_apart(pool, self.var_ready, t + 1, self.c.passed_pool)
        nc.gpsimd.tensor_scalar(self.rstd[:, par, 0:1], self.mv[:, par, 1:2], LN_EPS, None,
                                ALU.add).then_inc(self.eps_added, 1)
        pool.wait_ge(self.eps_added, t + 1)
        nc.gpsimd.tensor_tensor(self.rstd[:, par, 1:2], self.rstd[:, par, 0:1],
                                self.c.minus_half[:, 0:1], ALU.pow).then_inc(self.rstd_ready, 1)

    def normalise(self, dve, nc, t, par, free_sem, per_tile=1):
        dve.wait_ge(self.rstd_ready, t + 1)
        wait(dve, free_sem, (t - 1) * per_tile)
        nc.vector.tensor_scalar(self.xn[:, par, :], self.x[:, t, :], self.mv[:, par, 0:1],
                                self.rstd[:, par, 1:2], ALU.subtract, ALU.mult)\
            .then_inc(self.xn_ready, 1)


def cross_attention_0(nc, c, X, d, x_tiles_loaded):
    with ExitStack() as ctx:
        ph = Phase(nc, ctx, "xa")
        wq, wk, wv = (ph.sb(n, [P, KC, E]) for n in ("wq", "wk", "wv"))
        wo = ph.sb("wo", [P, 2, E])
        bq, bk = ph.sb("bq", [P, KC]), ph.sb("bk", [P, KC])
        bq4 = ph.sb("bq4", [P, KC])
        bv = ph.sb("bv", [P, 2])
        bo = ph.sb("bo", [P, E])
        attn_raw, attn = ph.sb("attn_raw", [P, S]), ph.sb("attn", [P, S])
        pad = ph.sb("pad", [P, B, S], U8)
        padT = ph.sb("padT", [P, NT, SC], U8)
        keep = ph.sb("keep", [P, NT, SC])
        ctxT = ph.sb("ctxT", [P, 2, KC, 2 * S])
        xT = ph.sb("xT", [P, 2, KC, P])
        qT = ph.sb("qT", [P, 2, KC, P])
        qz = ph.sb("qz", [P, 2, KC, 2, HG * T])
        kT = ph.sb("kT", [P, 2, KC, 2 * S])
        v = ph.sb("v", [P, 2, SC, H, D1])
        mask = ph.sb("mask", [P, 2, S])
        neg_s = ph.sb("neg_s", [P, 2, 2, S])
        neg_max = ph.sb("neg_max", [P, 2, 2])
        prob = ph.sb("prob", [P, 2, 2, S])
        probT = ph.sb("probT", [P, 2, 2, 2, P])
        rz = ph.sb("rz", [P, 2, HG])
        y = ph.sb("y", [P, 2, HG, D])
        yT = ph.sb("yT", [P, 2, 2, P])
        o = ph.sb("o", [P, 2, E])
        ln = LayerNorm(ph, c, X)

        ps_s = [ph.ps(f"s{i}") for i in range(2)]
        ps_t = [ph.ps(f"t{i}") for i in range(2)]
        ps_o = [ph.ps(f"o{i}") for i in range(2)]
        ps_a, ps_b = ph.ps("a"), ph.ps("b")

        w_loaded = ph.sem("w_loaded")
        ctx_loaded = [ph.sem(f"ctx_loaded{i}") for i in range(2)]
        mask_loaded = ph.sem("mask_loaded")
        const_ready = ph.sem("const_ready")
        xT_done, xT_ready = ph.sem("xT_done"), ph.sem("xT_ready")
        q_done, q_ready, qz_ready = ph.sem("q_done"), ph.sem("q_ready"), ph.sem("qz_ready")
        k_done, k_ready = ph.sem("k_done"), ph.sem("k_ready")
        v_done, v_ready, ones_ready = ph.sem("v_done"), ph.sem("v_ready"), ph.sem("ones_ready")
        mask_ready = ph.sem("mask_ready")
        s_done, s_ready = ph.sem("s_done"), ph.sem("s_ready")
        exp_ready = ph.sem("exp_ready")
        t_done, t_ready = ph.sem("t_done"), ph.sem("t_ready")
        pv_done = ph.sem("pv_done")
        rz_ready, y_ready = ph.sem("rz_ready"), ph.sem("y_ready")
        yT_done, yT_ready = ph.sem("yT_done"), ph.sem("yT_ready")
        o_done, o_ready, x_updated = ph.sem("o_done"), ph.sem("o_ready"), ph.sem("x_updated")

        block = ph.block()

        @block.sync
        def _(sp):
            for dst, src in ((wq[:, :, :], d["xa_wqT"]), (wk[:, :, :], d["xa_wkT"]),
                             (wv[:, :, :], d["xa_wvT"]), (wo[:, :, :], d["xa_woP"]),
                             (bq[:, :], d["xa_bq"]), (bk[:, :], d["xa_bk"]), (bv[:, :], d["xa_bvP"]),
                             (bo[:, :], d["xa_bo"].to_broadcast([P, E]))):
                sp.dma_start(dst, src).then_inc(w_loaded, 16)
            sp.dma_start(padT[:, :, :], d["padT"]).then_inc(mask_loaded, 16)
            for h2 in range(2):
                sp.dma_start(attn_raw[h2 * T:(h2 + 1) * T, :], d["attn_mask"]).then_inc(mask_loaded, 16)
            sp.dma_start(pad[:, :, :], d["pad"].to_broadcast([P, B, S])).then_inc(mask_loaded, 16)

            def step(s, par):
                if live(s):
                    if not (isinstance(s, int) and s < 2):
                        sp.wait_ge(v_done, 2 * (s - 1))
                    sp.dma_start(ctxT[:, par, :, :], d["ctxT"][s, :, :, :]).then_inc(ctx_loaded[par], 16)
            tile_steps(sp, step, lag=0)

        @block.gpsimd
        def _(pool):
            def step(s, par):
                p, pp = s - 1, 1 - par
                if live(p):
                    if isinstance(p, int) and p == 0:
                        pool.wait_ge(const_ready, 3)
                    wait(pool, pv_done, 8 * (p - 1))
                    nc.gpsimd.tensor_copy(v[:, pp, :, :, D:D1],
                                          keep[:, p, :].unsqueeze(2).unsqueeze(3).to_broadcast([P, SC, H, 1]))\
                        .then_inc(ones_ready, 1)
                    pool.wait_ge(q_ready, p + 1)
                    wait(pool, s_done, 8 * (p - 1))
                    for g in range(KC):
                        for b in range(2):
                            ins = nc.gpsimd.tensor_tensor(
                                qz[:, pp, g, b, :].rearrange("p (h t) -> p h t", h=HG),
                                qT[:, pp, g, b * T:(b + 1) * T].unsqueeze(1).to_broadcast([P, HG, T]),
                                c.head_mask[:, :].unsqueeze(2).to_broadcast([P, HG, T]), ALU.mult)
                    ins.then_inc(qz_ready, 1)
                if live(s):
                    ln.inverse_std(pool, nc, s, par)
                a = s - 3
                if live(a):
                    pool.wait_ge(o_ready, a + 1)
                    nc.gpsimd.tensor_tensor(X[:, a, :], X[:, a, :], o[:, 1 - par, :], ALU.add)\
                        .then_inc(x_updated, 1)
            tile_steps(pool, step, lag=3, peel=6)

        @block.vector
        def _(dve):
            dve.wait_ge(mask_loaded, 16 * 4)
            nc.vector.tensor_scalar(attn[:, :], attn_raw[:, :], MASKED, None, ALU.max).then_inc(const_ready, 1)
            nc.vector.tensor_scalar(keep[:, :, :], padT[:, :, :], -1.0, 1.0, ALU.mult, ALU.add)\
                .then_inc(const_ready, 1)
            dve.wait_ge(w_loaded, 16 * 8)
            nc.vector.tensor_scalar(bq4[:, :], bq[:, :], D ** -0.5, None, ALU.mult).then_inc(const_ready, 1)
            dve.wait_ge(const_ready, 3)

            def masked_scores(a, u):
                if u % 4 == 0:
                    b = u // 4
                    wait(dve, s_ready, 8 * a + u - 4)
                    nc.vector.scalar_tensor_tensor(mask[:, b, :], pad[:, 2 * a + b, :], MASKED, attn[:, :],
                                                   ALU.mult, ALU.add).then_inc(mask_ready, 1)
                    dve.wait_ge(mask_ready, 2 * a + b + 1)
                wait(dve, exp_ready, 8 * a + u - 1)
                wait_apart(dve, s_done, 8 * a + u + 1, c.passed_dve)
                for i in range(2):
                    ins = nc.vector.tensor_tensor_reduce(
                        neg_s[:, u % 2, i, :], ps_s[u % 2][:, i * S:(i + 1) * S], mask[:, u // 4, :],
                        -1.0, 3e38, ALU.add, ALU.min, neg_max[:, u % 2, i:i + 1])
                ins.then_inc(s_ready, 1)

            def normalised_heads(a, b):
                dve.wait_ge(pv_done, 8 * a + 4 * b + 4)
                wait(dve, yT_done, 2 * a + b - 1)
                for h2 in range(2):
                    rows = slice(h2 * T, (h2 + 1) * T)
                    heads = ps_o[b][rows, 0:H * D1].rearrange("p (q h d) -> p q h d", h=2, d=D1)
                    nc.vector.reciprocal(rz[rows, b, :], heads[:, :, h2, D]).then_inc(rz_ready, 1)
                dve.wait_ge(rz_ready, 4 * a + 2 * b + 2)
                for h2 in range(2):
                    rows = slice(h2 * T, (h2 + 1) * T)
                    heads = ps_o[b][rows, 0:H * D1].rearrange("p (q h d) -> p q h d", h=2, d=D1)
                    ins = nc.vector.tensor_tensor(
                        y[rows, b, :, :], heads[:, :, h2, 0:D],
                        rz[rows, b, :].unsqueeze(2).to_broadcast([T, HG, D]), ALU.mult)
                ins.then_inc(y_ready, 1)

            def heads_out(a, b, tp):
                dve.wait_ge(yT_done, 2 * a + b + 1)
                wait(dve, o_done, a - 1)
                for h2 in range(2):
                    ins = nc.vector.tensor_scalar(yT[:, tp, h2, b * T:(b + 1) * T],
                                                  ps_of_yT[b][:, h2 * T:(h2 + 1) * T], bv[:, h2:h2 + 1], None,
                                                  ALU.add)
                ins.then_inc(yT_ready, 1)
            ps_of_yT = (ps_a, ps_b)

            def step(s, par):
                p, a, e = s - 1, s - 2, s - 3
                for u in range(8):
                    if live(a):
                        masked_scores(a, u)
                    if u == 0 and live(p):
                        dve.wait_ge(xT_done, p + 1)
                        wait(dve, q_done, p - 1)
                        nc.vector.tensor_copy(xT[:, 1 - par, :, :], ps_a[:, 0:E].rearrange("p (k t) -> p k t", k=KC))\
                            .then_inc(xT_ready, 1)
                    if u in (1, 4) and live(p):
                        g = u // 4
                        dve.wait_ge(k_done, 2 * p + g + 1)
                        wait(dve, s_done, 8 * (p - 1))
                        nc.vector.tensor_scalar(kT[:, 1 - par, g, :], (ps_b, ps_a)[g][:, :], bk[:, g:g + 1], None,
                                                ALU.add).then_inc(k_ready, 1)
                    if u == 2 and live(p):
                        dve.wait_ge(q_done, p + 1)
                        wait(dve, qz_ready, p - 1)
                        for g in range(KC):
                            ins = nc.vector.tensor_scalar(qT[:, 1 - par, g, :], ps_a[:, g * P:(g + 1) * P],
                                                          D ** -0.5, bq4[:, g:g + 1], ALU.mult, ALU.add)
                        ins.then_inc(q_ready, 1)
                    if u == 2 and live(e):
                        normalised_heads(e, 1)
                    if u == 3 and live(e):
                        heads_out(e, 1, 1 - par)
                    if u == 5 and live(e):
                        dve.wait_ge(o_done, e + 1)
                        wait(dve, x_updated, e - 1)
                        nc.vector.tensor_tensor(o[:, 1 - par, :], ps_b[:, 0:E], bo[:, :], ALU.add)\
                            .then_inc(o_ready, 1)
                    if u == 5 and live(s):
                        if isinstance(s, int):
                            dve.wait_ge(x_tiles_loaded[s // (NT // 4)], 16)
                        elif par == 0:
                            for sem in x_tiles_loaded:
                                dve.wait_ge(sem, 16)
                        ln.statistics(dve, nc, s, par)
                    if u == 6 and live(p):
                        for half in range(2):
                            dve.wait_ge(v_done, 2 * p + half + 1)
                            wait(dve, pv_done, 8 * (p - 1))
                            for i in range(2):
                                ch = 2 * half + i
                                ins = nc.vector.tensor_scalar(
                                    v[:, 1 - par, ch, :, 0:D],
                                    (ps_a, ps_b)[half][:, i * E:(i + 1) * E].rearrange("p (h d) -> p h d", h=H),
                                    keep[:, p, ch:ch + 1], None, ALU.mult)
                            ins.then_inc(v_ready, 1)
                    if u == 6 and live(a):
                        normalised_heads(a, 0)
                    if u == 7 and live(s):
                        ln.normalise(dve, nc, s, par, xT_done)
                    if u == 7 and live(a):
                        heads_out(a, 0, par)
            tile_steps(dve, step, lag=3, peel=6)

        @block.scalar
        def _(act):
            def probabilities(a, u):
                act.wait_ge(s_ready, 8 * a + u + 1)
                wait(act, t_done, 8 * a + u - 1)
                for i in range(2):
                    ins = nc.scalar.activation(prob[:, u % 2, i, :], neg_s[:, u % 2, i, :], ACT.Exp,
                                               bias=neg_max[:, u % 2, i:i + 1], scale=-1.0)
                ins.then_inc(exp_ready, 1)

            def transposed(a, u):
                act.wait_ge(t_done, 8 * a + u + 1)
                wait(act, pv_done, 8 * a + u - 1)
                nc.scalar.activation(probT[:, u % 2, :, :, :].rearrange("p i c t -> p (i c t)"),
                                     ps_t[u % 2][:, :], ACT.Copy).then_inc(t_ready, 1)

            def step(s, par):
                a, e = s - 2, s - 3
                for u in range(8):
                    if live(a):
                        probabilities(a, u)
                    if u >= 1 and live(a):
                        transposed(a, u - 1)
                    if u == 0 and live(e):
                        transposed(e, 7)
            tile_steps(act, step, lag=3, peel=6)

        @block.tensor
        def _(pe):
            def scores(a, u, ap):
                b, g, jj = u // 4, u // 2 % 2, u % 2
                if u == 0:
                    pe.wait_ge(k_ready, 2 * a + 2)
                    pe.wait_ge(qz_ready, a + 1)
                wait(pe, s_ready, 8 * a + u - 1)
                for i in range(2):
                    j = 2 * jj + i
                    mm = nc.tensor.matmul(ps_s[u % 2][:, i * S:(i + 1) * S],
                                          qz[:, ap, g, b, j * P:(j + 1) * P],
                                          kT[:, ap, g, b * S:(b + 1) * S], start=True, stop=True)
                mm.then_inc(s_done, 1)

            def transposes(a, u):
                pe.wait_ge(exp_ready, 8 * a + u + 1)
                wait(pe, t_ready, 8 * a + u - 1)
                for i in range(2):
                    for ch in range(2):
                        k = (2 * i + ch) * P
                        mm = nc.tensor.transpose(ps_t[u % 2][:, k:k + P], prob[:, u % 2, i, ch * P:(ch + 1) * P],
                                                 c.ident[:, :])
                mm.then_inc(t_done, 1)

            def attended(a, u, ap):
                b, g, jj = u // 4, u // 2 % 2, u % 2
                pe.wait_ge(t_ready, 8 * a + u + 1)
                if u == 0:
                    pe.wait_ge(v_ready, 2 * a + 2)
                    pe.wait_ge(ones_ready, a + 1)
                if u % 4 == 0:
                    wait(pe, y_ready, 2 * a + b - 1)
                for i in range(2):
                    q = 4 * g + 2 * jj + i
                    for ch in range(2):
                        mm = nc.tensor.matmul(ps_o[b][:, q * 2 * D1:(q + 1) * 2 * D1], probT[:, u % 2, i, ch, :],
                                              v[:, ap, 2 * b + ch, 2 * q:2 * q + 2, :],
                                              start=(ch == 0), stop=(ch == 1))
                mm.then_inc(pv_done, 1)

            def heads_transposed(a, b):
                pe.wait_ge(y_ready, 2 * a + b + 1)
                nc.tensor.transpose((ps_a, ps_b)[b][:, 0:P], y[:, b, :, :].rearrange("p q d -> p (q d)"),
                                    c.ident[:, :]).then_inc(yT_done, 1)

            pe.wait_ge(w_loaded, 16 * 8)
            pe.wait_ge(c.loaded, 16 * c.n_loads)

            def step(s, par):
                p, a, e = s - 1, s - 2, s - 3
                pp, ap, ep = 1 - par, par, 1 - par
                for u in range(8):
                    if live(a):
                        scores(a, u, ap)
                    if u == 0 and live(p):
                        pe.wait_ge(ln.xn_ready, p + 1)
                        wait(pe, v_ready, 2 * p - 1)
                        wait(pe, yT_ready, 2 * p - 3)
                        for k in range(KC):
                            mm = nc.tensor.transpose(ps_a[:, k * P:(k + 1) * P], ln.xn[:, pp, k * P:(k + 1) * P],
                                                     c.ident[:, :])
                        mm.then_inc(xT_done, 1)
                    if u in (1, 4) and live(p):
                        g = u // 4
                        if g == 0:
                            if isinstance(p, int):
                                pe.wait_ge(ctx_loaded[pp], 16 * (p // 2 + 1))
                            else:
                                pe.wait_ge(ctx_loaded[pp], p * 8 + (16 if pp == 0 else 8))
                            wait(pe, v_ready, 2 * p)
                        else:
                            pe.wait_ge(q_ready, p + 1)
                        for k in range(KC):
                            mm = nc.tensor.matmul((ps_b, ps_a)[g][:, :], wk[:, k, g * P:(g + 1) * P],
                                                  ctxT[:, pp, k, :], start=(k == 0), stop=(k == KC - 1))
                        mm.then_inc(k_done, 1)
                    if u == 2 and live(p):
                        pe.wait_ge(xT_ready, p + 1)
                        for g in range(KC):
                            for k in range(KC):
                                mm = nc.tensor.matmul(ps_a[:, g * P:(g + 1) * P], wq[:, k, g * P:(g + 1) * P],
                                                      xT[:, pp, k, :], start=(k == 0), stop=(k == KC - 1))
                        mm.then_inc(q_done, 1)
                    if u == 3 and live(e):
                        if live(p):
                            pe.wait_ge(k_ready, 2 * p + 1)
                        else:
                            pe.wait_ge(v_ready, 2 * NT)
                            pe.wait_ge(o_ready, e)
                        heads_transposed(e, 1)
                    if u == 5 and live(e):
                        pe.wait_ge(yT_ready, 2 * e + 2)
                        for h2 in range(2):
                            mm = nc.tensor.matmul(ps_b[:, 0:E], yT[:, ep, h2, :], wo[:, h2, :],
                                                  start=(h2 == 0), stop=(h2 == 1))
                        mm.then_inc(o_done, 1)
                    if u == 6 and live(p):
                        for half in range(2):
                            if half == 0:
                                pe.wait_ge(k_ready, 2 * p + 2)
                            elif live(e):
                                pe.wait_ge(o_ready, e + 1)
                            for i in range(2):
                                ch = 2 * half + i
                                for k in range(KC):
                                    mm = nc.tensor.matmul((ps_a, ps_b)[half][:, i * E:(i + 1) * E],
                                                          ctxT[:, pp, k, ch * P:(ch + 1) * P], wv[:, k, :],
                                                          start=(k == 0), stop=(k == KC - 1))
                            mm.then_inc(v_done, 1)
                    if u == 7 and live(a):
                        if live(p):
                            pe.wait_ge(v_ready, 2 * p + 1)
                        else:
                            pe.wait_ge(yT_ready, 2 * a - 1)
                        heads_transposed(a, 0)
                    if u >= 2 and live(a):
                        attended(a, u - 2, ap)
                    if u < 2 and live(e):
                        attended(e, u + 6, ep)
                    if u >= 1 and live(a):
                        transposes(a, u - 1)
                    if u == 0 and live(e):
                        transposes(e, 7)
            tile_steps(pe, step, lag=3, peel=6)


def causal_attention(nc, c, X, d, layer):
    soft = layer == 1
    with ExitStack() as ctx:
        ph = Phase(nc, ctx, f"sa{layer}")
        wqkv = ph.sb("wqkv", [P, KC, 3 * E])
        wo = ph.sb("wo", [P, KC, E])
        mask = ph.sb("mask", [P, P])
        xT = ph.sb("xT", [P, 2, KC, P])
        plain = ph.sb("plain", [P, 2, KC, P])
        other = ph.sb("other", [P, 2, KC, P])
        apart = ph.sb("apart", [P, 2, KC, HG, P])
        v = ph.sb("v", [P, 2, H, D1])
        w = ph.sb("w", [P, 2, 4, P])
        z, rz = ph.sb("z", [P, 2, H]), ph.sb("rz", [P, 2, H])
        y = ph.sb("y", [P, 2, H, D])
        yT = ph.sb("yT", [P, 2, KC, P])
        if soft:
            neg_s = ph.sb("neg_s", [P, 2, 4, P])
            neg_max = ph.sb("neg_max", [P, 2, 4])
            prob = ph.sb("prob", [P, 2, 4, P])
            bo = ph.sb("bo", [P, E])
            o = ph.sb("o", [P, 2, E])
        else:
            square = ph.sb("square", [P, 2, 4, P])
        ln = LayerNorm(ph, c, X)

        ps_s = [ph.ps(f"s{i}") for i in range(2)]
        ps_t = [ph.ps(f"t{i}") for i in range(2)] if soft else None
        ps_o = [ph.ps(f"o{i}") for i in range(2)]
        ps_a, ps_b = ph.ps("a"), ph.ps("b")

        loaded, n_loads = ph.sem("loaded"), 4 if soft else 3
        ones_ready = ph.sem("ones_ready")
        xT_done, xT_ready = ph.sem("xT_done"), ph.sem("xT_ready")
        qk_done, qk_ready, apart_ready = ph.sem("qk_done"), ph.sem("qk_ready"), ph.sem("apart_ready")
        v_done, v_ready = ph.sem("v_done"), ph.sem("v_ready")
        s_done = ph.sem("s_done")
        s_ready = ph.sem("s_ready")
        exp_ready, t_done = ph.sem("exp_ready"), ph.sem("t_done")
        w_ready = ph.sem("w_ready")
        pv_done = ph.sem("pv_done")
        z_ready, rz_ready, y_ready = ph.sem("z_ready"), ph.sem("rz_ready"), ph.sem("y_ready")
        yT_done, yT_ready = ph.sem("yT_done"), ph.sem("yT_ready")
        o_done, o_ready, x_updated = ph.sem("o_done"), ph.sem("o_ready"), ph.sem("x_updated")

        block = ph.block()

        @block.sync
        def _(sp):
            sp.dma_start(wqkv[:, :, :], d[f"sa{layer}_wqkvT"]).then_inc(loaded, 16)
            sp.dma_start(wo[:, :, :], d[f"sa{layer}_woT"]).then_inc(loaded, 16)
            sp.dma_start(mask[:, :], d[f"sa{layer}_mask"]).then_inc(loaded, 16)
            if soft:
                sp.dma_start(bo[:, :], d["sa1_bo"].to_broadcast([P, E])).then_inc(loaded, 16)

        @block.gpsimd
        def _(pool):
            nc.gpsimd.memset(v[:, :, :, D:D1], 1.0).then_inc(ones_ready, 1)

            def step(s, par):
                p, e = s - 1, s - 3
                if live(p):
                    pool.wait_ge(qk_ready, p + 1)
                    wait(pool, s_done, 4 * (p - 1))
                    for g in range(KC):
                        ins = nc.gpsimd.tensor_tensor(
                            apart[:, 1 - par, g, :, :],
                            other[:, 1 - par, g, :].unsqueeze(1).to_broadcast([P, HG, P]),
                            c.head_mask[:, :].unsqueeze(2).to_broadcast([P, HG, P]), ALU.mult)
                    ins.then_inc(apart_ready, 1)
                if live(s):
                    ln.inverse_std(pool, nc, s, par)
                if soft and live(e):
                    pool.wait_ge(o_ready, e + 1)
                    nc.gpsimd.tensor_tensor(X[:, e, :], X[:, e, :], o[:, 1 - par, :], ALU.add)\
                        .then_inc(x_updated, 1)
            tile_steps(pool, step, lag=3, peel=6)

        @block.vector
        def _(dve):
            dve.wait_ge(loaded, 16 * n_loads)

            def masked(a, u):
                b = u % 2
                if soft:
                    wait(dve, exp_ready, 4 * a + u - 1)
                    wait_apart(dve, s_done, 4 * a + u + 1, c.passed_dve)
                    for i in range(4):
                        ins = nc.vector.tensor_tensor_reduce(
                            neg_s[:, b, i, :], ps_s[b][:, i * P:(i + 1) * P], mask[:, :],
                            -1.0, 3e38, ALU.add, ALU.min, neg_max[:, b, i:i + 1])
                    ins.then_inc(s_ready, 1)
                else:
                    dve.wait_ge(s_ready, 4 * a + u + 1)
                    wait(dve, pv_done, 4 * a + u - 1)
                    nc.vector.scalar_tensor_tensor(w[:, b, :, :], square[:, b, :, :], 1.0,
                                                   mask[:, :].unsqueeze(1).to_broadcast([P, 4, P]),
                                                   ALU.add, ALU.mult).then_inc(w_ready, 1)

            def step(s, par):
                p, a, e = s - 1, s - 2, s - 3
                for u in range(4):
                    if live(a):
                        masked(a, u)
                    if u == 0 and live(p):
                        dve.wait_ge(xT_done, p + 1)
                        wait(dve, v_done, p - 1)
                        nc.vector.tensor_copy(xT[:, 1 - par, :, :], ps_a[:, 0:E].rearrange("p (k t) -> p k t", k=KC))\
                            .then_inc(xT_ready, 1)
                    if u == 1 and live(p):
                        q_out, k_out = (plain, other) if soft else (other, plain)
                        dve.wait_ge(qk_done, p + 1)
                        wait(dve, s_done, 4 * (p - 1))
                        wait(dve, apart_ready, p - 1)
                        nc.vector.tensor_scalar(q_out[:, 1 - par, :, :],
                                                ps_b[:, 0:E].rearrange("p (k t) -> p k t", k=KC),
                                                D ** -0.5, None, ALU.mult)
                        nc.vector.tensor_copy(k_out[:, 1 - par, :, :],
                                              ps_b[:, E:2 * E].rearrange("p (k t) -> p k t", k=KC))\
                            .then_inc(qk_ready, 1)
                    if u == 1 and live(s):
                        ln.statistics(dve, nc, s, par)
                    if u == 2 and live(p):
                        dve.wait_ge(v_done, p + 1)
                        wait(dve, pv_done, 4 * (p - 1))
                        nc.vector.tensor_copy(v[:, 1 - par, :, 0:D],
                                              ps_a[:, 0:E].rearrange("p (h d) -> p h d", h=H)).then_inc(v_ready, 1)
                    if u == 2 and live(e):
                        dve.wait_ge(pv_done, 4 * e + 4)
                        heads = ps_o[1 - par][:, 0:H * D1].rearrange("p (h d) -> p h d", d=D1)
                        sums = heads[:, :, D]
                        if not soft:
                            nc.vector.tensor_scalar(z[:, 1 - par, :], sums, 1e-6, None, ALU.add).then_inc(z_ready, 1)
                            dve.wait_ge(z_ready, e + 1)
                            sums = z[:, 1 - par, :]
                        nc.vector.reciprocal(rz[:, 1 - par, :], sums).then_inc(rz_ready, 1)
                        wait(dve, yT_done, e - 1)
                        dve.wait_ge(rz_ready, e + 1)
                        nc.vector.tensor_tensor(y[:, 1 - par, :, :], heads[:, :, 0:D],
                                                rz[:, 1 - par, :].unsqueeze(2).to_broadcast([P, H, D]),
                                                ALU.mult).then_inc(y_ready, 1)
                    if u == 3 and live(s):
                        ln.normalise(dve, nc, s, par, xT_done)
                    if u == 3 and live(e):
                        dve.wait_ge(yT_done, e + 1)
                        wait(dve, o_done, e - 1)
                        nc.vector.tensor_copy(yT[:, 1 - par, :, :], ps_b[:, 0:E].rearrange("p (k t) -> p k t", k=KC))\
                            .then_inc(yT_ready, 1)
                        dve.wait_ge(o_done, e + 1)
                        if soft:
                            wait(dve, x_updated, e - 1)
                            nc.vector.tensor_tensor(o[:, 1 - par, :], ps_a[:, 0:E], bo[:, :], ALU.add)\
                                .then_inc(o_ready, 1)
                        else:
                            nc.vector.tensor_tensor(X[:, e, :], X[:, e, :], ps_a[:, 0:E], ALU.add)\
                                .then_inc(o_ready, 1)
            tile_steps(dve, step, lag=3, peel=6)

        @block.scalar
        def _(act):
            def step(s, par):
                a, e = s - 2, s - 3
                for u in range(4):
                    b = u % 2
                    if live(a) and not soft:
                        act.wait_ge(s_done, 4 * a + u + 1)
                        wait(act, w_ready, 4 * a + u - 1)
                        nc.scalar.activation(square[:, b, :, :].rearrange("p h t -> p (h t)"), ps_s[b][:, :],
                                             ACT.Square, bias=1.0).then_inc(s_ready, 1)
                    if live(a) and soft:
                        act.wait_ge(s_ready, 4 * a + u + 1)
                        wait(act, t_done, 4 * a + u - 1)
                        for i in range(4):
                            ins = nc.scalar.activation(prob[:, b, i, :], neg_s[:, b, i, :], ACT.Exp,
                                                       bias=neg_max[:, b, i:i + 1], scale=-1.0)
                        ins.then_inc(exp_ready, 1)
                    t, ut = (a, u - 1) if u else (e, 3)
                    if soft and live(t):
                        act.wait_ge(t_done, 4 * t + ut + 1)
                        wait(act, pv_done, 4 * t + ut - 1)
                        nc.scalar.activation(w[:, ut % 2, :, :].rearrange("p h t -> p (h t)"), ps_t[ut % 2][:, :],
                                             ACT.Copy).then_inc(w_ready, 1)
            tile_steps(act, step, lag=3, peel=6)

        @block.tensor
        def _(pe):
            def scores(a, u, ap):
                g, half, b = u // 2, u % 2, u % 2
                if u == 0:
                    pe.wait_ge(apart_ready, a + 1)
                    pe.wait_ge(qk_ready, a + 1)
                wait(pe, s_ready, 4 * a + u - 1)
                nc.tensor.matmul(ps_s[b][:, :], plain[:, ap, g, :],
                                 apart[:, ap, g, 4 * half:4 * half + 4, :].rearrange("p h t -> p (h t)"),
                                 start=True, stop=True).then_inc(s_done, 1)

            def transposes(a, u):
                pe.wait_ge(exp_ready, 4 * a + u + 1)
                wait(pe, w_ready, 4 * a + u - 1)
                for i in range(4):
                    mm = nc.tensor.transpose(ps_t[u % 2][:, i * P:(i + 1) * P], prob[:, u % 2, i, :], c.ident[:, :])
                mm.then_inc(t_done, 1)

            def attended(a, u, ap):
                pe.wait_ge(w_ready, 4 * a + u + 1)
                if u == 0:
                    pe.wait_ge(v_ready, a + 1)
                    wait(pe, y_ready, a - 1)
                for i in range(4):
                    h = 4 * u + i
                    mm = nc.tensor.matmul(ps_o[ap][:, h * D1:(h + 1) * D1], w[:, u % 2, i, :], v[:, ap, h, :],
                                          start=True, stop=True)
                mm.then_inc(pv_done, 1)

            pe.wait_ge(loaded, 16 * n_loads)
            pe.wait_ge(ones_ready, 1)

            def step(s, par):
                p, a, e = s - 1, s - 2, s - 3
                pp, ap, ep = 1 - par, par, 1 - par
                for u in range(4):
                    if live(a):
                        scores(a, u, ap)
                    if u == 0 and live(p):
                        pe.wait_ge(ln.xn_ready, p + 1)
                        wait(pe, v_ready, p)
                        wait(pe, o_ready, p - 2)
                        for k in range(KC):
                            mm = nc.tensor.transpose(ps_a[:, k * P:(k + 1) * P], ln.xn[:, pp, k * P:(k + 1) * P],
                                                     c.ident[:, :])
                        mm.then_inc(xT_done, 1)
                    if u == 1 and live(p):
                        pe.wait_ge(xT_ready, p + 1)
                        wait(pe, qk_ready, p)
                        wait(pe, yT_ready, p - 2)
                        for g in range(2 * KC):
                            for k in range(KC):
                                mm = nc.tensor.matmul(ps_b[:, g * P:(g + 1) * P], wqkv[:, k, g * P:(g + 1) * P],
                                                      xT[:, pp, k, :], start=(k == 0), stop=(k == KC - 1))
                        mm.then_inc(qk_done, 1)
                    if u == 2 and live(p):
                        for k in range(KC):
                            mm = nc.tensor.matmul(ps_a[:, 0:E], xT[:, pp, k, :], wqkv[:, k, 2 * E:3 * E],
                                                  start=(k == 0), stop=(k == KC - 1))
                        mm.then_inc(v_done, 1)
                    if u == 3 and live(e):
                        pe.wait_ge(y_ready, e + 1)
                        if live(p):
                            pe.wait_ge(qk_ready, p + 1)
                        else:
                            pe.wait_ge(qk_ready, NT)
                            pe.wait_ge(yT_ready, e)
                        for k in range(KC):
                            mm = nc.tensor.transpose(ps_b[:, k * P:(k + 1) * P],
                                                     y[:, ep, :, :].rearrange("p h d -> p (h d)")[:, k * P:(k + 1) * P],
                                                     c.ident[:, :])
                        mm.then_inc(yT_done, 1)
                    if u >= 2 and live(a):
                        attended(a, u - 2, ap)
                    if u < 2 and live(e):
                        attended(e, u + 2, ep)
                    if soft and u >= 1 and live(a):
                        transposes(a, u - 1)
                    if soft and u == 0 and live(e):
                        transposes(e, 3)
                    if u == 3 and live(e):
                        pe.wait_ge(yT_ready, e + 1)
                        if live(p):
                            pe.wait_ge(v_ready, p + 1)
                        else:
                            pe.wait_ge(v_ready, NT)
                            pe.wait_ge(o_ready, e)
                        for k in range(KC):
                            mm = nc.tensor.matmul(ps_a[:, 0:E], yT[:, ep, k, :], wo[:, k, :],
                                                  start=(k == 0), stop=(k == KC - 1))
                        mm.then_inc(o_done, 1)
            tile_steps(pe, step, lag=3, peel=6)


class Chain:

    def __init__(self, eng, sem):
        self.eng, self.sem, self.n = eng, sem, 0

    def add(self, ins):
        ins.then_inc(self.sem, 1)
        self.n += 1

    def done(self):
        self.eng.wait_ge(self.sem, self.n)

    def then(self, ins):
        self.add(ins)
        self.done()


def clear_lists(nc, c):
    with ExitStack() as ctx:
        ph = Phase(nc, ctx, "cl")
        zero = ph.sb("zero", [P, 16 * E])
        ready = ph.sem("ready")
        block = ph.block()

        @block.gpsimd
        def _(pool):
            nc.gpsimd.memset(zero[:, :], 0.0).then_inc(ready, 1)

        @block.sync
        def _(sp):
            sp.wait_ge(ready, 1)
            lists = c.xg_dram.rearrange("(n p r) e -> n p (r e)", p=P, r=16)
            c.n_zeroed = NS // 16
            for n in range(NS // 16):
                sp.dma_start(lists[n, :, :], zero[:, :]).then_inc(c.zeroed, 16)
            sp.wait_ge(c.zeroed, 16 * c.n_zeroed)


def route(nc, c, X, d):
    with ExitStack() as ctx:
        ph = Phase(nc, ctx, "rt")
        rw = ph.sb("rw", [P, KC, NE])
        bias = ph.sb("bias", [P, NE])
        before = ph.sb("before", [P, NG * NG])
        upper = ph.sb("upper", [P, P])
        ones = ph.sb("ones", [P, P])
        count16 = ph.sb("count16", [P, NE])
        count_tiles = ph.sb("count_tiles", [1, NS])
        carry = ph.sb("carry", [P, NE, NT])
        xT = ph.sb("xT", [P, 2, KC, P])
        ln = LayerNorm(ph, c, X)
        arrays = {}

        def arr(name, shape, dt=F32):
            arrays[name] = ph.sb(name, [P, *shape], dt)
            return arrays[name]

        e1, score, sc_b = arr("e1", [NT, NE]), arr("score", [NT, NE]), arr("sc_b", [NT, NE])
        pairs, gs = arr("pairs", [NT * NG, 6]), arr("gs", [NT * NG])
        gt, ge = arr("gt", [NT, NG, NG]), arr("ge", [NT, NG, NG])
        grank, gm, gm1 = arr("grank", [NT * NG]), arr("gm", [NT * NG]), arr("gm1", [NT * NG])
        cand = arr("cand", [NT, NE])
        best, best_i, best_f = arr("best", [NT, 8]), arr("best_i", [NT, 8], mybir.dt.uint32), arr("best_f", [NT, 8])
        hot = arr("hot", [TOP, NT, NE])
        chosen = arr("chosen", [NT, NE])
        picked = arr("picked", [TOP, NT, NE])
        wk, wsum = arr("wk", [NT, TOP]), arr("wsum", [NT])
        incl, excl = arr("incl", [NE, NT]), arr("excl", [NE, NT])
        tiles, ends, starts = arr("tiles", [NE]), arr("ends", [NE]), arr("starts", [NE])
        slot_all = arr("slot_all", [NE, NT])
        slot_f = arr("slot_f", [NT, TOP])
        owned = ph.sb("owned", [1, NS, NE])
        owner_f = ph.sb("owner_f", [1, NS])

        ps_x = [ph.ps(f"x{i}") for i in range(2)]
        ps_l, ps_rank, ps_total = ph.ps("l"), ph.ps("rank"), ph.ps("total")

        loaded, n_loads = ph.sem("loaded"), 8
        xT_done, xT_ready, l_done = ph.sem("xT_done"), ph.sem("xT_ready"), ph.sem("l_done")
        stored = [ph.sem(f"stored{i}") for i in range(2)]
        exp_ready, steps, chosen_ready, counted = (ph.sem(n) for n in ("exp_ready", "steps", "chosen_ready", "counted"))

        block = ph.block()

        @block.sync
        def _(sp):
            for dst, src in ((rw[:, :, :], "rt_w"), (before[:, :], "rt_before"), (upper[:, :], "rt_upper"),
                             (ones[:, :], "rt_ones"), (count16[:, :], "rt_count16"),
                             (count_tiles[:, :], "rt_count_tiles"), (carry[:, :, :], "rt_carry")):
                sp.dma_start(dst, d[src]).then_inc(loaded, 16)
            sp.dma_start(bias[:, :], d["rt_bias"].to_broadcast([P, NE])).then_inc(loaded, 16)

            def step(s, par):
                if live(s):
                    sp.wait_ge(ln.xn_ready, s + 1)
                    sp.dma_start(c.xn_dram[s, :, :], ln.xn[:, par, :]).then_inc(stored[par], 16)
            tile_steps(sp, step, lag=0)
            for par in range(2):
                sp.wait_ge(stored[par], 16 * (NT // 2))

        @block.gpsimd
        def _(pool):
            def step(s, par):
                if live(s):
                    ln.inverse_std(pool, nc, s, par)
            tile_steps(pool, step, lag=0)

        @block.scalar
        def _(act):
            act.wait_ge(l_done, NT)
            nc.scalar.activation(e1[:, :, :].rearrange("p t e -> p (t e)"), ps_l[:, :], ACT.Exp, scale=-1.0)\
                .then_inc(exp_ready, 1)

        @block.tensor
        def _(pe):
            pe.wait_ge(loaded, 16 * n_loads)

            def step(s, par):
                p = s - 1
                if live(s):
                    pe.wait_ge(ln.xn_ready, s + 1)
                    wait(pe, xT_ready, s - 1)
                    for k in range(KC):
                        mm = nc.tensor.transpose(ps_x[par][:, k * P:(k + 1) * P], ln.xn[:, par, k * P:(k + 1) * P],
                                                 c.ident[:, :])
                    mm.then_inc(xT_done, 1)
                if live(p):
                    pe.wait_ge(xT_ready, p + 1)
                    logits = ps_l[:, :].rearrange("p (t e) -> p t e", e=NE)
                    for k in range(KC):
                        mm = nc.tensor.matmul(logits[:, p, :], xT[:, 1 - par, k, :], rw[:, k, :],
                                              start=(k == 0), stop=(k == KC - 1))
                    mm.then_inc(l_done, 1)
            tile_steps(pe, step, lag=1)
            pe.wait_ge(chosen_ready, 1)
            by_expert = chosen[:, :, :].rearrange("p t e -> p e t")
            nc.tensor.matmul(ps_rank[:, :], upper[:, :], by_expert, start=True, stop=True)
            nc.tensor.matmul(ps_total[:, :], ones[:, :], by_expert, start=True, stop=True).then_inc(counted, 1)

        @block.vector
        def _(dve):
            V = nc.vector

            def step(s, par):
                p = s - 1
                if live(s):
                    wait(dve, stored[par], (s - par) * 8)
                    ln.statistics(dve, nc, s, par)
                if live(p):
                    dve.wait_ge(xT_done, p + 1)
                    wait(dve, l_done, p - 1)
                    V.tensor_copy(xT[:, 1 - par, :, :], ps_x[1 - par][:, 0:E].rearrange("p (k t) -> p k t", k=KC))\
                        .then_inc(xT_ready, 1)
                if live(s):
                    ln.normalise(dve, nc, s, par, xT_done)
            tile_steps(dve, step, lag=1)

            ch = Chain(dve, steps)
            dve.wait_ge(loaded, 16 * n_loads)
            dve.wait_ge(exp_ready, 1)
            ch.then(V.tensor_scalar(e1[:, :, :], e1[:, :, :], 1.0, None, ALU.add))
            ch.then(V.reciprocal(score[:, :, :], e1[:, :, :]))
            ch.then(V.tensor_tensor(sc_b[:, :, :], score[:, :, :],
                                    bias[:, :].unsqueeze(1).to_broadcast([P, NT, NE]), ALU.add))
            of_group = sc_b[:, :, :].rearrange("p t (g m) -> p (t g) m", g=NG)
            for n, (i, j) in enumerate(((0, 1), (0, 2), (0, 3), (1, 2), (1, 3), (2, 3))):
                ch.add(V.tensor_tensor(pairs[:, :, n], of_group[:, :, i], of_group[:, :, j], ALU.add))
            ch.done()
            ch.then(V.tensor_reduce(gs[:, :], pairs[:, :, :], AX.X, ALU.max))
            theirs = gs[:, :].rearrange("p (t g) -> p t g", g=NG).unsqueeze(2).to_broadcast([P, NT, NG, NG])
            own = gs[:, :].rearrange("p (t g) -> p t g", g=NG).unsqueeze(3).to_broadcast([P, NT, NG, NG])
            ch.add(V.tensor_tensor(gt[:, :, :, :], theirs, own, ALU.is_gt))
            ch.then(V.tensor_tensor(ge[:, :, :, :], theirs, own, ALU.is_ge))
            flat = lambda a: a[:, :, :, :].rearrange("p t g h -> p t (g h)")
            ch.then(V.tensor_tensor(flat(ge), flat(ge), before[:, :].unsqueeze(1).to_broadcast([P, NT, NG * NG]),
                                    ALU.mult))
            ch.then(V.tensor_tensor(flat(gt), flat(gt), flat(ge), ALU.max))
            ch.then(V.tensor_reduce(grank[:, :], gt[:, :, :, :].rearrange("p t g h -> p (t g) h"), AX.X, ALU.add))
            ch.then(V.tensor_scalar(gm[:, :], grank[:, :], float(TOP_GROUPS), None, ALU.is_lt))
            ch.add(V.tensor_scalar(gm1[:, :], gm[:, :], -1.0, None, ALU.add))
            per_group = lambda a: a[:, :].unsqueeze(2).to_broadcast([P, NT * NG, NE // NG])
            of_cand = cand[:, :, :].rearrange("p t (g m) -> p (t g) m", g=NG)
            ch.then(V.tensor_tensor(of_cand, of_group, per_group(gm), ALU.mult))
            ch.then(V.tensor_tensor(of_cand, of_cand, per_group(gm1), ALU.add))
            for t in range(NT):
                ch.add(V.max(best[:, t, :], cand[:, t, :]))
            ch.done()
            for t in range(NT):
                ch.add(V.max_index(best_i[:, t, :], best[:, t, :], cand[:, t, :]))
            ch.done()
            ch.then(V.tensor_copy(best_f[:, :, :], best_i[:, :, :]))
            for k in range(TOP):
                ch.add(V.tensor_tensor(hot[:, k, :, :], count16[:, :].unsqueeze(1).to_broadcast([P, NT, NE]),
                                       best_f[:, :, k:k + 1].to_broadcast([P, NT, NE]), ALU.is_equal))
            ch.done()
            ch.then(V.tensor_tensor(chosen[:, :, :], hot[:, 0, :, :], hot[:, 1, :, :], ALU.add))
            ch.then(V.tensor_tensor(chosen[:, :, :], chosen[:, :, :], hot[:, 2, :, :], ALU.add))
            V.tensor_tensor(chosen[:, :, :], chosen[:, :, :], hot[:, 3, :, :], ALU.add).then_inc(chosen_ready, 1)
            for k in range(TOP):
                ch.add(V.tensor_tensor(picked[:, k, :, :], hot[:, k, :, :], score[:, :, :], ALU.mult))
            ch.done()
            for k in range(TOP):
                ch.add(V.tensor_reduce(wk[:, :, k], picked[:, k, :, :], AX.X, ALU.add))
            ch.done()
            ch.then(V.tensor_reduce(wsum[:, :], wk[:, :, :], AX.X, ALU.add))
            ch.then(V.tensor_scalar(wsum[:, :], wsum[:, :], 1e-20, None, ALU.add))
            ch.then(V.reciprocal(wsum[:, :], wsum[:, :]))
            ch.add(V.scalar_tensor_tensor(c.weight[:, :, :], wk[:, :, :], 2.5,
                                          wsum[:, :].unsqueeze(2).to_broadcast([P, NT, TOP]), ALU.mult, ALU.mult))
            dve.wait_ge(counted, 1)
            ch.then(V.tensor_tensor_scan(incl[:, :, :].rearrange("p e t -> p (e t)"),
                                         carry[:, :, :].rearrange("p e t -> p (e t)"), ps_total[:, :], 0.0,
                                         ALU.mult, ALU.add))
            ch.add(V.tensor_tensor(excl[:, :, :].rearrange("p e t -> p (e t)"),
                                   incl[:, :, :].rearrange("p e t -> p (e t)"), ps_total[:, :], ALU.subtract))
            ch.then(V.tensor_scalar(tiles[:, :], incl[:, :, NT - 1], 1.0 / P, (P - 1) / 2 / P, ALU.mult, ALU.add))
            ch.then(V.tensor_scalar(tiles[:, :], tiles[:, :], ROUND, ROUND, ALU.add, ALU.subtract))
            ch.then(V.tensor_tensor_scan(ends[:, :], ones[:, 0:NE], tiles[:, :], 0.0, ALU.mult, ALU.add))
            ch.then(V.tensor_tensor(starts[:, :], ends[:, :], tiles[:, :], ALU.subtract))
            ch.then(V.scalar_tensor_tensor(excl[:, :, :], starts[:, :].unsqueeze(2).to_broadcast([P, NE, NT]), float(P),
                                           excl[:, :, :], ALU.mult, ALU.add))
            ch.then(V.tensor_tensor(slot_all[:, :, :].rearrange("p e t -> p (e t)"),
                                    excl[:, :, :].rearrange("p e t -> p (e t)"), ps_rank[:, :], ALU.add))
            for k in range(TOP):
                ch.add(V.tensor_tensor(picked[:, k, :, :], hot[:, k, :, :],
                                       slot_all[:, :, :].rearrange("p e t -> p t e"), ALU.mult))
            ch.done()
            for k in range(TOP):
                ch.add(V.tensor_reduce(slot_f[:, :, k], picked[:, k, :, :], AX.X, ALU.add))
            ch.done()
            ch.add(V.tensor_copy(c.slot[:, :, :], slot_f[:, :, :]))
            ch.then(V.tensor_tensor(owned[:, :, :], count_tiles[:, :].unsqueeze(2).to_broadcast([1, NS, NE]),
                                    ends[0:1, :].unsqueeze(1).to_broadcast([1, NS, NE]), ALU.is_ge))
            ch.then(V.tensor_reduce(owner_f[:, :], owned[:, :, :], AX.X, ALU.add))
            ch.then(V.tensor_scalar(c.owner[:, :], owner_f[:, :], NE - 1.0, None, ALU.min))


def shared_expert(nc, c, X, d):
    G = 4
    n = NT // G
    F = 2 * E
    with ExitStack() as ctx:
        ph = Phase(nc, ctx, "sh")
        wg, wu = ph.sb("wg", [P, KC, F]), ph.sb("wu", [P, KC, F])
        wd = ph.sb("wd", [P, F // P, E])
        xn = ph.sb("xn", [P, 2, G, E])
        xT = ph.sb("xT", [P, 2, KC, G * P])
        idx = ph.sb("idx", [P, 2, G * TOP], I32)
        act_g = ph.sb("act_g", [P, 2, G * P])
        gT = ph.sb("gT", [P, 2, F // P, G * P])
        ps_x = [ph.ps(f"x{i}") for i in range(2)]
        ps_g = [ph.ps(f"g{i}") for i in range(2)]
        ps_u = [ph.ps(f"u{i}") for i in range(2)]
        ps_o = [ph.ps(f"o{i}") for i in range(2)]
        loaded = ph.sem("loaded")
        xn_loaded = [ph.sem(f"xn_loaded{i}") for i in range(2)]
        scattered = [ph.sem(f"scattered{i}") for i in range(2)]
        idx_ready = ph.sem("idx_ready")
        xT_done, xT_ready = ph.sem("xT_done"), ph.sem("xT_ready")
        h_done, act_ready, g_ready = ph.sem("h_done"), ph.sem("act_ready"), ph.sem("g_ready")
        o_done, x_updated = ph.sem("o_done"), ph.sem("x_updated")
        block = ph.block()

        @block.sync
        def _(sp):
            sp.dma_start(wg[:, :, :], d["sh_wg"]).then_inc(loaded, 16)
            sp.dma_start(wu[:, :, :], d["sh_wu"]).then_inc(loaded, 16)
            sp.dma_start(wd[:, :, :], d["sh_wd"]).then_inc(loaded, 16)

            def step(s, par):
                if live(s, n):
                    if not (isinstance(s, int) and s < 2):
                        sp.wait_ge(xT_done, 2 * (s - 1))
                        sp.wait_ge(scattered[par], (s - par) * 8 * G * TOP)
                    sp.dma_start(xn[:, par, :, :], c.xn_dram[G * s:G * s + G, :, :].rearrange("t p e -> p t e")
                                 if isinstance(s, int) else
                                 c.xn_dram.rearrange("(n t) p e -> n p t e", t=G)[s, :, :, :])\
                        .then_inc(xn_loaded[par], 16)
            tile_steps(sp, step, n=n, lag=0)

        @block.gpsimd
        def _(pool):
            pool.wait_ge(c.zeroed, 16 * c.n_zeroed)

            def step(s, par):
                if live(s, n):
                    wait(pool, scattered[par], (s - par) * 8 * G * TOP)
                    nc.gpsimd.tensor_copy(idx[:, par, :],
                                          c.slot[:, :, :].rearrange("p (n t) k -> p n (t k)", t=G)[:, s, :])\
                        .then_inc(idx_ready, 1)
                    pool.wait_ge(idx_ready, s + 1)
                    wait_apart(pool, xn_loaded[par], s * 8 + (16 - 8 * par), c.passed_pool)
                    for i in range(G):
                        for k in range(TOP):
                            nc.gpsimd.indirect_dma_start(
                                c.xg_dram[:, :],
                                bass.IndirectOffsetOnAxis(ap=idx[:, par, TOP * i + k:TOP * i + k + 1], axis=0),
                                xn[:, par, i, :], None).then_inc(scattered[par], 16)
            tile_steps(pool, step, n=n, lag=0)
            for par in range(2):
                pool.wait_ge(scattered[par], 16 * G * TOP * n // 2)

        @block.scalar
        def _(act):
            act.dma_start(c.w1[:, :, :, :], d["moe_w1"]).then_inc(c.moe_loaded, 16)
            act.dma_start(c.w2[:, :, :, :], d["moe_w2"]).then_inc(c.moe_loaded, 16)

            def step(s, par):
                t = s - 1
                if live(t, n):
                    for f in range(4):
                        act.wait_ge(h_done, 4 * t + f + 1)
                        wait(act, g_ready, 4 * t + f - 1)
                        nc.scalar.activation(act_g[:, f % 2, :], ps_g[f % 2][:, :], ACT.Silu).then_inc(act_ready, 1)
            tile_steps(act, step, n=n, lag=1)

        @block.vector
        def _(dve):
            def step(s, par):
                p, e = s - 1, s - 2
                if live(s, n):
                    for k in range(KC):
                        dve.wait_ge(xT_done, 2 * s + k + 1)
                        wait(dve, h_done, 4 * (s - 1))
                        nc.vector.tensor_copy(xT[:, par, k, :], ps_x[k][:, :]).then_inc(xT_ready, 1)
                for f in range(4):
                    if live(p, n):
                        dve.wait_ge(act_ready, 4 * p + f + 1)
                        wait(dve, o_done, 4 * (p - 1))
                        nc.vector.tensor_tensor(gT[:, 1 - par, f, :], act_g[:, f % 2, :], ps_u[f % 2][:, :], ALU.mult)\
                            .then_inc(g_ready, 1)
                    if live(e, n):
                        dve.wait_ge(o_done, 4 * e + f + 1)
                        nc.vector.tensor_tensor(X[:, G * e + f, :], X[:, G * e + f, :], ps_o[f % 2][:, 0:E], ALU.add)\
                            .then_inc(x_updated, 1)
            tile_steps(dve, step, n=n, lag=2)

        @block.tensor
        def _(pe):
            pe.wait_ge(loaded, 16 * 3)

            def step(s, par):
                p, e = s - 1, s - 2
                if live(s, n):
                    pe.wait_ge(xn_loaded[par], s * 8 + (16 - 8 * par))
                    wait(pe, xT_ready, 2 * s)
                    for k in range(KC):
                        for i in range(G):
                            mm = nc.tensor.transpose(ps_x[k][:, i * P:(i + 1) * P], xn[:, par, i, k * P:(k + 1) * P],
                                                     c.ident[:, :])
                        mm.then_inc(xT_done, 1)
                for f in range(4):
                    if live(p, n):
                        wait(pe, g_ready, 4 * p + f - 1)
                        if f == 0:
                            pe.wait_ge(xT_ready, 2 * p + 2)
                        for ps, w in ((ps_g, wg), (ps_u, wu)):
                            for k in range(KC):
                                mm = nc.tensor.matmul(ps[f % 2][:, :], w[:, k, f * P:(f + 1) * P],
                                                      xT[:, 1 - par, k, :], start=(k == 0), stop=(k == KC - 1))
                        mm.then_inc(h_done, 1)
                    if live(e, n):
                        if f == 0:
                            pe.wait_ge(g_ready, 4 * e + 4)
                        wait(pe, x_updated, 4 * e + f - 1)
                        for k in range(F // P):
                            mm = nc.tensor.matmul(ps_o[f % 2][:, 0:E], gT[:, par, k, f * P:(f + 1) * P], wd[:, k, :],
                                                  start=(k == 0), stop=(k == F // P - 1))
                        mm.then_inc(o_done, 1)
            tile_steps(pe, step, n=n, lag=2)


def experts(nc, c, d):
    with ExitStack() as ctx:
        ph = Phase(nc, ctx, "ex")
        xg = ph.sb("xg", [P, 4, E])
        xT = ph.sb("xT", [P, 2, KC, P])
        act_g = ph.sb("act_g", [P, 2, E])
        g = ph.sb("g", [P, 2, E])
        gT = ph.sb("gT", [P, 2, KC, P])
        y = ph.sb("y", [P, 2, E])
        ps_h = [ph.ps(f"h{i}") for i in range(2)]
        ps_x, ps_g = ph.ps("x"), ph.ps("g")
        ps_y = [ph.ps(f"y{i}") for i in range(2)]
        x_loaded = [ph.sem(f"x_loaded{i}") for i in range(4)]
        stored = [ph.sem(f"stored{i}") for i in range(2)]
        xT_done, xT_ready = ph.sem("xT_done"), ph.sem("xT_ready")
        h_done, act_ready, g_ready = ph.sem("h_done"), ph.sem("act_ready"), ph.sem("g_ready")
        gT_done, gT_ready = ph.sem("gT_done"), ph.sem("gT_ready")
        y_done, y_ready = ph.sem("y_done"), ph.sem("y_ready")
        block = ph.block()

        def steps4(eng, step, lag):
            for s in range(8):
                step(s, s % 4)
            with eng.Fori(0, (NS - 8) // 4) as i:
                for u in range(4):
                    step(i * 4 + (8 + u), u)
            for s in range(NS, NS + lag):
                step(s, s % 4)

        @block.sync
        def _(sp):
            def step(s, q):
                if live(s, NS):
                    wait(sp, xT_done, s - 3)
                    sp.dma_start(xg[:, q, :], c.xg_dram.rearrange("(n p) e -> n p e", p=P)[s, :, :])\
                        .then_inc(x_loaded[q], 16)
            steps4(sp, step, 0)

        @block.tensor
        def _(pe):
            pe.wait_ge(c.moe_loaded, 32)

            def step(s, q):
                t, p, a, e = s, s - 1, s - 2, s - 3
                par = q % 2
                if live(p, NS):
                    own = pe.value_load(c.owner[0:1, bass.ds(p, 1)], min_val=0, max_val=NE - 1)
                    pe.wait_ge(xT_ready, p + 1)
                    wait(pe, g_ready, p - 1)
                    for k in range(KC):
                        mm = nc.tensor.matmul(ps_h[1 - par][:, :], xT[:, 1 - par, k, :], c.w1[:, own, k, :],
                                              start=(k == 0), stop=(k == KC - 1))
                    mm.then_inc(h_done, 1)
                if live(t, NS):
                    pe.wait_ge(x_loaded[q], (s - q) * 4 + 16)
                    wait(pe, xT_ready, t)
                    for k in range(KC):
                        mm = nc.tensor.transpose(ps_x[:, k * P:(k + 1) * P], xg[:, q, k * P:(k + 1) * P], c.ident[:, :])
                    mm.then_inc(xT_done, 1)
                if live(e, NS):
                    own = pe.value_load(c.owner[0:1, bass.ds(e, 1)], min_val=0, max_val=NE - 1)
                    pe.wait_ge(gT_ready, e + 1)
                    wait(pe, y_ready, e - 1)
                    for k in range(KC):
                        mm = nc.tensor.matmul(ps_y[1 - par][:, 0:E], gT[:, 1 - par, k, :], c.w2[:, own, k, :],
                                              start=(k == 0), stop=(k == KC - 1))
                    mm.then_inc(y_done, 1)
                if live(a, NS):
                    pe.wait_ge(g_ready, a + 1)
                    wait(pe, gT_ready, a)
                    for k in range(KC):
                        mm = nc.tensor.transpose(ps_g[:, k * P:(k + 1) * P], g[:, par, k * P:(k + 1) * P], c.ident[:, :])
                    mm.then_inc(gT_done, 1)
            steps4(pe, step, 3)

        @block.scalar
        def _(act):
            def step(s, q):
                p, a, e = s - 1, s - 2, s - 3
                par = q % 2
                if live(p, NS):
                    act.wait_ge(h_done, p + 1)
                    wait(act, g_ready, p - 1)
                    nc.scalar.activation(act_g[:, 1 - par, :], ps_h[1 - par][:, 0:E], ACT.Silu).then_inc(act_ready, 1)
                if live(e, NS):
                    act.wait_ge(y_done, e + 1)
                    wait(act, stored[1 - par], (e - (1 - par)) * 8)
                    nc.scalar.activation(y[:, 1 - par, :], ps_y[1 - par][:, 0:E], ACT.Copy).then_inc(y_ready, 1)
                    act.wait_ge(y_ready, e + 1)
                    act.dma_start(c.y_dram.rearrange("(n p) e -> n p e", p=P)[e, :, :], y[:, 1 - par, :])\
                        .then_inc(stored[1 - par], 16)
            steps4(act, step, 3)
            for par in range(2):
                act.wait_ge(stored[par], 16 * (NS // 2))

        @block.vector
        def _(dve):
            def step(s, q):
                t, p, a = s, s - 1, s - 2
                par = q % 2
                if live(p, NS):
                    dve.wait_ge(act_ready, p + 1)
                    wait(dve, gT_done, p - 1)
                    nc.vector.tensor_tensor(g[:, 1 - par, :], act_g[:, 1 - par, :], ps_h[1 - par][:, E:2 * E], ALU.mult)\
                        .then_inc(g_ready, 1)
                if live(t, NS):
                    dve.wait_ge(xT_done, t + 1)
                    wait(dve, h_done, t - 1)
                    nc.vector.tensor_copy(xT[:, par, :, :], ps_x[:, 0:E].rearrange("p (k t) -> p k t", k=KC))\
                        .then_inc(xT_ready, 1)
                if live(a, NS):
                    dve.wait_ge(gT_done, a + 1)
                    wait(dve, y_done, a - 1)
                    nc.vector.tensor_copy(gT[:, par, :, :], ps_g[:, 0:E].rearrange("p (k t) -> p k t", k=KC))\
                        .then_inc(gT_ready, 1)
            steps4(dve, step, 2)


def combine(nc, c, X):
    with ExitStack() as ctx:
        ph = Phase(nc, ctx, "cb")
        idx = ph.sb("idx", [P, 2, TOP], I32)
        y = ph.sb("y", [P, 2, TOP, E])
        idx_ready = ph.sem("idx_ready")
        gathered = [ph.sem(f"gathered{i}") for i in range(2)]
        added = ph.sem("added")
        block = ph.block()

        @block.gpsimd
        def _(pool):
            def step(s, par):
                if live(s):
                    wait(pool, added, TOP * (s - 1))
                    nc.gpsimd.tensor_copy(idx[:, par, :], c.slot[:, s, :]).then_inc(idx_ready, 1)
                    wait_apart(pool, idx_ready, s + 1, c.passed_pool)
                    for k in range(TOP):
                        nc.gpsimd.indirect_dma_start(
                            y[:, par, k, :], None, c.y_dram[:, :],
                            bass.IndirectOffsetOnAxis(ap=idx[:, par, k:k + 1], axis=0)).then_inc(gathered[par], 16)
            tile_steps(pool, step, lag=0)

        @block.vector
        def _(dve):
            def step(s, par):
                if live(s):
                    dve.wait_ge(gathered[par], (s - par) * 8 * TOP + 16 * TOP)
                    for k in range(TOP):
                        wait(dve, added, TOP * s + k)
                        nc.vector.scalar_tensor_tensor(X[:, s, :], y[:, par, k, :], c.weight[:, s, k:k + 1], X[:, s, :],
                                                       ALU.mult, ALU.add).then_inc(added, 1)
            tile_steps(dve, step, lag=0)


def cross_attention_1(nc, c, X, d):
    with ExitStack() as ctx:
        ph = Phase(nc, ctx, "xb")
        ctxT = ph.sb("ctxT", [P, 4, KC, 2 * S])
        ctx_rows = ph.sb("ctx_rows", [P, 4, SC, E])
        xT = ph.sb("xT", [P, 2, KC, P])
        sT = ph.sb("sT", [P, 2, SC, T])
        neg_max = ph.sb("neg_max", [P, 2])
        ex = ph.sb("ex", [P, 2, E])
        total, rz = ph.sb("total", [P, 2]), ph.sb("rz", [P, 2])
        ln = LayerNorm(ph, c, X)
        ps_x = [ph.ps(f"x{i}") for i in range(2)]
        ps_s = [ph.ps(f"s{i}") for i in range(2)]
        ps_o = [ph.ps(f"o{i}") for i in range(2)]
        ctx_loaded = [ph.sem(f"ctx_loaded{i}") for i in range(4)]
        xT_done, xT_ready = ph.sem("xT_done"), ph.sem("xT_ready")
        s_done, s_ready = ph.sem("s_done"), ph.sem("s_ready")
        o_done, max_ready, exp_ready = ph.sem("o_done"), ph.sem("max_ready"), ph.sem("exp_ready")
        rz_ready, x_updated = ph.sem("rz_ready"), ph.sem("x_updated")
        block = ph.block()

        @block.sync
        def _(sp):
            def step(s, q):
                if live(s):
                    wait(sp, s_done, s - 3)
                    sp.dma_start(ctxT[:, q, :, :], d["ctxT"][s, :, :, :]).then_inc(ctx_loaded[q], 16)
                    wait(sp, o_done, s - 3)
                    sp.dma_start(ctx_rows[:, q, :, :], d["ctx_rows"][s, :, :, :]).then_inc(ctx_loaded[q], 16)
            tile_steps(sp, step, lag=0, turn=4, peel=8)

        @block.gpsimd
        def _(pool):
            def step(s, q):
                if live(s):
                    ln.inverse_std(pool, nc, s, q % 2)
            tile_steps(pool, step, lag=0, turn=4, peel=8)

        @block.tensor
        def _(pe):
            def step(s, q):
                t, m, o = s - 1, s - 2, s - 3
                if live(m):
                    pe.wait_ge(ctx_loaded[(q - 2) % 4], (m - (q - 2) % 4) * 8 + 32)
                    pe.wait_ge(xT_ready, m + 1)
                    wait(pe, s_ready, m - 1)
                    for ch in range(SC):
                        for k in range(KC):
                            mm = nc.tensor.matmul(ps_s[q % 2][:, ch * T:(ch + 1) * T],
                                                  ctxT[:, (q - 2) % 4, k, ch * P:(ch + 1) * P],
                                                  xT[:, q % 2, k, (ch // 2) * T:(ch // 2 + 1) * T],
                                                  start=(k == 0), stop=(k == KC - 1))
                    mm.then_inc(s_done, 1)
                if live(t):
                    pe.wait_ge(ln.xn_ready, t + 1)
                    wait(pe, xT_ready, t - 1)
                    for k in range(KC):
                        mm = nc.tensor.transpose(ps_x[1 - q % 2][:, k * P:(k + 1) * P],
                                                 ln.xn[:, 1 - q % 2, k * P:(k + 1) * P], c.ident[:, :])
                    mm.then_inc(xT_done, 1)
                if live(o):
                    pe.wait_ge(s_ready, o + 1)
                    wait(pe, exp_ready, o - 1)
                    for ch in range(SC):
                        mm = nc.tensor.matmul(ps_o[1 - q % 2][(ch // 2) * T:(ch // 2 + 1) * T, 0:E],
                                              sT[:, 1 - q % 2, ch, :], ctx_rows[:, (q - 3) % 4, ch, :],
                                              start=(ch % 2 == 0), stop=(ch % 2 == 1))
                    mm.then_inc(o_done, 1)
            tile_steps(pe, step, lag=3, turn=4, peel=8)

        @block.scalar
        def _(act):
            def step(s, q):
                m, o = s - 2, s - 3
                if live(m):
                    act.wait_ge(s_done, m + 1)
                    wait(act, o_done, m - 1)
                    nc.scalar.activation(sT[:, q % 2, :, :].rearrange("p c t -> p (c t)"), ps_s[q % 2][:, 0:SC * T],
                                         ACT.Copy, scale=E ** -0.5).then_inc(s_ready, 1)
                if live(o):
                    act.wait_ge(max_ready, o + 1)
                    wait(act, x_updated, o - 1)
                    nc.scalar.activation(ex[:, 1 - q % 2, :], ps_o[1 - q % 2][:, 0:E], ACT.Exp,
                                         bias=neg_max[:, 1 - q % 2:2 - q % 2],
                                         accum_out=total[:, 1 - q % 2:2 - q % 2]).then_inc(exp_ready, 1)
            tile_steps(act, step, lag=3, turn=4, peel=8)

        @block.vector
        def _(dve):
            def step(s, q):
                t, o = s - 1, s - 3
                par = q % 2
                if live(s):
                    ln.statistics(dve, nc, s, par)
                if live(t):
                    dve.wait_ge(xT_done, t + 1)
                    wait(dve, s_done, t - 1)
                    nc.vector.tensor_copy(xT[:, 1 - par, :, :], ps_x[1 - par][:, 0:E].rearrange("p (k t) -> p k t", k=KC))\
                        .then_inc(xT_ready, 1)
                if live(o):
                    dve.wait_ge(o_done, o + 1)
                    nc.vector.tensor_reduce(neg_max[:, 1 - par:2 - par], ps_o[1 - par][:, 0:E], AX.X, ALU.max,
                                            negate=True).then_inc(max_ready, 1)
                if live(s):
                    ln.normalise(dve, nc, s, par, xT_done)
                if live(o):
                    dve.wait_ge(exp_ready, o + 1)
                    nc.vector.reciprocal(rz[:, 1 - par:2 - par], total[:, 1 - par:2 - par]).then_inc(rz_ready, 1)
                    dve.wait_ge(rz_ready, o + 1)
                    nc.vector.scalar_tensor_tensor(X[:, o, :], ex[:, 1 - par, :], rz[:, 1 - par:2 - par], X[:, o, :],
                                                   ALU.mult, ALU.add).then_inc(x_updated, 1)
            tile_steps(dve, step, lag=3, turn=4, peel=8)


def feed_forward(nc, c, X, d):
    G, n, F = 4, NT // 4, 1024
    FC = F // P
    W = G * P
    with ExitStack() as ctx:
        ph = Phase(nc, ctx, "ff")
        w_raw = [ph.sb("w1_raw", [P, KC * F]), ph.sb("w2_raw", [P, FC * E])]
        w1 = ph.sb("w1", [P, KC, F], BF16)
        w2 = ph.sb("w2", [P, FC, E], BF16)
        cw, cb = ph.sb("cw", [P, FC, 3]), ph.sb("cb", [P, FC])
        ones = ph.sb("ones", [P, P])
        w_sum, w_scale = ph.sb("w_sum", [P, 2]), ph.sb("w_scale", [P, 2])
        w_mean = ph.sb("w_mean", [P, 2])
        rounding = ph.sb("rounding", [P, 2])
        stats = ph.sb("stats", [P, G, 6])
        mv = ph.sb("mv", [P, G, 2])
        var_eps, rstd = ph.sb("var_eps", [P, G]), ph.sb("rstd", [P, G])
        xn = ph.sb("xn", [P, G, E])
        xr = ph.sb("xr", [P, G, E])
        top1, top2 = ph.sb("top1", [P, G]), ph.sb("top2", [P, G])
        scale1, scale2 = ph.sb("scale1", [P, G]), ph.sb("scale2", [P, G])
        back1, back2 = ph.sb("back1", [P, G]), ph.sb("back2", [P, 2, G])
        diag1, diag2 = ph.sb("diag1", [P, G, P]), ph.sb("diag2", [P, G, P])
        xqT = ph.sb("xqT", [P, 2, KC, W], BF16)
        back_b = ph.sb("back_b", [P, 2, W])
        scale_b = ph.sb("scale_b", [P, 2, W])
        h = ph.sb("h", [P, 2, W])
        y = ph.sb("y", [P, 2, FC, W])
        peak = ph.sb("peak", [P, 2, W])
        hq = ph.sb("hq", [P, 2, FC, W], BF16)
        ps_h = [ph.ps(f"h{i}") for i in range(2)]
        ps_x = [ph.ps(f"x{i}") for i in range(2)]
        ps_t, ps_b = ph.ps("t"), ph.ps("b")
        ps_o = [ph.ps(f"o{i}") for i in range(2)]
        loaded, n_loads = ph.sem("loaded"), 4
        consts_set, w_summed, w_totalled = ph.sem("consts_set"), ph.sem("w_summed"), ph.sem("w_totalled")
        prepared, w_ready = ph.sem("prepared"), ph.sem("w_ready")
        stats_done, var_ready, eps_added = ph.sem("stats_done"), ph.sem("var_ready"), ph.sem("eps_added")
        rstd_ready, xn_ready = ph.sem("rstd_ready"), ph.sem("xn_ready")
        top1_ready, scale1_ready = ph.sem("top1_ready"), ph.sem("scale1_ready")
        xr_ready, diag1_ready = ph.sem("xr_ready"), ph.sem("diag1_ready")
        xT_done, xqT_ready = ph.sem("xT_done"), ph.sem("xqT_ready")
        back_done, back_ready = ph.sem("back_done"), ph.sem("back_ready")
        h_done, h_ready = ph.sem("h_done"), ph.sem("h_ready")
        tap1_ready, tap0_ready, taps_ready = ph.sem("tap1_ready"), ph.sem("tap0_ready"), ph.sem("taps_ready")
        silu_ready, peak_ready, peak_done = ph.sem("silu_ready"), ph.sem("peak_ready"), ph.sem("peak_done")
        top2_ready, scale2_ready = ph.sem("top2_ready"), ph.sem("scale2_ready")
        diag2_ready, scale_done, scale_ready = ph.sem("diag2_ready"), ph.sem("scale_done"), ph.sem("scale_ready")
        scaled, rounded, hq_ready = ph.sem("scaled"), ph.sem("rounded"), ph.sem("hq_ready")
        o_done, x_updated = ph.sem("o_done"), ph.sem("x_updated")

        def unit(s, f, ahead):
            g = s - 1 - (1 if f < ahead else 0)
            return g, (f - ahead) % FC
        block = ph.block()

        @block.sync
        def _(sp):
            sp.dma_start(w_raw[0][:, :], d["ff_w1T"].rearrange("p k n -> p (k n)")).then_inc(loaded, 16)
            sp.dma_start(w_raw[1][:, :], d["ff_w2T"].rearrange("p k n -> p (k n)")).then_inc(loaded, 16)
            sp.dma_start(cw[:, :, :], d["ff_cw"]).then_inc(loaded, 16)
            sp.dma_start(cb[:, :], d["ff_cb"]).then_inc(loaded, 16)

        @block.gpsimd
        def _(pool):
            nc.gpsimd.memset(rounding[:, 0:1], ROUND).then_inc(consts_set, 1)
            nc.gpsimd.memset(rounding[:, 1:2], -ROUND).then_inc(consts_set, 1)
            nc.gpsimd.memset(ones[:, :], 1.0).then_inc(consts_set, 1)

            def step(s, par):
                for f in range(FC):
                    if f == 2 and live(s, n):
                        wait_apart(pool, var_ready, s + 1, c.passed_pool)
                        nc.gpsimd.tensor_scalar(var_eps[:, :], mv[:, :, 1], LN_EPS, None, ALU.add).then_inc(eps_added, 1)
                        pool.wait_ge(eps_added, s + 1)
                        nc.gpsimd.tensor_tensor(rstd[:, :], var_eps[:, :], c.minus_half[:, 0:1].to_broadcast([P, G]),
                                                ALU.pow).then_inc(rstd_ready, 1)
                    g, j = (s - 2 if f >= 5 else s - 3), (f - 5) % FC
                    if live(g, n):
                        gp = (par + (f < 5)) % 2
                        pool.wait_ge(scale_ready, g + 1)
                        nc.gpsimd.tensor_tensor(y[:, gp, j, :], y[:, gp, j, :], scale_b[:, gp, :], ALU.mult)\
                            .then_inc(scaled, 1)
                    g, j = (s - 2, f - 6) if f >= 6 else (s - 3, f + 2)
                    if live(g, n):
                        gp = (par + (f < 6)) % 2
                        pool.wait_ge(scaled, FC * g + j + 1)
                        nc.gpsimd.tensor_tensor(y[:, gp, j, :], y[:, gp, j, :],
                                                rounding[:, 0:1].to_broadcast([P, W]), ALU.add).then_inc(rounded, 1)
            tile_steps(pool, step, n=n, lag=3)

        @block.vector
        def _(dve):
            V = nc.vector
            ch = Chain(dve, prepared)
            dve.wait_ge(loaded, 16 * n_loads)
            for i in range(2):
                V.tensor_reduce(w_sum[:, i:i + 1], w_raw[i][:, :], AX.X, ALU.add, apply_absolute_value=True)\
                    .then_inc(w_summed, 1)
            dve.wait_ge(w_totalled, 1)
            ch.then(V.tensor_scalar(w_mean[:, :], ps_t[:, 0:2], 1.0 / (F * E), 1e-5, ALU.mult, ALU.max))
            ch.then(V.reciprocal(w_scale[:, :], w_mean[:, :]))
            for i in range(2):
                ch.add(V.tensor_scalar(w_raw[i][:, :], w_raw[i][:, :], w_scale[:, i:i + 1], ROUND, ALU.mult, ALU.add))
            ch.done()
            for i in range(2):
                ch.add(V.tensor_scalar(w_raw[i][:, :], w_raw[i][:, :], ROUND, 1.0, ALU.subtract, ALU.min))
            ch.done()
            for i, w in enumerate((w1, w2)):
                V.tensor_scalar(w[:, :, :].rearrange("p k n -> p (k n)"), w_raw[i][:, :], -1.0, None, ALU.max)\
                    .then_inc(w_ready, 1)
            dve.wait_ge(consts_set, 3)

            def step(s, par):
                q, r = s - 2, s - 3
                for f in range(FC):
                    g = s - 1
                    if live(g, n):
                        if f == 0:
                            dve.wait_ge(back_ready, g + 1)
                        dve.wait_ge(h_done, FC * g + f + 1)
                        wait(dve, taps_ready, FC * g + f - 1)
                        V.tensor_tensor(h[:, f % 2, :], ps_h[f % 2][:, :], back_b[:, 1 - par, :], ALU.mult)\
                            .then_inc(h_ready, 1)
                    g, j = unit(s, f, 1)
                    if live(g, n):
                        yb = y[:, (par + 1 + (f < 1)) % 2, j, :].rearrange("p (b t) -> p b t", t=T)
                        hb = h[:, j % 2, :].rearrange("p (b t) -> p b t", t=T)
                        dve.wait_ge(tap1_ready, FC * g + j + 1)
                        V.scalar_tensor_tensor(yb[:, :, 1:T], hb[:, :, 0:T - 1], cw[:, j, 0:1], yb[:, :, 1:T],
                                               ALU.mult, ALU.add).then_inc(tap0_ready, 1)
                        dve.wait_ge(tap0_ready, FC * g + j + 1)
                        V.scalar_tensor_tensor(yb[:, :, 0:T - 1], hb[:, :, 1:T], cw[:, j, 2:3], yb[:, :, 0:T - 1],
                                               ALU.mult, ALU.add).then_inc(taps_ready, 1)
                    g, half = (s - 1, 0) if f == 6 else (q, 1)
                    if f in (2, 6) and live(g, n):
                        dve.wait_ge(silu_ready, FC * g + 4 * half + 4)
                        wait(dve, peak_done, g)
                        V.tensor_reduce(peak[:, half, :],
                                        y[:, (par + 1 + half) % 2, 4 * half:4 * half + 4, :].rearrange("p j t -> p t j"),
                                        AX.X, ALU.max, apply_absolute_value=True).then_inc(peak_ready, 1)
                        if half:
                            dve.wait_ge(peak_ready, 3 * g + 2)
                            V.tensor_tensor(peak[:, 0, :], peak[:, 0, :], peak[:, 1, :], ALU.max).then_inc(peak_ready, 1)
                    if f == 0 and live(s, n):
                        for i in range(G):
                            V.bn_stats(stats[:, i, :], X[:, s * G + i, :]).then_inc(stats_done, 1)
                    if f == 1 and live(s, n):
                        wait_apart(dve, stats_done, G * s + G, c.passed_dve)
                        for i in range(G):
                            ins = V.bn_aggr(mv[:, i, :], stats[:, i, :])
                        ins.then_inc(var_ready, 1)
                    if f == 3 and live(s, n):
                        dve.wait_ge(rstd_ready, s + 1)
                        wait(dve, xr_ready, s)
                        for i in range(G):
                            ins = V.tensor_scalar(xn[:, i, :], X[:, s * G + i, :], mv[:, i, 0:1], rstd[:, i:i + 1],
                                                  ALU.subtract, ALU.mult)
                        ins.then_inc(xn_ready, 1)
                    if f == 4 and live(s, n):
                        dve.wait_ge(xn_ready, s + 1)
                        wait(dve, diag1_ready, s)
                        V.tensor_reduce(top1[:, :], xn[:, :, :], AX.X, ALU.max, apply_absolute_value=True)\
                            .then_inc(top1_ready, 1)
                        dve.wait_ge(top1_ready, 3 * s + 1)
                        V.tensor_scalar(top1[:, :], top1[:, :], 1e-5, None, ALU.max).then_inc(top1_ready, 1)
                        dve.wait_ge(top1_ready, 3 * s + 2)
                        V.reciprocal(scale1[:, :], top1[:, :]).then_inc(top1_ready, 1)
                        dve.wait_ge(top1_ready, 3 * s + 3)
                        V.tensor_scalar(scale1[:, :], scale1[:, :], 127.0, None, ALU.mult)
                        V.tensor_scalar(back1[:, :], top1[:, :], w_mean[:, 0:1], 1.0 / 127, ALU.mult, ALU.mult)\
                            .then_inc(scale1_ready, 1)
                    if f == 3 and live(q, n):
                        dve.wait_ge(peak_done, q + 1)
                        wait(dve, diag2_ready, q)
                        V.tensor_reduce(top2[:, :], ps_t[:, :].rearrange("p (i c) -> p i c", i=G), AX.X, ALU.max)\
                            .then_inc(top2_ready, 1)
                        dve.wait_ge(top2_ready, 3 * q + 1)
                        V.tensor_scalar(top2[:, :], top2[:, :], 1e-5, None, ALU.max).then_inc(top2_ready, 1)
                        dve.wait_ge(top2_ready, 3 * q + 2)
                        V.reciprocal(scale2[:, :], top2[:, :]).then_inc(top2_ready, 1)
                        dve.wait_ge(top2_ready, 3 * q + 3)
                        V.tensor_scalar(scale2[:, :], scale2[:, :], 127.0, None, ALU.mult)
                        V.tensor_scalar(back2[:, par, :], top2[:, :], w_mean[:, 1:2], 1.0 / 127, ALU.mult, ALU.mult)\
                            .then_inc(scale2_ready, 1)
                    if f == 7 and live(r, n):
                        for i in range(G):
                            dve.wait_ge(o_done, G * r + i + 1)
                            V.scalar_tensor_tensor(X[:, r * G + i, :], ps_o[i % 2][:, 0:E], back2[:, 1 - par, i:i + 1],
                                                   X[:, r * G + i, :], ALU.mult, ALU.add).then_inc(x_updated, 1)
            tile_steps(dve, step, n=n, lag=3)

        @block.scalar
        def _(act):
            act.wait_ge(consts_set, 3)

            def step(s, par):
                q = s - 2
                for f in range(FC):
                    if f == 5 and live(q, n):
                        act.wait_ge(scale_done, q + 1)
                        wait(act, scaled, FC * (q - 1))
                        nc.scalar.activation(scale_b[:, par, :], ps_b[:, :], ACT.Copy).then_inc(scale_ready, 1)
                    g = s - 1
                    if live(g, n):
                        act.wait_ge(h_ready, FC * g + f + 1)
                        wait(act, hq_ready, FC * (g - 2) + f + 1)
                        nc.scalar.activation(y[:, 1 - par, f, :], h[:, f % 2, :], ACT.Identity, bias=cb[:, f:f + 1],
                                             scale=cw[:, f, 1:2]).then_inc(tap1_ready, 1)
                    g, j = unit(s, f, 2)
                    if live(g, n):
                        yj = y[:, (par + 1 + (f < 2)) % 2, j, :]
                        act.wait_ge(taps_ready, FC * g + j + 1)
                        nc.scalar.activation(yj, yj, ACT.Silu).then_inc(silu_ready, 1)
                    g, j = (q, f - 7) if f >= 7 else (s - 3, f + 1)
                    if live(g, n):
                        gp = (par + (f < 7)) % 2
                        act.wait_ge(rounded, FC * g + j + 1)
                        nc.scalar.activation(hq[:, gp, j, :], y[:, gp, j, :], ACT.Identity,
                                             bias=rounding[:, 1:2]).then_inc(hq_ready, 1)
                    if f == 3 and live(q, n):
                        act.wait_ge(scale2_ready, q + 1)
                        wait(act, scale_done, q)
                        for i in range(G):
                            ins = nc.scalar.activation(diag2[:, i, :], c.ident[:, :], ACT.Copy, scale=scale2[:, i:i + 1])
                        ins.then_inc(diag2_ready, 1)
                    if f == 5 and live(s, n):
                        act.wait_ge(scale1_ready, s + 1)
                        wait(act, xT_done, KC * s)
                        for i in range(G):
                            ins = nc.scalar.activation(xr[:, i, :], xn[:, i, :], ACT.Identity, bias=rounding[:, 0:1],
                                                       scale=scale1[:, i:i + 1])
                        ins.then_inc(xr_ready, 1)
                        wait(act, back_done, s)
                        for i in range(G):
                            ins = nc.scalar.activation(diag1[:, i, :], c.ident[:, :], ACT.Copy, scale=back1[:, i:i + 1])
                        ins.then_inc(diag1_ready, 1)
                    if f == 7 and live(s, n):
                        wait(act, h_done, FC * (s - 1))
                        for k in range(KC):
                            act.wait_ge(xT_done, KC * s + k + 1)
                            nc.scalar.activation(xqT[:, par, k, :], ps_x[k][:, :], ACT.Identity,
                                                 bias=rounding[:, 1:2]).then_inc(xqT_ready, 1)
                        act.wait_ge(back_done, s + 1)
                        wait(act, h_ready, FC * (s - 1))
                        nc.scalar.activation(back_b[:, par, :], ps_b[:, :], ACT.Copy).then_inc(back_ready, 1)
            tile_steps(act, step, n=n, lag=3)

        @block.tensor
        def _(pe):
            pe.wait_ge(consts_set, 3)
            pe.wait_ge(w_summed, 2)
            nc.tensor.matmul(ps_t[:, 0:2], ones[:, :], w_sum[:, :], start=True, stop=True).then_inc(w_totalled, 1)
            pe.wait_ge(w_ready, 2)

            def step(s, par):
                q, r = s - 2, s - 3
                for f in range(FC):
                    g = s - 1
                    if live(g, n):
                        if f == 0:
                            pe.wait_ge(xqT_ready, KC * g + KC)
                        wait(pe, h_ready, FC * g + f - 1)
                        for k in range(KC):
                            mm = nc.tensor.matmul(ps_h[f % 2][:, :], w1[:, k, f * P:(f + 1) * P],
                                                  xqT[:, 1 - par, k, :], start=(k == 0), stop=(k == KC - 1))
                        mm.then_inc(h_done, 1)
                    if f == 2 and live(q, n):
                        pe.wait_ge(peak_ready, 3 * q + 3)
                        wait(pe, top2_ready, 3 * q)
                        for i in range(G):
                            mm = nc.tensor.transpose(ps_t[:, i * P:(i + 1) * P], peak[:, 0, i * P:(i + 1) * P],
                                                     c.ident[:, :])
                        mm.then_inc(peak_done, 1)
                    if f == 4 and live(q, n):
                        pe.wait_ge(diag2_ready, q + 1)
                        pe.wait_ge(back_ready, q + 2 if not isinstance(q, int) else min(n, q + 2))
                        nc.tensor.matmul(ps_b[:, :], ones[:, :], diag2[:, :, :].rearrange("p i t -> p (i t)"),
                                         start=True, stop=True).then_inc(scale_done, 1)
                    if f == 6 and live(s, n):
                        pe.wait_ge(xr_ready, s + 1)
                        wait(pe, xqT_ready, KC * s)
                        for k in range(KC):
                            for i in range(G):
                                mm = nc.tensor.transpose(ps_x[k][:, i * P:(i + 1) * P], xr[:, i, k * P:(k + 1) * P],
                                                         c.ident[:, :])
                            mm.then_inc(xT_done, 1)
                        pe.wait_ge(diag1_ready, s + 1)
                        wait(pe, scale_ready, s - 1)
                        wait(pe, back_ready, s)
                        nc.tensor.matmul(ps_b[:, :], ones[:, :], diag1[:, :, :].rearrange("p i t -> p (i t)"),
                                         start=True, stop=True).then_inc(back_done, 1)
                    if f >= 6 and live(r, n):
                        pe.wait_ge(hq_ready, FC * r + FC)
                        for i in (2 * (f - 6), 2 * (f - 6) + 1):
                            wait(pe, x_updated, G * r + i - 1)
                            for k in range(FC):
                                mm = nc.tensor.matmul(ps_o[i % 2][:, 0:E], hq[:, 1 - par, k, i * P:(i + 1) * P],
                                                      w2[:, k, :], start=(k == 0), stop=(k == FC - 1))
                            mm.then_inc(o_done, 1)
            tile_steps(pe, step, n=n, lag=3)


class Constants:
    pass


def kernel_program(nc, d, out):
    with ExitStack() as ctx:
        ph = Phase(nc, ctx, "g")
        X = ph.sb("x", [P, NT, E])
        c = Constants()
        c.ident = ph.sb("ident", [P, P])
        c.head_mask = ph.sb("head_mask", [P, HG])
        c.minus_half = ph.sb("minus_half", [P, 1])
        c.loaded, c.n_loads = ph.sem("const_loaded"), 3
        x_loaded = [ph.sem(f"x_loaded{i}") for i in range(4)]
        stored = ph.sem("stored")
        c.passed_dve, c.passed_pool = ph.sem("passed_dve"), ph.sem("passed_pool")
        with nc.Block() as block:
            @block.sync
            def _(sp):
                q = NT // 4
                for i in range(4):
                    sp.dma_start(X[:, i * q:(i + 1) * q, :],
                                 d["x"].rearrange("t p e -> p t e")[:, i * q:(i + 1) * q, :]).then_inc(x_loaded[i], 16)

            @block.scalar
            def _(act):
                act.dma_start(c.ident[:, :], d["ident"]).then_inc(c.loaded, 16)
                act.dma_start(c.head_mask[:, :], d["head_mask"]).then_inc(c.loaded, 16)
                act.dma_start(c.minus_half[:, :], d["minus_half"]).then_inc(c.loaded, 16)

            @block.gpsimd
            def _(pool):
                pool.wait_ge(c.loaded, 16 * c.n_loads)
        cross_attention_0(nc, c, X, d, x_loaded)
        causal_attention(nc, c, X, d, 0)
        c.xn_dram = nc.dram_tensor("xn_rows", [NT, P, E], F32).ap()
        c.xg_dram = nc.dram_tensor("expert_rows", [NS * P, E], F32).ap()
        c.y_dram = nc.dram_tensor("expert_outs", [NS * P, E], F32).ap()
        with ExitStack() as moe:
            mp = Phase(nc, moe, "moe")
            c.slot = mp.sb("slot", [P, NT, TOP], I32)
            c.weight = mp.sb("weight", [P, NT, TOP])
            c.owner = mp.sb("owner", [1, NS], I32)
            c.moe_loaded = mp.sem("loaded")
            c.zeroed, c.n_zeroed = mp.sem("zeroed"), 0
            clear_lists(nc, c)
            route(nc, c, X, d)
            with ExitStack() as weights:
                wp = Phase(nc, weights, "moew")
                c.w1 = wp.sb("w1", [P, NE, KC, 2 * E])
                c.w2 = wp.sb("w2", [P, NE, KC, E])
                shared_expert(nc, c, X, d)
                experts(nc, c, d)
            combine(nc, c, X)
        cross_attention_1(nc, c, X, d)
        causal_attention(nc, c, X, d, 1)
        feed_forward(nc, c, X, d)
        with nc.Block() as block:
            @block.sync
            def _(sp):
                sp.dma_start(out.rearrange("t p e -> p t e"), X[:, :, :]).then_inc(stored, 16)
                sp.wait_ge(stored, 16)


def laid_out(i):
    f = {k: np.asarray(v) for k, v in i.items()}
    c = np.ascontiguousarray

    def rows(w):
        return c(w.reshape(w.shape[0] // P, P, -1).transpose(1, 0, 2))

    pair = lambda w: c(w.reshape(H // 2, 2, D, -1).transpose(0, 2, 1, 3).reshape(P, 2, -1))
    q, k = np.arange(P)[:, None], np.arange(P)[None, :]
    in_order = (q // T == k // T) & (k <= q)
    pad = f["mask_BxS2_bf0"]
    return {
        "x": c(f["x"].reshape(NT, P, E)),
        "ctxT": c(f["ctx_1024"].reshape(NT, 2 * S, KC, P).transpose(0, 3, 2, 1)),
        "ctx_rows": c(f["ctx_1024"].reshape(NT, SC, P, E).transpose(0, 2, 1, 3)),
        "attn_mask": f["fside_SxS2_0"],
        "pad": c(pad.reshape(1, B, S)),
        "padT": c(pad.reshape(NT, SC, P).transpose(2, 0, 1)),
        "xa_wqT": rows(f["L0_xattn_Wq"].T), "xa_wkT": rows(f["L0_xattn_Wk"].T), "xa_wvT": rows(f["L0_xattn_Wv"].T),
        "xa_woP": pair(f["L0_xattn_Wo"].T),
        "xa_bq": c(f["L0_xattn_bq"].reshape(KC, P).T), "xa_bk": c(f["L0_xattn_bk"].reshape(KC, P).T),
        "xa_bvP": c(pair(f["L0_xattn_bv"][:, None])[:, :, 0]),
        "xa_bo": c(f["L0_xattn_bo"].reshape(1, E)),
        "sa0_wqkvT": rows(np.concatenate([f["L0_attn_Wq"].T, f["L0_attn_Wk"].T, f["L0_attn_Wv"].T], 1)),
        "sa0_woT": rows(f["L0_attn_Wo"].T),
        "sa0_mask": c(np.where(in_order.T, 0.5, 0.0).astype(np.float32)),
        "sa1_wqkvT": rows(f["L1_attn_Wqkv"].T), "sa1_woT": rows(f["L1_attn_Wout"].T),
        "sa1_mask": np.where(in_order, 0.0, MASKED).astype(np.float32),
        "sa1_bo": c(f["L1_attn_bout"].reshape(1, E)),
        "rt_w": rows(f["L0_ffn_router_w"].T), "rt_bias": c(f["L0_ffn_bias"].reshape(1, NE)),
        "rt_before": np.tile((np.arange(NG)[None, :] < np.arange(NG)[:, None]).reshape(1, -1), (P, 1)).astype(np.float32),
        "rt_upper": (q < k).astype(np.float32), "rt_ones": np.ones((P, P), np.float32),
        "rt_count16": np.tile(np.arange(NE, dtype=np.float32), (P, 1)),
        "rt_count_tiles": np.arange(NS, dtype=np.float32)[None],
        "rt_carry": np.tile((np.arange(NT) > 0).astype(np.float32), (P, NE, 1)),
        "sh_wg": rows(f["L0_ffn_sh_gate_w"]), "sh_wu": rows(f["L0_ffn_sh_up_w"]), "sh_wd": rows(f["L0_ffn_sh_down_w"]),
        "moe_w1": c(np.concatenate([f["L0_ffn_gate_w"], f["L0_ffn_up_w"]], 2)
                    .reshape(NE, KC, P, 2 * E).transpose(2, 0, 1, 3)),
        "moe_w2": c(f["L0_ffn_down_w"].reshape(NE, KC, P, E).transpose(2, 0, 1, 3)),
        "ff_w1T": rows(f["L1_ffn_w1"].T), "ff_w2T": rows(f["L1_ffn_w2"].T),
        "ff_cw": rows(f["L1_ffn_conv_w"].reshape(-1, 3)), "ff_cb": rows(f["L1_ffn_conv_b"].reshape(-1, 1))[:, :, 0],
        "ident": np.eye(P, dtype=np.float32),
        "head_mask": (np.arange(P)[:, None] // D == np.arange(HG)[None, :]).astype(np.float32),
        "minus_half": np.full((P, 1), -0.5, np.float32),
    }


def kernel(**inputs):
    import concourse.bacc as bacc
    from concourse.bass_utils import run_bass_kernel_spmd

    nc = bacc.Bacc("TRN2", target_bir_lowering=False, num_devices=1)
    arrays = {f"in_{name}_dram": a for name, a in laid_out(inputs).items()}
    d = {name[3:-5]: nc.dram_tensor(name, a.shape, mybir.dt.from_np(a.dtype), kind="ExternalInput").ap()
         for name, a in arrays.items()}
    out = nc.dram_tensor("out_dram", (NT, P, E), F32, kind="ExternalOutput").ap()
    kernel_program(nc, d, out)
    result = run_bass_kernel_spmd(nc, [arrays], core_ids=[0])
    return result.results[0]["out_dram"].reshape(B, T, E)
```

```python
from contextlib import ExitStack

import numpy as np

import concourse.bass as bass
from concourse import mybir

F32 = mybir.dt.float32
BF16 = mybir.dt.bfloat16
F32R = mybir.dt.float32r
THREE_PASSES = ((0, 0), (0, 1), (1, 0))
I32 = mybir.dt.int32
U8 = mybir.dt.uint8
ALU = mybir.AluOpType
ACT = mybir.ActivationFunctionType
AX = mybir.AxisListType

P = 128
B, T, S, E = 64, 64, 256, 256
H, D = 16, 16
NT = B * T // P
KC = E // P
SC = 2 * S // P
HG = H // KC
D1 = D + 1
MASKED = -1e30
NE, NG, TOP, TOP_GROUPS = 16, 4, 4, 2
NS = (B * T * TOP + NE * (P - 1)) // P + 1
NS += -NS % 4
ZERO_TILES = 12
ROUND = 1.5 * 2.0 ** 23
LN_EPS = 1e-5


class Phase:

    def __init__(self, nc, ctx, name):
        self.nc, self.ctx, self.name, self.sems = nc, ctx, name, []

    def sb(self, name, shape, dt=F32):
        return self.ctx.enter_context(self.nc.sbuf_tensor(f"{self.name}_{name}", shape, dt))

    def ps(self, name, dt=F32):
        return self.ctx.enter_context(self.nc.psum_tensor(f"{self.name}_ps_{name}", [P, 512], dt))

    def sem(self, name):
        s = self.ctx.enter_context(self.nc.semaphore(f"{self.name}_{name}"))
        self.sems.append(s)
        return s

    def block(self):
        self.ctx.callback(self.clear_semaphores)
        return self.ctx.enter_context(self.nc.Block())

    def clear_semaphores(self):
        numbers = sorted(s.num for s in self.sems)
        with self.nc.Block() as block:
            @block.gpsimd
            def _(pool):
                first = last = numbers[0]
                for number in numbers[1:] + [None]:
                    if number != last + 1:
                        pool.sem_clear(range(first, last + 1))
                        first = number
                    last = number


def wait(eng, sem, value):
    if isinstance(value, int) and value <= 0:
        return
    eng.wait_ge(sem, value)


def wait_apart(eng, sem, value, passed):
    eng.wait_ge(sem, value)
    if not isinstance(value, int):
        eng.sem_inc(passed)


def live(t, n=NT):
    return not isinstance(t, int) or 0 <= t < n


def tile_steps(eng, step, n=NT, lag=2, peel=4, turn=2):
    for s in range(peel):
        step(s, s % turn)
    with eng.Fori(0, (n - peel) // turn) as i:
        for u in range(turn):
            step(i * turn + (peel + u), u)
    for s in range(n, n + lag):
        step(s, s % turn)


class LayerNorm:

    def __init__(self, ph, c, x):
        self.c, self.x = c, x
        self.stats = ph.sb("ln_stats", [P, 2, 6])
        self.mv = ph.sb("ln_mv", [P, 2, 2])
        self.rstd = ph.sb("ln_rstd", [P, 2, 2])
        self.xn = ph.sb("xn", [P, 2, E])
        self.stats_done = ph.sem("ln_stats_done")
        self.var_ready = ph.sem("ln_var_ready")
        self.eps_added = ph.sem("ln_eps_added")
        self.rstd_ready = ph.sem("ln_rstd_ready")
        self.xn_ready = ph.sem("xn_ready")

    def statistics(self, dve, nc, t, par):
        nc.vector.bn_stats(self.stats[:, par, :], self.x[:, t, :]).then_inc(self.stats_done, 1)
        wait_apart(dve, self.stats_done, t + 1, self.c.passed_dve)
        nc.vector.bn_aggr(self.mv[:, par, :], self.stats[:, par, :]).then_inc(self.var_ready, 1)

    def inverse_std(self, pool, nc, t, par):
        wait_apart(pool, self.var_ready, t + 1, self.c.passed_pool)
        nc.gpsimd.tensor_scalar(self.rstd[:, par, 0:1], self.mv[:, par, 1:2], LN_EPS, None,
                                ALU.add).then_inc(self.eps_added, 1)
        pool.wait_ge(self.eps_added, t + 1)
        nc.gpsimd.tensor_tensor(self.rstd[:, par, 1:2], self.rstd[:, par, 0:1],
                                self.c.minus_half[:, 0:1], ALU.pow).then_inc(self.rstd_ready, 1)

    def normalise(self, dve, nc, t, par, free_sem, per_tile=1):
        dve.wait_ge(self.rstd_ready, t + 1)
        wait(dve, free_sem, (t - 1) * per_tile)
        nc.vector.tensor_scalar(self.xn[:, par, :], self.x[:, t, :], self.mv[:, par, 0:1],
                                self.rstd[:, par, 1:2], ALU.subtract, ALU.mult)\
            .then_inc(self.xn_ready, 1)


def cross_attention_0(nc, c, X, d, x_tiles_loaded):
    with ExitStack() as ctx:
        ph = Phase(nc, ctx, "xa")
        wq, wk, wv = (ph.sb(n, [P, KC, E]) for n in ("wq", "wk", "wv"))
        wo = ph.sb("wo", [P, 2, E])
        bq, bk = ph.sb("bq", [P, KC]), ph.sb("bk", [P, KC])
        bq4 = ph.sb("bq4", [P, KC])
        bv = ph.sb("bv", [P, 2])
        bo = ph.sb("bo", [P, E])
        attn_raw, attn = ph.sb("attn_raw", [P, S]), ph.sb("attn", [P, S])
        pad = ph.sb("pad", [P, B, S], U8)
        padT = ph.sb("padT", [P, NT, SC], U8)
        keep = ph.sb("keep", [P, NT, SC])
        ctxT = ph.sb("ctxT", [P, 2, KC, 2 * S])
        wk2, wv2 = ph.sb("wk2", [P, 2, KC, E], F32R), ph.sb("wv2", [P, 2, KC, E], F32R)
        ctx2 = ph.sb("ctx2", [P, 2, 2, KC, 2 * S], F32R)
        kT = ph.sb("kT", [P, 2, 2, KC, 2 * S], F32R)
        q2 = ph.sb("q2", [P, 2, 2, KC, P], F32R)
        qz = ph.sb("qz", [P, 2, 2, KC, 2, HG * T], F32R)
        xT = ph.sb("xT", [P, 2, KC, P])
        qT = ph.sb("qT", [P, 2, KC, P])
        v = ph.sb("v", [P, 2, SC, H, D1])
        mask = ph.sb("mask", [P, 2, S])
        neg_s = ph.sb("neg_s", [P, 2, 2, S])
        neg_max = ph.sb("neg_max", [P, 2, 2])
        prob = ph.sb("prob", [P, 2, 2, S])
        probT = ph.sb("probT", [P, 2, 2, 2, P])
        rz = ph.sb("rz", [P, 2, HG])
        y = ph.sb("y", [P, 2, HG, D])
        yT = ph.sb("yT", [P, 2, 2, P])
        o = ph.sb("o", [P, 2, E])
        ln = LayerNorm(ph, c, X)

        ps_s = [ph.ps(f"s{i}") for i in range(2)]
        ps_t = [ph.ps(f"t{i}") for i in range(2)]
        ps_o = [ph.ps(f"o{i}") for i in range(2)]
        ps_a, ps_b = ph.ps("a"), ph.ps("b")

        w_loaded = ph.sem("w_loaded")
        ctx_loaded = [ph.sem(f"ctx_loaded{i}") for i in range(2)]
        mask_loaded = ph.sem("mask_loaded")
        const_ready = ph.sem("const_ready")
        xT_done, xT_ready = ph.sem("xT_done"), ph.sem("xT_ready")
        q_done, q_ready, qz_ready = ph.sem("q_done"), ph.sem("q_ready"), ph.sem("qz_ready")
        ctx_high, ctx_low = ph.sem("ctx_high"), ph.sem("ctx_low")
        w_high, w_split = ph.sem("w_high"), ph.sem("w_split")
        k_high, q_scaled, q_high = ph.sem("k_high"), ph.sem("q_scaled"), ph.sem("q_high")
        k_done, k_ready = ph.sem("k_done"), ph.sem("k_ready")
        v_done, v_ready, ones_ready = ph.sem("v_done"), ph.sem("v_ready"), ph.sem("ones_ready")
        mask_ready = ph.sem("mask_ready")
        s_done, s_ready = ph.sem("s_done"), ph.sem("s_ready")
        exp_ready = ph.sem("exp_ready")
        t_done, t_ready = ph.sem("t_done"), ph.sem("t_ready")
        pv_done = ph.sem("pv_done")
        rz_ready, y_ready = ph.sem("rz_ready"), ph.sem("y_ready")
        yT_done, yT_ready = ph.sem("yT_done"), ph.sem("yT_ready")
        o_done, o_ready, x_updated = ph.sem("o_done"), ph.sem("o_ready"), ph.sem("x_updated")

        block = ph.block()

        @block.sync
        def _(sp):
            for dst, src in ((wq[:, :, :], d["xa_wqT"]), (wk[:, :, :], d["xa_wkT"]),
                             (wv[:, :, :], d["xa_wvT"]), (wo[:, :, :], d["xa_woP"]),
                             (bq[:, :], d["xa_bq"]), (bk[:, :], d["xa_bk"]), (bv[:, :], d["xa_bvP"]),
                             (bo[:, :], d["xa_bo"].to_broadcast([P, E]))):
                sp.dma_start(dst, src).then_inc(w_loaded, 16)
            sp.dma_start(padT[:, :, :], d["padT"]).then_inc(mask_loaded, 16)
            for h2 in range(2):
                sp.dma_start(attn_raw[h2 * T:(h2 + 1) * T, :], d["attn_mask"]).then_inc(mask_loaded, 16)
            sp.dma_start(pad[:, :, :], d["pad"].to_broadcast([P, B, S])).then_inc(mask_loaded, 16)

            def step(s, par):
                if live(s):
                    wait(sp, ctx_low, s - 1)
                    sp.dma_start(ctxT[:, par, :, :], d["ctxT"][s, :, :, :]).then_inc(ctx_loaded[par], 16)
            tile_steps(sp, step, lag=0)

        @block.gpsimd
        def _(pool):
            def step(s, par):
                p, pp = s - 1, 1 - par
                if live(p):
                    if isinstance(p, int) and p == 0:
                        pool.wait_ge(const_ready, 3)
                    wait(pool, pv_done, 8 * (p - 1))
                    nc.gpsimd.tensor_copy(v[:, pp, :, :, D:D1],
                                          keep[:, p, :].unsqueeze(2).unsqueeze(3).to_broadcast([P, SC, H, 1]))\
                        .then_inc(ones_ready, 1)
                    pool.wait_ge(q_ready, p + 1)
                    wait(pool, s_done, 8 * (p - 1))
                    for part in range(2):
                        for g in range(KC):
                            for b in range(2):
                                ins = nc.gpsimd.tensor_tensor(
                                    qz[:, pp, part, g, b, :].rearrange("p (h t) -> p h t", h=HG),
                                    q2[:, pp, part, g, b * T:(b + 1) * T].unsqueeze(1).to_broadcast([P, HG, T]),
                                    c.head_mask[:, :].unsqueeze(2).to_broadcast([P, HG, T]), ALU.mult)
                    ins.then_inc(qz_ready, 1)
                if live(s):
                    pool.wait_ge(ctx_high, s + 1)
                    wait(pool, v_done, 2 * (s - 1))
                    nc.gpsimd.tensor_tensor(ctx2[:, par, 1, :, :], ctxT[:, par, :, :], ctx2[:, par, 0, :, :],
                                            ALU.subtract).then_inc(ctx_low, 1)
                    ln.inverse_std(pool, nc, s, par)
                a = s - 3
                if live(a):
                    pool.wait_ge(o_ready, a + 1)
                    nc.gpsimd.tensor_tensor(X[:, a, :], X[:, a, :], o[:, 1 - par, :], ALU.add)\
                        .then_inc(x_updated, 1)
            tile_steps(pool, step, lag=3, peel=6)

        @block.vector
        def _(dve):
            dve.wait_ge(mask_loaded, 16 * 4)
            nc.vector.tensor_scalar(attn[:, :], attn_raw[:, :], MASKED, None, ALU.max).then_inc(const_ready, 1)
            nc.vector.tensor_scalar(keep[:, :, :], padT[:, :, :], -1.0, 1.0, ALU.mult, ALU.add)\
                .then_inc(const_ready, 1)
            dve.wait_ge(w_loaded, 16 * 8)
            nc.vector.tensor_scalar(bq4[:, :], bq[:, :], D ** -0.5, None, ALU.mult).then_inc(const_ready, 1)
            for w2, w in ((wk2, wk), (wv2, wv)):
                nc.vector.tensor_copy(w2[:, 0, :, :], w[:, :, :]).then_inc(w_high, 1)
            dve.wait_ge(w_high, 2)
            for w2, w in ((wk2, wk), (wv2, wv)):
                nc.vector.tensor_tensor(w2[:, 1, :, :], w[:, :, :], w2[:, 0, :, :], ALU.subtract).then_inc(w_split, 1)
            dve.wait_ge(const_ready, 3)

            def masked_scores(a, u):
                if u % 4 == 0:
                    b = u // 4
                    wait(dve, s_ready, 8 * a + u - 4)
                    nc.vector.scalar_tensor_tensor(mask[:, b, :], pad[:, 2 * a + b, :], MASKED, attn[:, :],
                                                   ALU.mult, ALU.add).then_inc(mask_ready, 1)
                    dve.wait_ge(mask_ready, 2 * a + b + 1)
                wait(dve, exp_ready, 8 * a + u - 1)
                wait_apart(dve, s_done, 8 * a + u + 1, c.passed_dve)
                for i in range(2):
                    ins = nc.vector.tensor_tensor_reduce(
                        neg_s[:, u % 2, i, :], ps_s[u % 2][:, i * S:(i + 1) * S], mask[:, u // 4, :],
                        -1.0, 3e38, ALU.add, ALU.min, neg_max[:, u % 2, i:i + 1])
                ins.then_inc(s_ready, 1)

            def normalised_heads(a, b):
                dve.wait_ge(pv_done, 8 * a + 4 * b + 4)
                wait(dve, yT_done, 2 * a + b - 1)
                for h2 in range(2):
                    rows = slice(h2 * T, (h2 + 1) * T)
                    heads = ps_o[b][rows, 0:H * D1].rearrange("p (q h d) -> p q h d", h=2, d=D1)
                    nc.vector.reciprocal(rz[rows, b, :], heads[:, :, h2, D]).then_inc(rz_ready, 1)
                dve.wait_ge(rz_ready, 4 * a + 2 * b + 2)
                for h2 in range(2):
                    rows = slice(h2 * T, (h2 + 1) * T)
                    heads = ps_o[b][rows, 0:H * D1].rearrange("p (q h d) -> p q h d", h=2, d=D1)
                    ins = nc.vector.tensor_tensor(
                        y[rows, b, :, :], heads[:, :, h2, 0:D],
                        rz[rows, b, :].unsqueeze(2).to_broadcast([T, HG, D]), ALU.mult)
                ins.then_inc(y_ready, 1)

            def heads_out(a, b, tp):
                dve.wait_ge(yT_done, 2 * a + b + 1)
                wait(dve, o_done, a - 1)
                for h2 in range(2):
                    ins = nc.vector.tensor_scalar(yT[:, tp, h2, b * T:(b + 1) * T],
                                                  ps_of_yT[b][:, h2 * T:(h2 + 1) * T], bv[:, h2:h2 + 1], None,
                                                  ALU.add)
                ins.then_inc(yT_ready, 1)
            ps_of_yT = (ps_a, ps_b)

            def step(s, par):
                p, a, e = s - 1, s - 2, s - 3
                for u in range(8):
                    if live(a):
                        masked_scores(a, u)
                    if u == 0 and live(p):
                        dve.wait_ge(xT_done, p + 1)
                        wait(dve, q_done, p - 1)
                        nc.vector.tensor_copy(xT[:, 1 - par, :, :], ps_a[:, 0:E].rearrange("p (k t) -> p k t", k=KC))\
                            .then_inc(xT_ready, 1)
                    if u in (1, 4) and live(p):
                        g = u // 4
                        dve.wait_ge(k_done, 2 * p + g + 1)
                        wait(dve, s_done, 8 * (p - 1))
                        nc.vector.tensor_scalar(kT[:, 1 - par, 0, g, :], (ps_b, ps_a)[g][:, :], bk[:, g:g + 1], None,
                                                ALU.add).then_inc(k_high, 1)
                        dve.wait_ge(k_high, 2 * p + g + 1)
                        nc.vector.scalar_tensor_tensor(kT[:, 1 - par, 1, g, :], (ps_b, ps_a)[g][:, :], bk[:, g:g + 1],
                                                       kT[:, 1 - par, 0, g, :], ALU.add, ALU.subtract)\
                            .then_inc(k_ready, 1)
                    if u == 2 and live(p):
                        dve.wait_ge(q_done, p + 1)
                        wait(dve, qz_ready, p - 1)
                        for g in range(KC):
                            ins = nc.vector.tensor_scalar(qT[:, 1 - par, g, :], ps_a[:, g * P:(g + 1) * P],
                                                          D ** -0.5, bq4[:, g:g + 1], ALU.mult, ALU.add)
                        ins.then_inc(q_scaled, 1)
                        dve.wait_ge(q_scaled, p + 1)
                        nc.vector.tensor_copy(q2[:, 1 - par, 0, :, :], qT[:, 1 - par, :, :]).then_inc(q_high, 1)
                        dve.wait_ge(q_high, p + 1)
                        nc.vector.tensor_tensor(q2[:, 1 - par, 1, :, :], qT[:, 1 - par, :, :], q2[:, 1 - par, 0, :, :],
                                                ALU.subtract).then_inc(q_ready, 1)
                    if u == 2 and live(e):
                        normalised_heads(e, 1)
                    if u == 3 and live(e):
                        heads_out(e, 1, 1 - par)
                    if u == 5 and live(e):
                        dve.wait_ge(o_done, e + 1)
                        wait(dve, x_updated, e - 1)
                        nc.vector.tensor_tensor(o[:, 1 - par, :], ps_b[:, 0:E], bo[:, :], ALU.add)\
                            .then_inc(o_ready, 1)
                    if u == 5 and live(s):
                        if isinstance(s, int):
                            dve.wait_ge(x_tiles_loaded[s // (NT // 4)], 16)
                        elif par == 0:
                            for sem in x_tiles_loaded:
                                dve.wait_ge(sem, 16)
                        ln.statistics(dve, nc, s, par)
                    if u == 6 and live(p):
                        for half in range(2):
                            dve.wait_ge(v_done, 2 * p + half + 1)
                            wait(dve, pv_done, 8 * (p - 1))
                            for i in range(2):
                                ch = 2 * half + i
                                ins = nc.vector.tensor_scalar(
                                    v[:, 1 - par, ch, :, 0:D],
                                    (ps_a, ps_b)[half][:, i * E:(i + 1) * E].rearrange("p (h d) -> p h d", h=H),
                                    keep[:, p, ch:ch + 1], None, ALU.mult)
                            ins.then_inc(v_ready, 1)
                    if u == 6 and live(a):
                        normalised_heads(a, 0)
                    if u == 7 and live(s):
                        ln.normalise(dve, nc, s, par, xT_done)
                    if u == 7 and live(a):
                        heads_out(a, 0, par)
            tile_steps(dve, step, lag=3, peel=6)

        @block.scalar
        def _(act):
            def probabilities(a, u):
                act.wait_ge(s_ready, 8 * a + u + 1)
                wait(act, t_done, 8 * a + u - 1)
                for i in range(2):
                    ins = nc.scalar.activation(prob[:, u % 2, i, :], neg_s[:, u % 2, i, :], ACT.Exp,
                                               bias=neg_max[:, u % 2, i:i + 1], scale=-1.0)
                ins.then_inc(exp_ready, 1)

            def transposed(a, u):
                act.wait_ge(t_done, 8 * a + u + 1)
                wait(act, pv_done, 8 * a + u - 1)
                nc.scalar.activation(probT[:, u % 2, :, :, :].rearrange("p i c t -> p (i c t)"),
                                     ps_t[u % 2][:, :], ACT.Copy).then_inc(t_ready, 1)

            def step(s, par):
                a, e = s - 2, s - 3
                for u in range(8):
                    if u == 1 and live(s):
                        if isinstance(s, int):
                            act.wait_ge(ctx_loaded[par], 16 * (s // 2 + 1))
                        else:
                            act.wait_ge(ctx_loaded[par], s * 8 + (16 if par == 0 else 8))
                        wait(act, v_done, 2 * (s - 1))
                        nc.scalar.activation(ctx2[:, par, 0, :, :], ctxT[:, par, :, :], ACT.Copy).then_inc(ctx_high, 1)
                    if live(a):
                        probabilities(a, u)
                    if u >= 1 and live(a):
                        transposed(a, u - 1)
                    if u == 0 and live(e):
                        transposed(e, 7)
            tile_steps(act, step, lag=3, peel=6)

        @block.tensor
        def _(pe):
            def scores(a, u, ap):
                b, g, jj = u // 4, u // 2 % 2, u % 2
                if u == 0:
                    pe.wait_ge(k_ready, 2 * a + 2)
                    pe.wait_ge(qz_ready, a + 1)
                wait(pe, s_ready, 8 * a + u - 1)
                for i in range(2):
                    j = 2 * jj + i
                    for n, (x, z) in enumerate(THREE_PASSES):
                        mm = nc.tensor.matmul(ps_s[u % 2][:, i * S:(i + 1) * S],
                                              qz[:, ap, x, g, b, j * P:(j + 1) * P],
                                              kT[:, ap, z, g, b * S:(b + 1) * S], start=(n == 0), stop=(n == 2))
                mm.then_inc(s_done, 1)

            def transposes(a, u):
                pe.wait_ge(exp_ready, 8 * a + u + 1)
                wait(pe, t_ready, 8 * a + u - 1)
                for i in range(2):
                    for ch in range(2):
                        k = (2 * i + ch) * P
                        mm = nc.tensor.transpose(ps_t[u % 2][:, k:k + P], prob[:, u % 2, i, ch * P:(ch + 1) * P],
                                                 c.ident[:, :])
                mm.then_inc(t_done, 1)

            def attended(a, u, ap):
                b, g, jj = u // 4, u // 2 % 2, u % 2
                pe.wait_ge(t_ready, 8 * a + u + 1)
                if u == 0:
                    pe.wait_ge(v_ready, 2 * a + 2)
                    pe.wait_ge(ones_ready, a + 1)
                if u % 4 == 0:
                    wait(pe, y_ready, 2 * a + b - 1)
                for i in range(2):
                    q = 4 * g + 2 * jj + i
                    for ch in range(2):
                        mm = nc.tensor.matmul(ps_o[b][:, q * 2 * D1:(q + 1) * 2 * D1], probT[:, u % 2, i, ch, :],
                                              v[:, ap, 2 * b + ch, 2 * q:2 * q + 2, :],
                                              start=(ch == 0), stop=(ch == 1))
                mm.then_inc(pv_done, 1)

            def heads_transposed(a, b):
                pe.wait_ge(y_ready, 2 * a + b + 1)
                nc.tensor.transpose((ps_a, ps_b)[b][:, 0:P], y[:, b, :, :].rearrange("p q d -> p (q d)"),
                                    c.ident[:, :]).then_inc(yT_done, 1)

            pe.wait_ge(w_loaded, 16 * 8)
            pe.wait_ge(w_split, 2)
            pe.wait_ge(c.loaded, 16 * c.n_loads)

            def step(s, par):
                p, a, e = s - 1, s - 2, s - 3
                pp, ap, ep = 1 - par, par, 1 - par
                for u in range(8):
                    if live(a):
                        scores(a, u, ap)
                    if u == 0 and live(p):
                        pe.wait_ge(ln.xn_ready, p + 1)
                        wait(pe, v_ready, 2 * p - 1)
                        wait(pe, yT_ready, 2 * p - 3)
                        for k in range(KC):
                            mm = nc.tensor.transpose(ps_a[:, k * P:(k + 1) * P], ln.xn[:, pp, k * P:(k + 1) * P],
                                                     c.ident[:, :])
                        mm.then_inc(xT_done, 1)
                    if u in (1, 4) and live(p):
                        g = u // 4
                        if g == 0:
                            pe.wait_ge(ctx_high, p + 1)
                            pe.wait_ge(ctx_low, p + 1)
                            wait(pe, v_ready, 2 * p)
                        else:
                            pe.wait_ge(q_ready, p + 1)
                        for n, (k, (x, z)) in enumerate((k, xz) for k in range(KC) for xz in THREE_PASSES):
                            mm = nc.tensor.matmul((ps_b, ps_a)[g][:, :], wk2[:, x, k, g * P:(g + 1) * P],
                                                  ctx2[:, pp, z, k, :], start=(n == 0), stop=(n == 3 * KC - 1))
                        mm.then_inc(k_done, 1)
                    if u == 2 and live(p):
                        pe.wait_ge(xT_ready, p + 1)
                        for g in range(KC):
                            for k in range(KC):
                                mm = nc.tensor.matmul(ps_a[:, g * P:(g + 1) * P], wq[:, k, g * P:(g + 1) * P],
                                                      xT[:, pp, k, :], start=(k == 0), stop=(k == KC - 1))
                        mm.then_inc(q_done, 1)
                    if u == 3 and live(e):
                        if live(p):
                            pe.wait_ge(k_ready, 2 * p + 1)
                        else:
                            pe.wait_ge(v_ready, 2 * NT)
                            pe.wait_ge(o_ready, e)
                        heads_transposed(e, 1)
                    if u == 5 and live(e):
                        pe.wait_ge(yT_ready, 2 * e + 2)
                        for h2 in range(2):
                            mm = nc.tensor.matmul(ps_b[:, 0:E], yT[:, ep, h2, :], wo[:, h2, :],
                                                  start=(h2 == 0), stop=(h2 == 1))
                        mm.then_inc(o_done, 1)
                    if u == 6 and live(p):
                        for half in range(2):
                            if half == 0:
                                pe.wait_ge(k_ready, 2 * p + 2)
                            elif live(e):
                                pe.wait_ge(o_ready, e + 1)
                            for i in range(2):
                                ch = 2 * half + i
                                for n, (k, (x, z)) in enumerate((k, xz) for k in range(KC) for xz in THREE_PASSES):
                                    mm = nc.tensor.matmul((ps_a, ps_b)[half][:, i * E:(i + 1) * E],
                                                          ctx2[:, pp, x, k, ch * P:(ch + 1) * P], wv2[:, z, k, :],
                                                          start=(n == 0), stop=(n == 3 * KC - 1))
                            mm.then_inc(v_done, 1)
                    if u == 7 and live(a):
                        if live(p):
                            pe.wait_ge(v_ready, 2 * p + 1)
                        else:
                            pe.wait_ge(yT_ready, 2 * a - 1)
                        heads_transposed(a, 0)
                    if u >= 2 and live(a):
                        attended(a, u - 2, ap)
                    if u < 2 and live(e):
                        attended(e, u + 6, ep)
                    if u >= 1 and live(a):
                        transposes(a, u - 1)
                    if u == 0 and live(e):
                        transposes(e, 7)
            tile_steps(pe, step, lag=3, peel=6)


def causal_attention(nc, c, X, d, layer):
    soft = layer == 1
    with ExitStack() as ctx:
        ph = Phase(nc, ctx, f"sa{layer}")
        wqkv = ph.sb("wqkv", [P, KC, 3 * E])
        wo = ph.sb("wo", [P, KC, E])
        mask = ph.sb("mask", [P, P])
        xT = ph.sb("xT", [P, 2, KC, P])
        parts, dt, passes = (1, F32, ((0, 0),)) if soft else (2, F32R, THREE_PASSES)
        plain = ph.sb("plain", [P, 2, parts, KC, P], dt)
        other = ph.sb("other", [P, 2, parts, KC, P], dt)
        apart = ph.sb("apart", [P, 2, parts, KC, HG, P], dt)
        v = ph.sb("v", [P, 2, H, D1])
        w = ph.sb("w", [P, 2, 4, P])
        z, rz = ph.sb("z", [P, 2, H]), ph.sb("rz", [P, 2, H])
        y = ph.sb("y", [P, 2, H, D])
        yT = ph.sb("yT", [P, 2, KC, P])
        if soft:
            neg_s = ph.sb("neg_s", [P, 2, 4, P])
            neg_max = ph.sb("neg_max", [P, 2, 4])
            prob = ph.sb("prob", [P, 2, 4, P])
            bo = ph.sb("bo", [P, E])
            o = ph.sb("o", [P, 2, E])
        else:
            square = ph.sb("square", [P, 2, 4, P])
            q_full, k_full = ph.sb("q_full", [P, 2, KC, P]), ph.sb("k_full", [P, 2, KC, P])
            zero, zero_set = ph.sb("zero", [P, E]), ph.sem("zero_set")
        ln = LayerNorm(ph, c, X)

        ps_s = [ph.ps(f"s{i}") for i in range(2)]
        ps_t = [ph.ps(f"t{i}") for i in range(2)] if soft else None
        ps_o = [ph.ps(f"o{i}") for i in range(2)]
        ps_a, ps_b = ph.ps("a"), ph.ps("b")

        loaded, n_loads = ph.sem("loaded"), 4 if soft else 3
        ones_ready = ph.sem("ones_ready")
        xT_done, xT_ready = ph.sem("xT_done"), ph.sem("xT_ready")
        qk_copied, qk_high = ph.sem("qk_copied"), ph.sem("qk_high")
        qk_done, qk_ready, apart_ready = ph.sem("qk_done"), ph.sem("qk_ready"), ph.sem("apart_ready")
        v_done, v_ready = ph.sem("v_done"), ph.sem("v_ready")
        s_done = ph.sem("s_done")
        s_ready = ph.sem("s_ready")
        exp_ready, t_done = ph.sem("exp_ready"), ph.sem("t_done")
        w_ready = ph.sem("w_ready")
        pv_done = ph.sem("pv_done")
        z_ready, rz_ready, y_ready = ph.sem("z_ready"), ph.sem("rz_ready"), ph.sem("y_ready")
        yT_done, yT_ready = ph.sem("yT_done"), ph.sem("yT_ready")
        o_done, o_ready, x_updated = ph.sem("o_done"), ph.sem("o_ready"), ph.sem("x_updated")

        def unit(s, u, back):
            return (s - 3 if u >= back else s - 4), (u - back) % 4

        block = ph.block()

        @block.sync
        def _(sp):
            sp.dma_start(wqkv[:, :, :], d[f"sa{layer}_wqkvT"]).then_inc(loaded, 16)
            sp.dma_start(wo[:, :, :], d[f"sa{layer}_woT"]).then_inc(loaded, 16)
            sp.dma_start(mask[:, :], d[f"sa{layer}_mask"]).then_inc(loaded, 16)
            if soft:
                sp.dma_start(bo[:, :], d["sa1_bo"].to_broadcast([P, E])).then_inc(loaded, 16)
            else:
                sp.wait_ge(zero_set, 1)
                lists = c.xg_dram.rearrange("(n r p) e -> n p r e", p=P, r=ZERO_TILES)
                for n in range(NS // ZERO_TILES):
                    sp.dma_start(lists[n, :, :, :], zero[:, :].unsqueeze(1).to_broadcast([P, ZERO_TILES, E]))\
                        .then_inc(c.zeroed, 16)

        @block.gpsimd
        def _(pool):
            nc.gpsimd.memset(v[:, :, :, D:D1], 1.0).then_inc(ones_ready, 1)
            if not soft:
                nc.gpsimd.memset(zero[:, :], 0.0).then_inc(zero_set, 1)

            def step(s, par):
                q, done = s - 2, s - 6
                if live(s):
                    ln.inverse_std(pool, nc, s, par)
                if live(q):
                    pool.wait_ge(qk_ready, q + 1)
                    wait(pool, s_done, 4 * (q - 1))
                    for part in range(parts):
                        for k in range(KC):
                            ins = nc.gpsimd.tensor_tensor(
                                apart[:, par, part, k, :, :],
                                other[:, par, part, k, :].unsqueeze(1).to_broadcast([P, HG, P]),
                                c.head_mask[:, :].unsqueeze(2).to_broadcast([P, HG, P]), ALU.mult)
                    ins.then_inc(apart_ready, 1)
                if soft and live(done):
                    pool.wait_ge(o_ready, done + 1)
                    nc.gpsimd.tensor_tensor(X[:, done, :], X[:, done, :], o[:, par, :], ALU.add)\
                        .then_inc(x_updated, 1)
            tile_steps(pool, step, lag=6, peel=8)

        @block.vector
        def _(dve):
            dve.wait_ge(loaded, 16 * n_loads)

            def masked(a, u):
                b = u % 2
                if soft:
                    wait(dve, exp_ready, 4 * a + u - 1)
                    wait_apart(dve, s_done, 4 * a + u + 1, c.passed_dve)
                    for i in range(4):
                        ins = nc.vector.tensor_tensor_reduce(
                            neg_s[:, b, i, :], ps_s[b][:, i * P:(i + 1) * P], mask[:, :],
                            -1.0, 3e38, ALU.add, ALU.min, neg_max[:, b, i:i + 1])
                    ins.then_inc(s_ready, 1)
                else:
                    dve.wait_ge(s_ready, 4 * a + u + 1)
                    wait(dve, pv_done, 4 * a + u - 1)
                    nc.vector.scalar_tensor_tensor(w[:, b, :, :], square[:, b, :, :], 1.0,
                                                   mask[:, :].unsqueeze(1).to_broadcast([P, 4, P]),
                                                   ALU.add, ALU.mult).then_inc(w_ready, 1)

            def step(s, par):
                p, q, a, e, f, done = (s - lag for lag in range(1, 7))
                for u in range(4):
                    if soft and live(a):
                        masked(a, u)
                    if u == 0 and live(s):
                        ln.statistics(dve, nc, s, par)
                    if u == 0 and live(q):
                        q_out, k_out = (plain, other) if soft else (other, plain)
                        dve.wait_ge(qk_done, q + 1)
                        wait(dve, s_done, 4 * (q - 1))
                        wait(dve, apart_ready, q - 1)
                        q_all, k_all = (q_out[:, par, 0, :, :], k_out[:, par, 0, :, :]) if soft else \
                            (q_full[:, par, :, :], k_full[:, par, :, :])
                        nc.vector.tensor_scalar(q_all, ps_a[:, 0:E].rearrange("p (k t) -> p k t", k=KC),
                                                D ** -0.5, None, ALU.mult)
                        nc.vector.tensor_copy(k_all, ps_a[:, E:2 * E].rearrange("p (k t) -> p k t", k=KC))\
                            .then_inc(qk_ready if soft else qk_copied, 1)
                        if not soft:
                            dve.wait_ge(qk_copied, q + 1)
                            nc.vector.tensor_copy(q_out[:, par, 0, :, :], q_all)
                            nc.vector.tensor_copy(k_out[:, par, 0, :, :], k_all).then_inc(qk_high, 1)
                            dve.wait_ge(qk_high, q + 1)
                            nc.vector.tensor_tensor(q_out[:, par, 1, :, :], q_all, q_out[:, par, 0, :, :], ALU.subtract)
                            nc.vector.tensor_tensor(k_out[:, par, 1, :, :], k_all, k_out[:, par, 0, :, :], ALU.subtract)\
                                .then_inc(qk_ready, 1)
                    if u == 0 and live(f):
                        dve.wait_ge(yT_done, f + 1)
                        wait(dve, o_done, f - 1)
                        nc.vector.tensor_copy(yT[:, 1 - par, :, :], ps_b[:, 0:E].rearrange("p (k t) -> p k t", k=KC))\
                            .then_inc(yT_ready, 1)
                    if u == 0 and live(done):
                        dve.wait_ge(o_done, done + 1)
                        if soft:
                            wait(dve, x_updated, done - 1)
                            nc.vector.tensor_tensor(o[:, par, :], ps_b[:, E:2 * E], bo[:, :], ALU.add)\
                                .then_inc(o_ready, 1)
                        else:
                            nc.vector.tensor_tensor(X[:, done, :], X[:, done, :], ps_b[:, E:2 * E], ALU.add)\
                                .then_inc(o_ready, 1)
                    if u == 2 and live(p):
                        dve.wait_ge(xT_done, p + 1)
                        wait(dve, v_done, p - 1)
                        nc.vector.tensor_copy(xT[:, 1 - par, :, :], ps_a[:, E:2 * E].rearrange("p (k t) -> p k t", k=KC))\
                            .then_inc(xT_ready, 1)
                    if u == 2 and live(q):
                        dve.wait_ge(v_done, q + 1)
                        wait(dve, pv_done, 4 * (q - 1))
                        nc.vector.tensor_copy(v[:, par, :, 0:D],
                                              ps_a[:, 0:E].rearrange("p (h d) -> p h d", h=H)).then_inc(v_ready, 1)
                    if u == 2 and live(e):
                        dve.wait_ge(pv_done, 4 * e + 4)
                        heads = ps_o[par][:, 0:H * D1].rearrange("p (h d) -> p h d", d=D1)
                        sums = heads[:, :, D]
                        if not soft:
                            nc.vector.tensor_scalar(z[:, par, :], sums, 1e-6, None, ALU.add).then_inc(z_ready, 1)
                            dve.wait_ge(z_ready, e + 1)
                            sums = z[:, par, :]
                        nc.vector.reciprocal(rz[:, par, :], sums).then_inc(rz_ready, 1)
                        wait(dve, yT_done, e - 1)
                        dve.wait_ge(rz_ready, e + 1)
                        nc.vector.tensor_tensor(y[:, par, :, :], heads[:, :, 0:D],
                                                rz[:, par, :].unsqueeze(2).to_broadcast([P, H, D]),
                                                ALU.mult).then_inc(y_ready, 1)
                    if u == 3 and live(s):
                        ln.normalise(dve, nc, s, par, xT_done)
                    if not soft and live(a):
                        masked(a, u)
            tile_steps(dve, step, lag=6, peel=8)

        @block.scalar
        def _(act):
            def step(s, par):
                a, e = s - 3, s - 4
                for u in range(4):
                    b = u % 2
                    if live(a) and not soft:
                        act.wait_ge(s_done, 4 * a + u + 1)
                        wait(act, w_ready, 4 * a + u - 1)
                        nc.scalar.activation(square[:, b, :, :].rearrange("p h t -> p (h t)"), ps_s[b][:, :],
                                             ACT.Square, bias=1.0).then_inc(s_ready, 1)
                    t, ut = unit(s, u, 2)
                    if soft and live(t):
                        act.wait_ge(t_done, 4 * t + ut + 1)
                        wait(act, pv_done, 4 * t + ut - 1)
                        nc.scalar.activation(w[:, ut % 2, :, :].rearrange("p h t -> p (h t)"), ps_t[ut % 2][:, :],
                                             ACT.Copy).then_inc(w_ready, 1)
                    if live(a) and soft:
                        act.wait_ge(s_ready, 4 * a + u + 1)
                        wait(act, t_done, 4 * a + u - 1)
                        for i in range(4):
                            ins = nc.scalar.activation(prob[:, b, i, :], neg_s[:, b, i, :], ACT.Exp,
                                                       bias=neg_max[:, b, i:i + 1], scale=-1.0)
                        ins.then_inc(exp_ready, 1)
            tile_steps(act, step, lag=4, peel=8)

        @block.tensor
        def _(pe):
            def scores(a, u, ap):
                g, half, b = u // 2, u % 2, u % 2
                if u == 0:
                    pe.wait_ge(apart_ready, a + 1)
                    pe.wait_ge(qk_ready, a + 1)
                wait(pe, s_ready, 4 * a + u - 1)
                for n, (x, z) in enumerate(passes):
                    mm = nc.tensor.matmul(ps_s[b][:, :], plain[:, ap, x, g, :],
                                          apart[:, ap, z, g, 4 * half:4 * half + 4, :].rearrange("p h t -> p (h t)"),
                                          start=(n == 0), stop=(n == len(passes) - 1))
                mm.then_inc(s_done, 1)

            def transposes(a, u):
                pe.wait_ge(exp_ready, 4 * a + u + 1)
                wait(pe, w_ready, 4 * a + u - 1)
                for i in range(4):
                    mm = nc.tensor.transpose(ps_t[u % 2][:, i * P:(i + 1) * P], prob[:, u % 2, i, :], c.ident[:, :])
                mm.then_inc(t_done, 1)

            def attended(a, u, ap):
                pe.wait_ge(w_ready, 4 * a + u + 1)
                if u == 0:
                    pe.wait_ge(v_ready, a + 1)
                    wait(pe, y_ready, a - 1)
                for i in range(4):
                    h = 4 * u + i
                    mm = nc.tensor.matmul(ps_o[ap][:, h * D1:(h + 1) * D1], w[:, u % 2, i, :], v[:, ap, h, :],
                                          start=True, stop=True)
                mm.then_inc(pv_done, 1)

            pe.wait_ge(loaded, 16 * n_loads)
            pe.wait_ge(ones_ready, 1)

            def step(s, par):
                p, q, a, e, f, done = (s - lag for lag in range(1, 7))
                for u in range(4):
                    if live(a):
                        scores(a, u, 1 - par)
                    t, ut = unit(s, u, 2)
                    if soft and live(t):
                        transposes(t, ut)
                    t, ut = unit(s, u, 3 if soft else 2)
                    if live(t):
                        attended(t, ut, 1 - par if u >= (3 if soft else 2) else par)
                    if u == 1 and live(q):
                        pe.wait_ge(qk_ready if soft else qk_copied, q + 1)
                        for k in range(KC):
                            mm = nc.tensor.matmul(ps_a[:, 0:E], xT[:, par, k, :], wqkv[:, k, 2 * E:3 * E],
                                                  start=(k == 0), stop=(k == KC - 1))
                        mm.then_inc(v_done, 1)
                    if u == 1 and live(p):
                        pe.wait_ge(ln.xn_ready, p + 1)
                        for k in range(KC):
                            mm = nc.tensor.transpose(ps_a[:, E + k * P:E + (k + 1) * P],
                                                     ln.xn[:, 1 - par, k * P:(k + 1) * P], c.ident[:, :])
                        mm.then_inc(xT_done, 1)
                    if u == 3 and live(p):
                        if live(q):
                            pe.wait_ge(v_ready, q + 1)
                        pe.wait_ge(xT_ready, p + 1)
                        for g in range(2 * KC):
                            for k in range(KC):
                                mm = nc.tensor.matmul(ps_a[:, g * P:(g + 1) * P], wqkv[:, k, g * P:(g + 1) * P],
                                                      xT[:, 1 - par, k, :], start=(k == 0), stop=(k == KC - 1))
                        mm.then_inc(qk_done, 1)
                    if u == 3 and live(f):
                        pe.wait_ge(yT_ready, f + 1)
                        if live(done):
                            pe.wait_ge(o_ready, done + 1)
                        for k in range(KC):
                            mm = nc.tensor.matmul(ps_b[:, E:2 * E], yT[:, 1 - par, k, :], wo[:, k, :],
                                                  start=(k == 0), stop=(k == KC - 1))
                        mm.then_inc(o_done, 1)
                    if u == 3 and live(e):
                        pe.wait_ge(y_ready, e + 1)
                        for k in range(KC):
                            mm = nc.tensor.transpose(ps_b[:, k * P:(k + 1) * P],
                                                     y[:, par, :, :].rearrange("p h d -> p (h d)")[:, k * P:(k + 1) * P],
                                                     c.ident[:, :])
                        mm.then_inc(yT_done, 1)
            tile_steps(pe, step, lag=6, peel=8)


class Chain:

    def __init__(self, eng, sem):
        self.eng, self.sem, self.n = eng, sem, 0

    def add(self, ins):
        ins.then_inc(self.sem, 1)
        self.n += 1

    def done(self):
        self.eng.wait_ge(self.sem, self.n)

    def then(self, ins):
        self.add(ins)
        self.done()


def route(nc, c, X, d):
    with ExitStack() as ctx:
        ph = Phase(nc, ctx, "rt")
        rw = ph.sb("rw", [P, KC, NE])
        bias = ph.sb("bias", [P, NE])
        before = ph.sb("before", [P, NG * NG])
        upper = ph.sb("upper", [P, P])
        ones = ph.sb("ones", [P, P])
        count16 = ph.sb("count16", [P, NE])
        count_tiles = ph.sb("count_tiles", [1, NS])
        carry = ph.sb("carry", [P, NE, NT])
        xT = ph.sb("xT", [P, 2, KC, P])
        ln = LayerNorm(ph, c, X)
        arrays = {}

        def arr(name, shape, dt=F32):
            arrays[name] = ph.sb(name, [P, *shape], dt)
            return arrays[name]

        e1, score, sc_b = arr("e1", [NT, NE]), arr("score", [NT, NE]), arr("sc_b", [NT, NE])
        pairs, gs = arr("pairs", [NT * NG, 6]), arr("gs", [NT * NG])
        gt, ge = arr("gt", [NT, NG, NG]), arr("ge", [NT, NG, NG])
        grank, gm, gm1 = arr("grank", [NT * NG]), arr("gm", [NT * NG]), arr("gm1", [NT * NG])
        cand = arr("cand", [NT, NE])
        best, best_i, best_f = arr("best", [NT, 8]), arr("best_i", [NT, 8], mybir.dt.uint32), arr("best_f", [NT, 8])
        hot = arr("hot", [TOP, NT, NE])
        chosen = arr("chosen", [NT, NE])
        picked = arr("picked", [TOP, NT, NE])
        wk, wsum = arr("wk", [NT, TOP]), arr("wsum", [NT])
        incl, excl = arr("incl", [NE, NT]), arr("excl", [NE, NT])
        tiles, ends, starts = arr("tiles", [NE]), arr("ends", [NE]), arr("starts", [NE])
        slot_all = arr("slot_all", [NE, NT])
        slot_f = arr("slot_f", [NT, TOP])
        owned = ph.sb("owned", [1, NS, NE])
        owner_f = ph.sb("owner_f", [1, NS])

        ps_x = [ph.ps(f"x{i}") for i in range(2)]
        ps_l, ps_rank, ps_total = ph.ps("l"), ph.ps("rank"), ph.ps("total")

        loaded, n_loads = ph.sem("loaded"), 8
        xT_done, xT_ready, l_done = ph.sem("xT_done"), ph.sem("xT_ready"), ph.sem("l_done")
        stored = [ph.sem(f"stored{i}") for i in range(2)]
        exp_ready, steps, chosen_ready, counted = (ph.sem(n) for n in ("exp_ready", "steps", "chosen_ready", "counted"))

        block = ph.block()

        @block.sync
        def _(sp):
            for dst, src in ((rw[:, :, :], "rt_w"), (before[:, :], "rt_before"), (upper[:, :], "rt_upper"),
                             (ones[:, :], "rt_ones"), (count16[:, :], "rt_count16"),
                             (count_tiles[:, :], "rt_count_tiles"), (carry[:, :, :], "rt_carry")):
                sp.dma_start(dst, d[src]).then_inc(loaded, 16)
            sp.dma_start(bias[:, :], d["rt_bias"].to_broadcast([P, NE])).then_inc(loaded, 16)

            def step(s, par):
                if live(s):
                    sp.wait_ge(ln.xn_ready, s + 1)
                    sp.dma_start(c.xn_dram[s, :, :], ln.xn[:, par, :]).then_inc(stored[par], 16)
            tile_steps(sp, step, lag=0)
            for par in range(2):
                sp.wait_ge(stored[par], 16 * (NT // 2))

        @block.gpsimd
        def _(pool):
            def step(s, par):
                if live(s):
                    ln.inverse_std(pool, nc, s, par)
            tile_steps(pool, step, lag=0)

        @block.scalar
        def _(act):
            act.wait_ge(l_done, NT)
            nc.scalar.activation(e1[:, :, :].rearrange("p t e -> p (t e)"), ps_l[:, :], ACT.Exp, scale=-1.0)\
                .then_inc(exp_ready, 1)

        @block.tensor
        def _(pe):
            pe.wait_ge(loaded, 16 * n_loads)

            def step(s, par):
                p = s - 1
                if live(s):
                    pe.wait_ge(ln.xn_ready, s + 1)
                    wait(pe, xT_ready, s - 1)
                    for k in range(KC):
                        mm = nc.tensor.transpose(ps_x[par][:, k * P:(k + 1) * P], ln.xn[:, par, k * P:(k + 1) * P],
                                                 c.ident[:, :])
                    mm.then_inc(xT_done, 1)
                if live(p):
                    pe.wait_ge(xT_ready, p + 1)
                    logits = ps_l[:, :].rearrange("p (t e) -> p t e", e=NE)
                    for k in range(KC):
                        mm = nc.tensor.matmul(logits[:, p, :], xT[:, 1 - par, k, :], rw[:, k, :],
                                              start=(k == 0), stop=(k == KC - 1))
                    mm.then_inc(l_done, 1)
            tile_steps(pe, step, lag=1)
            pe.wait_ge(chosen_ready, 1)
            by_expert = chosen[:, :, :].rearrange("p t e -> p e t")
            nc.tensor.matmul(ps_rank[:, :], upper[:, :], by_expert, start=True, stop=True)
            nc.tensor.matmul(ps_total[:, :], ones[:, :], by_expert, start=True, stop=True).then_inc(counted, 1)

        @block.vector
        def _(dve):
            V = nc.vector

            def step(s, par):
                p = s - 1
                if live(s):
                    wait(dve, stored[par], (s - par) * 8)
                    ln.statistics(dve, nc, s, par)
                if live(p):
                    dve.wait_ge(xT_done, p + 1)
                    wait(dve, l_done, p - 1)
                    V.tensor_copy(xT[:, 1 - par, :, :], ps_x[1 - par][:, 0:E].rearrange("p (k t) -> p k t", k=KC))\
                        .then_inc(xT_ready, 1)
                if live(s):
                    ln.normalise(dve, nc, s, par, xT_done)
            tile_steps(dve, step, lag=1)

            ch = Chain(dve, steps)
            dve.wait_ge(loaded, 16 * n_loads)
            dve.wait_ge(exp_ready, 1)
            ch.then(V.tensor_scalar(e1[:, :, :], e1[:, :, :], 1.0, None, ALU.add))
            ch.then(V.reciprocal(score[:, :, :], e1[:, :, :]))
            ch.then(V.tensor_tensor(sc_b[:, :, :], score[:, :, :],
                                    bias[:, :].unsqueeze(1).to_broadcast([P, NT, NE]), ALU.add))
            of_group = sc_b[:, :, :].rearrange("p t (g m) -> p (t g) m", g=NG)
            for n, (i, j) in enumerate(((0, 1), (0, 2), (0, 3), (1, 2), (1, 3), (2, 3))):
                ch.add(V.tensor_tensor(pairs[:, :, n], of_group[:, :, i], of_group[:, :, j], ALU.add))
            ch.done()
            ch.then(V.tensor_reduce(gs[:, :], pairs[:, :, :], AX.X, ALU.max))
            theirs = gs[:, :].rearrange("p (t g) -> p t g", g=NG).unsqueeze(2).to_broadcast([P, NT, NG, NG])
            own = gs[:, :].rearrange("p (t g) -> p t g", g=NG).unsqueeze(3).to_broadcast([P, NT, NG, NG])
            ch.add(V.tensor_tensor(gt[:, :, :, :], theirs, own, ALU.is_gt))
            ch.then(V.tensor_tensor(ge[:, :, :, :], theirs, own, ALU.is_ge))
            flat = lambda a: a[:, :, :, :].rearrange("p t g h -> p t (g h)")
            ch.then(V.tensor_tensor(flat(ge), flat(ge), before[:, :].unsqueeze(1).to_broadcast([P, NT, NG * NG]),
                                    ALU.mult))
            ch.then(V.tensor_tensor(flat(gt), flat(gt), flat(ge), ALU.max))
            ch.then(V.tensor_reduce(grank[:, :], gt[:, :, :, :].rearrange("p t g h -> p (t g) h"), AX.X, ALU.add))
            ch.then(V.tensor_scalar(gm[:, :], grank[:, :], float(TOP_GROUPS), None, ALU.is_lt))
            ch.add(V.tensor_scalar(gm1[:, :], gm[:, :], -1.0, None, ALU.add))
            per_group = lambda a: a[:, :].unsqueeze(2).to_broadcast([P, NT * NG, NE // NG])
            of_cand = cand[:, :, :].rearrange("p t (g m) -> p (t g) m", g=NG)
            ch.then(V.tensor_tensor(of_cand, of_group, per_group(gm), ALU.mult))
            ch.then(V.tensor_tensor(of_cand, of_cand, per_group(gm1), ALU.add))
            for t in range(NT):
                ch.add(V.max(best[:, t, :], cand[:, t, :]))
            ch.done()
            for t in range(NT):
                ch.add(V.max_index(best_i[:, t, :], best[:, t, :], cand[:, t, :]))
            ch.done()
            ch.then(V.tensor_copy(best_f[:, :, :], best_i[:, :, :]))
            for k in range(TOP):
                ch.add(V.tensor_tensor(hot[:, k, :, :], count16[:, :].unsqueeze(1).to_broadcast([P, NT, NE]),
                                       best_f[:, :, k:k + 1].to_broadcast([P, NT, NE]), ALU.is_equal))
            ch.done()
            ch.then(V.tensor_tensor(chosen[:, :, :], hot[:, 0, :, :], hot[:, 1, :, :], ALU.add))
            ch.then(V.tensor_tensor(chosen[:, :, :], chosen[:, :, :], hot[:, 2, :, :], ALU.add))
            V.tensor_tensor(chosen[:, :, :], chosen[:, :, :], hot[:, 3, :, :], ALU.add).then_inc(chosen_ready, 1)
            for k in range(TOP):
                ch.add(V.tensor_tensor(picked[:, k, :, :], hot[:, k, :, :], score[:, :, :], ALU.mult))
            ch.done()
            for k in range(TOP):
                ch.add(V.tensor_reduce(wk[:, :, k], picked[:, k, :, :], AX.X, ALU.add))
            ch.done()
            ch.then(V.tensor_reduce(wsum[:, :], wk[:, :, :], AX.X, ALU.add))
            ch.then(V.tensor_scalar(wsum[:, :], wsum[:, :], 1e-20, None, ALU.add))
            ch.then(V.reciprocal(wsum[:, :], wsum[:, :]))
            ch.add(V.scalar_tensor_tensor(c.weight[:, :, :], wk[:, :, :], 2.5,
                                          wsum[:, :].unsqueeze(2).to_broadcast([P, NT, TOP]), ALU.mult, ALU.mult))
            dve.wait_ge(counted, 1)
            ch.then(V.tensor_tensor_scan(incl[:, :, :].rearrange("p e t -> p (e t)"),
                                         carry[:, :, :].rearrange("p e t -> p (e t)"), ps_total[:, :], 0.0,
                                         ALU.mult, ALU.add))
            ch.add(V.tensor_tensor(excl[:, :, :].rearrange("p e t -> p (e t)"),
                                   incl[:, :, :].rearrange("p e t -> p (e t)"), ps_total[:, :], ALU.subtract))
            ch.then(V.tensor_scalar(tiles[:, :], incl[:, :, NT - 1], 1.0 / P, (P - 1) / 2 / P, ALU.mult, ALU.add))
            ch.then(V.tensor_scalar(tiles[:, :], tiles[:, :], ROUND, ROUND, ALU.add, ALU.subtract))
            ch.then(V.tensor_tensor_scan(ends[:, :], ones[:, 0:NE], tiles[:, :], 0.0, ALU.mult, ALU.add))
            ch.then(V.tensor_tensor(starts[:, :], ends[:, :], tiles[:, :], ALU.subtract))
            ch.then(V.scalar_tensor_tensor(excl[:, :, :], starts[:, :].unsqueeze(2).to_broadcast([P, NE, NT]), float(P),
                                           excl[:, :, :], ALU.mult, ALU.add))
            ch.then(V.tensor_tensor(slot_all[:, :, :].rearrange("p e t -> p (e t)"),
                                    excl[:, :, :].rearrange("p e t -> p (e t)"), ps_rank[:, :], ALU.add))
            for k in range(TOP):
                ch.add(V.tensor_tensor(picked[:, k, :, :], hot[:, k, :, :],
                                       slot_all[:, :, :].rearrange("p e t -> p t e"), ALU.mult))
            ch.done()
            for k in range(TOP):
                ch.add(V.tensor_reduce(slot_f[:, :, k], picked[:, k, :, :], AX.X, ALU.add))
            ch.done()
            ch.add(V.tensor_copy(c.slot[:, :, :], slot_f[:, :, :]))
            ch.then(V.tensor_tensor(owned[:, :, :], count_tiles[:, :].unsqueeze(2).to_broadcast([1, NS, NE]),
                                    ends[0:1, :].unsqueeze(1).to_broadcast([1, NS, NE]), ALU.is_ge))
            ch.then(V.tensor_reduce(owner_f[:, :], owned[:, :, :], AX.X, ALU.add))
            ch.then(V.tensor_scalar(c.owner[:, :], owner_f[:, :], NE - 1.0, None, ALU.min))


def shared_expert(nc, c, X, d):
    G = 4
    n = NT // G
    F = 2 * E
    with ExitStack() as ctx:
        ph = Phase(nc, ctx, "sh")
        wg, wu = ph.sb("wg", [P, KC, F]), ph.sb("wu", [P, KC, F])
        wd = ph.sb("wd", [P, F // P, E])
        xn = ph.sb("xn", [P, 2, G, E])
        xT = ph.sb("xT", [P, 2, KC, G * P])
        idx = ph.sb("idx", [P, 2, G * TOP], I32)
        act_g = ph.sb("act_g", [P, 2, G * P])
        gT = ph.sb("gT", [P, 2, F // P, G * P])
        ps_x = [ph.ps(f"x{i}") for i in range(2)]
        ps_g = [ph.ps(f"g{i}") for i in range(2)]
        ps_u = [ph.ps(f"u{i}") for i in range(2)]
        ps_o = [ph.ps(f"o{i}") for i in range(2)]
        loaded = ph.sem("loaded")
        xn_loaded = [ph.sem(f"xn_loaded{i}") for i in range(2)]
        scattered = [ph.sem(f"scattered{i}") for i in range(2)]
        idx_ready = ph.sem("idx_ready")
        xT_done, xT_ready = ph.sem("xT_done"), ph.sem("xT_ready")
        h_done, act_ready, g_ready = ph.sem("h_done"), ph.sem("act_ready"), ph.sem("g_ready")
        o_done, x_updated = ph.sem("o_done"), ph.sem("x_updated")
        block = ph.block()

        @block.sync
        def _(sp):
            sp.dma_start(wg[:, :, :], d["sh_wg"]).then_inc(loaded, 16)
            sp.dma_start(wu[:, :, :], d["sh_wu"]).then_inc(loaded, 16)
            sp.dma_start(wd[:, :, :], d["sh_wd"]).then_inc(loaded, 16)

            def step(s, par):
                if live(s, n):
                    if not (isinstance(s, int) and s < 2):
                        sp.wait_ge(xT_done, 2 * (s - 1))
                        sp.wait_ge(scattered[par], (s - par) * 8 * G * TOP)
                    sp.dma_start(xn[:, par, :, :], c.xn_dram[G * s:G * s + G, :, :].rearrange("t p e -> p t e")
                                 if isinstance(s, int) else
                                 c.xn_dram.rearrange("(n t) p e -> n p t e", t=G)[s, :, :, :])\
                        .then_inc(xn_loaded[par], 16)
            tile_steps(sp, step, n=n, lag=0)

        @block.gpsimd
        def _(pool):
            pool.wait_ge(c.zeroed, 16 * (NS // ZERO_TILES))

            def step(s, par):
                if live(s, n):
                    wait(pool, scattered[par], (s - par) * 8 * G * TOP)
                    nc.gpsimd.tensor_copy(idx[:, par, :],
                                          c.slot[:, :, :].rearrange("p (n t) k -> p n (t k)", t=G)[:, s, :])\
                        .then_inc(idx_ready, 1)
                    pool.wait_ge(idx_ready, s + 1)
                    wait_apart(pool, xn_loaded[par], s * 8 + (16 - 8 * par), c.passed_pool)
                    for i in range(G):
                        for k in range(TOP):
                            nc.gpsimd.indirect_dma_start(
                                c.xg_dram[:, :],
                                bass.IndirectOffsetOnAxis(ap=idx[:, par, TOP * i + k:TOP * i + k + 1], axis=0),
                                xn[:, par, i, :], None).then_inc(scattered[par], 16)
            tile_steps(pool, step, n=n, lag=0)
            for par in range(2):
                pool.wait_ge(scattered[par], 16 * G * TOP * n // 2)

        @block.scalar
        def _(act):
            act.wait_ge(loaded, 16 * 3)

            def step(s, par):
                t = s - 1
                if live(s, n):
                    for w, src in ((c.w1, "moe_w1"), (c.w2, "moe_w2")):
                        act.dma_start(w[:, :, :, :].rearrange("p (n e) k f -> p n e k f", n=n)[:, s, :, :, :],
                                      d[src].rearrange("p (n e) k f -> p n e k f", n=n)[:, s, :, :, :])\
                            .then_inc(c.moe_loaded, 16)
                if live(t, n):
                    for f in range(4):
                        act.wait_ge(h_done, 4 * t + f + 1)
                        wait(act, g_ready, 4 * t + f - 1)
                        nc.scalar.activation(act_g[:, f % 2, :], ps_g[f % 2][:, :], ACT.Silu).then_inc(act_ready, 1)
            tile_steps(act, step, n=n, lag=1)

        @block.vector
        def _(dve):
            def step(s, par):
                p, e = s - 1, s - 2
                if live(s, n):
                    for k in range(KC):
                        dve.wait_ge(xT_done, 2 * s + k + 1)
                        wait(dve, h_done, 4 * (s - 1))
                        nc.vector.tensor_copy(xT[:, par, k, :], ps_x[k][:, :]).then_inc(xT_ready, 1)
                for f in range(4):
                    if live(p, n):
                        dve.wait_ge(act_ready, 4 * p + f + 1)
                        wait(dve, o_done, 4 * (p - 1))
                        nc.vector.tensor_tensor(gT[:, 1 - par, f, :], act_g[:, f % 2, :], ps_u[f % 2][:, :], ALU.mult)\
                            .then_inc(g_ready, 1)
                    if live(e, n):
                        dve.wait_ge(o_done, 4 * e + f + 1)
                        nc.vector.tensor_tensor(X[:, G * e + f, :], X[:, G * e + f, :], ps_o[f % 2][:, 0:E], ALU.add)\
                            .then_inc(x_updated, 1)
            tile_steps(dve, step, n=n, lag=2)

        @block.tensor
        def _(pe):
            pe.wait_ge(loaded, 16 * 3)

            def step(s, par):
                p, e = s - 1, s - 2
                if live(s, n):
                    pe.wait_ge(xn_loaded[par], s * 8 + (16 - 8 * par))
                    wait(pe, xT_ready, 2 * s)
                    for k in range(KC):
                        for i in range(G):
                            mm = nc.tensor.transpose(ps_x[k][:, i * P:(i + 1) * P], xn[:, par, i, k * P:(k + 1) * P],
                                                     c.ident[:, :])
                        mm.then_inc(xT_done, 1)
                for f in range(4):
                    if live(p, n):
                        wait(pe, g_ready, 4 * p + f - 1)
                        if f == 0:
                            pe.wait_ge(xT_ready, 2 * p + 2)
                        for ps, w in ((ps_g, wg), (ps_u, wu)):
                            for k in range(KC):
                                mm = nc.tensor.matmul(ps[f % 2][:, :], w[:, k, f * P:(f + 1) * P],
                                                      xT[:, 1 - par, k, :], start=(k == 0), stop=(k == KC - 1))
                        mm.then_inc(h_done, 1)
                    if live(e, n):
                        if f == 0:
                            pe.wait_ge(g_ready, 4 * e + 4)
                        wait(pe, x_updated, 4 * e + f - 1)
                        for k in range(F // P):
                            mm = nc.tensor.matmul(ps_o[f % 2][:, 0:E], gT[:, par, k, f * P:(f + 1) * P], wd[:, k, :],
                                                  start=(k == 0), stop=(k == F // P - 1))
                        mm.then_inc(o_done, 1)
            tile_steps(pe, step, n=n, lag=2)


def experts(nc, c, d):
    with ExitStack() as ctx:
        ph = Phase(nc, ctx, "ex")
        xg = ph.sb("xg", [P, 4, E])
        xT = ph.sb("xT", [P, 2, KC, P])
        act_g = ph.sb("act_g", [P, 2, E])
        g = ph.sb("g", [P, 2, E])
        gT = ph.sb("gT", [P, 2, KC, P])
        y = ph.sb("y", [P, 2, E])
        ps_h = [ph.ps(f"h{i}") for i in range(2)]
        ps_x, ps_g = ph.ps("x"), ph.ps("g")
        ps_y = [ph.ps(f"y{i}") for i in range(2)]
        x_loaded = [ph.sem(f"x_loaded{i}") for i in range(4)]
        stored = [ph.sem(f"stored{i}") for i in range(2)]
        xT_done, xT_ready = ph.sem("xT_done"), ph.sem("xT_ready")
        h_done, act_ready, g_ready = ph.sem("h_done"), ph.sem("act_ready"), ph.sem("g_ready")
        gT_done, gT_ready = ph.sem("gT_done"), ph.sem("gT_ready")
        y_done, y_ready = ph.sem("y_done"), ph.sem("y_ready")
        block = ph.block()

        def steps4(eng, step, lag):
            for s in range(8):
                step(s, s % 4)
            with eng.Fori(0, (NS - 8) // 4) as i:
                for u in range(4):
                    step(i * 4 + (8 + u), u)
            for s in range(NS, NS + lag):
                step(s, s % 4)

        @block.sync
        def _(sp):
            def step(s, q):
                if live(s, NS):
                    wait(sp, xT_done, s - 3)
                    sp.dma_start(xg[:, q, :], c.xg_dram.rearrange("(n p) e -> n p e", p=P)[s, :, :])\
                        .then_inc(x_loaded[q], 16)
            steps4(sp, step, 0)

        @block.tensor
        def _(pe):
            pe.wait_ge(c.moe_loaded, 16 * 2 * NT // 4)

            def step(s, q):
                t, p, a, e = s, s - 1, s - 2, s - 3
                par = q % 2
                if live(p, NS):
                    own = pe.value_load(c.owner[0:1, bass.ds(p, 1)], min_val=0, max_val=NE - 1)
                    pe.wait_ge(xT_ready, p + 1)
                    wait(pe, g_ready, p - 1)
                    for k in range(KC):
                        mm = nc.tensor.matmul(ps_h[1 - par][:, :], xT[:, 1 - par, k, :], c.w1[:, own, k, :],
                                              start=(k == 0), stop=(k == KC - 1))
                    mm.then_inc(h_done, 1)
                if live(t, NS):
                    pe.wait_ge(x_loaded[q], (s - q) * 4 + 16)
                    wait(pe, xT_ready, t)
                    for k in range(KC):
                        mm = nc.tensor.transpose(ps_x[:, k * P:(k + 1) * P], xg[:, q, k * P:(k + 1) * P], c.ident[:, :])
                    mm.then_inc(xT_done, 1)
                if live(e, NS):
                    own = pe.value_load(c.owner[0:1, bass.ds(e, 1)], min_val=0, max_val=NE - 1)
                    pe.wait_ge(gT_ready, e + 1)
                    wait(pe, y_ready, e - 1)
                    for k in range(KC):
                        mm = nc.tensor.matmul(ps_y[1 - par][:, 0:E], gT[:, 1 - par, k, :], c.w2[:, own, k, :],
                                              start=(k == 0), stop=(k == KC - 1))
                    mm.then_inc(y_done, 1)
                if live(a, NS):
                    pe.wait_ge(g_ready, a + 1)
                    wait(pe, gT_ready, a)
                    for k in range(KC):
                        mm = nc.tensor.transpose(ps_g[:, k * P:(k + 1) * P], g[:, par, k * P:(k + 1) * P], c.ident[:, :])
                    mm.then_inc(gT_done, 1)
            steps4(pe, step, 3)

        @block.scalar
        def _(act):
            def step(s, q):
                p, a, e = s - 1, s - 2, s - 3
                par = q % 2
                if live(p, NS):
                    act.wait_ge(h_done, p + 1)
                    wait(act, g_ready, p - 1)
                    nc.scalar.activation(act_g[:, 1 - par, :], ps_h[1 - par][:, 0:E], ACT.Silu).then_inc(act_ready, 1)
                if live(e, NS):
                    act.wait_ge(y_done, e + 1)
                    wait(act, stored[1 - par], (e - (1 - par)) * 8)
                    nc.scalar.activation(y[:, 1 - par, :], ps_y[1 - par][:, 0:E], ACT.Copy).then_inc(y_ready, 1)
                    act.wait_ge(y_ready, e + 1)
                    act.dma_start(c.y_dram.rearrange("(n p) e -> n p e", p=P)[e, :, :], y[:, 1 - par, :])\
                        .then_inc(stored[1 - par], 16)
            steps4(act, step, 3)
            for par in range(2):
                act.wait_ge(stored[par], 16 * (NS // 2))

        @block.vector
        def _(dve):
            def step(s, q):
                t, p, a = s, s - 1, s - 2
                par = q % 2
                if live(p, NS):
                    dve.wait_ge(act_ready, p + 1)
                    wait(dve, gT_done, p - 1)
                    nc.vector.tensor_tensor(g[:, 1 - par, :], act_g[:, 1 - par, :], ps_h[1 - par][:, E:2 * E], ALU.mult)\
                        .then_inc(g_ready, 1)
                if live(t, NS):
                    dve.wait_ge(xT_done, t + 1)
                    wait(dve, h_done, t - 1)
                    nc.vector.tensor_copy(xT[:, par, :, :], ps_x[:, 0:E].rearrange("p (k t) -> p k t", k=KC))\
                        .then_inc(xT_ready, 1)
                if live(a, NS):
                    dve.wait_ge(gT_done, a + 1)
                    wait(dve, y_done, a - 1)
                    nc.vector.tensor_copy(gT[:, par, :, :], ps_g[:, 0:E].rearrange("p (k t) -> p k t", k=KC))\
                        .then_inc(gT_ready, 1)
            steps4(dve, step, 2)


def cross_attention_1(nc, c, X, d):
    with ExitStack() as ctx:
        ph = Phase(nc, ctx, "xb")
        ctxT = ph.sb("ctxT", [P, 4, KC, 2 * S])
        ctx_rows = ph.sb("ctx_rows", [P, 4, SC, E])
        xT = ph.sb("xT", [P, 2, KC, P])
        sT = ph.sb("sT", [P, 2, SC, T])
        neg_max = ph.sb("neg_max", [P, 2])
        ex = ph.sb("ex", [P, 2, E])
        total, rz = ph.sb("total", [P, 2]), ph.sb("rz", [P, 2])
        idx = ph.sb("idx", [P, 4, TOP], I32)
        expert_y = ph.sb("expert_y", [P, 4, TOP, E])
        ln = LayerNorm(ph, c, X)
        ps_x = [ph.ps(f"x{i}") for i in range(2)]
        ps_s = [ph.ps(f"s{i}") for i in range(2)]
        ps_o = [ph.ps(f"o{i}") for i in range(2)]
        ctx_loaded = [ph.sem(f"ctx_loaded{i}") for i in range(4)]
        xT_done, xT_ready = ph.sem("xT_done"), ph.sem("xT_ready")
        s_done, s_ready = ph.sem("s_done"), ph.sem("s_ready")
        o_done, max_ready, exp_ready = ph.sem("o_done"), ph.sem("max_ready"), ph.sem("exp_ready")
        idx_ready, added = ph.sem("idx_ready"), ph.sem("added")
        gathered = [ph.sem(f"gathered{i}") for i in range(4)]
        rz_ready, x_updated = ph.sem("rz_ready"), ph.sem("x_updated")
        block = ph.block()

        @block.sync
        def _(sp):
            def step(s, q):
                if live(s):
                    wait(sp, s_done, s - 3)
                    sp.dma_start(ctxT[:, q, :, :], d["ctxT"][s, :, :, :]).then_inc(ctx_loaded[q], 16)
                    wait(sp, o_done, s - 3)
                    sp.dma_start(ctx_rows[:, q, :, :], d["ctx_rows"][s, :, :, :]).then_inc(ctx_loaded[q], 16)
            tile_steps(sp, step, lag=0, turn=4, peel=8)

        @block.gpsimd
        def _(pool):
            def step(s, q):
                t = s - 2
                if live(s):
                    wait(pool, added, TOP * (s - 3))
                    nc.gpsimd.tensor_copy(idx[:, q, :], c.slot[:, s, :]).then_inc(idx_ready, 1)
                    wait_apart(pool, idx_ready, s + 1, c.passed_pool)
                    for k in range(TOP):
                        nc.gpsimd.indirect_dma_start(
                            expert_y[:, q, k, :], None, c.y_dram[:, :],
                            bass.IndirectOffsetOnAxis(ap=idx[:, q, k:k + 1], axis=0)).then_inc(gathered[q], 16)
                if live(t):
                    ln.inverse_std(pool, nc, t, q % 2)
            tile_steps(pool, step, lag=2, turn=4, peel=8)

        @block.tensor
        def _(pe):
            def step(s, q):
                t, m, o = s - 3, s - 4, s - 5
                if live(m):
                    pe.wait_ge(ctx_loaded[q], (m - q) * 8 + 32)
                    pe.wait_ge(xT_ready, m + 1)
                    wait(pe, s_ready, m - 1)
                    for ch in range(SC):
                        for k in range(KC):
                            mm = nc.tensor.matmul(ps_s[q % 2][:, ch * T:(ch + 1) * T],
                                                  ctxT[:, q, k, ch * P:(ch + 1) * P],
                                                  xT[:, q % 2, k, (ch // 2) * T:(ch // 2 + 1) * T],
                                                  start=(k == 0), stop=(k == KC - 1))
                    mm.then_inc(s_done, 1)
                if live(t):
                    pe.wait_ge(ln.xn_ready, t + 1)
                    wait(pe, xT_ready, t - 1)
                    for k in range(KC):
                        mm = nc.tensor.transpose(ps_x[1 - q % 2][:, k * P:(k + 1) * P],
                                                 ln.xn[:, 1 - q % 2, k * P:(k + 1) * P], c.ident[:, :])
                    mm.then_inc(xT_done, 1)
                if live(o):
                    pe.wait_ge(s_ready, o + 1)
                    wait(pe, exp_ready, o - 1)
                    for ch in range(SC):
                        mm = nc.tensor.matmul(ps_o[1 - q % 2][(ch // 2) * T:(ch // 2 + 1) * T, 0:E],
                                              sT[:, 1 - q % 2, ch, :], ctx_rows[:, (q - 1) % 4, ch, :],
                                              start=(ch % 2 == 0), stop=(ch % 2 == 1))
                    mm.then_inc(o_done, 1)
            tile_steps(pe, step, lag=5, turn=4, peel=8)

        @block.scalar
        def _(act):
            def step(s, q):
                m, o = s - 4, s - 5
                if live(m):
                    act.wait_ge(s_done, m + 1)
                    wait(act, o_done, m - 1)
                    nc.scalar.activation(sT[:, q % 2, :, :].rearrange("p c t -> p (c t)"), ps_s[q % 2][:, 0:SC * T],
                                         ACT.Copy, scale=E ** -0.5).then_inc(s_ready, 1)
                if live(o):
                    act.wait_ge(max_ready, o + 1)
                    wait(act, x_updated, o - 1)
                    nc.scalar.activation(ex[:, 1 - q % 2, :], ps_o[1 - q % 2][:, 0:E], ACT.Exp,
                                         bias=neg_max[:, 1 - q % 2:2 - q % 2],
                                         accum_out=total[:, 1 - q % 2:2 - q % 2]).then_inc(exp_ready, 1)
            tile_steps(act, step, lag=5, turn=4, peel=8)

        @block.vector
        def _(dve):
            def step(s, q):
                l, t, o = s - 2, s - 3, s - 5
                par = q % 2
                if live(l):
                    dve.wait_ge(gathered[(q - 2) % 4], (l - (q - 2) % 4) * 4 * TOP + 16 * TOP)
                    for k in range(TOP):
                        wait(dve, added, TOP * l + k)
                        nc.vector.scalar_tensor_tensor(X[:, l, :], expert_y[:, (q - 2) % 4, k, :],
                                                       c.weight[:, l, k:k + 1], X[:, l, :],
                                                       ALU.mult, ALU.add).then_inc(added, 1)
                    wait_apart(dve, added, TOP * l + TOP, c.passed_dve)
                    ln.statistics(dve, nc, l, par)
                if live(t):
                    dve.wait_ge(xT_done, t + 1)
                    wait(dve, s_done, t - 1)
                    nc.vector.tensor_copy(xT[:, 1 - par, :, :], ps_x[1 - par][:, 0:E].rearrange("p (k t) -> p k t", k=KC))\
                        .then_inc(xT_ready, 1)
                if live(o):
                    dve.wait_ge(o_done, o + 1)
                    nc.vector.tensor_reduce(neg_max[:, 1 - par:2 - par], ps_o[1 - par][:, 0:E], AX.X, ALU.max,
                                            negate=True).then_inc(max_ready, 1)
                if live(l):
                    ln.normalise(dve, nc, l, par, xT_done)
                if live(o):
                    dve.wait_ge(exp_ready, o + 1)
                    nc.vector.reciprocal(rz[:, 1 - par:2 - par], total[:, 1 - par:2 - par]).then_inc(rz_ready, 1)
                    dve.wait_ge(rz_ready, o + 1)
                    nc.vector.scalar_tensor_tensor(X[:, o, :], ex[:, 1 - par, :], rz[:, 1 - par:2 - par], X[:, o, :],
                                                   ALU.mult, ALU.add).then_inc(x_updated, 1)
            tile_steps(dve, step, lag=5, turn=4, peel=8)


def feed_forward(nc, c, X, d):
    G, n, F = 4, NT // 4, 1024
    FC = F // P
    W = G * P
    with ExitStack() as ctx:
        ph = Phase(nc, ctx, "ff")
        w_raw = [ph.sb("w1_raw", [P, KC * F]), ph.sb("w2_raw", [P, FC * E])]
        w1 = ph.sb("w1", [P, KC, F], BF16)
        w2 = ph.sb("w2", [P, FC, E], BF16)
        cw, cb = ph.sb("cw", [P, FC, 3]), ph.sb("cb", [P, FC])
        ones = ph.sb("ones", [P, P])
        w_sum, w_scale = ph.sb("w_sum", [P, 2]), ph.sb("w_scale", [P, 2])
        w_mean = ph.sb("w_mean", [P, 2])
        rounding = ph.sb("rounding", [P, 2])
        stats = ph.sb("stats", [P, G, 6])
        mv = ph.sb("mv", [P, G, 2])
        var_eps, rstd = ph.sb("var_eps", [P, G]), ph.sb("rstd", [P, G])
        xn = ph.sb("xn", [P, G, E])
        xr = ph.sb("xr", [P, G, E])
        top1, top2 = ph.sb("top1", [P, G]), ph.sb("top2", [P, G])
        scale1, scale2 = ph.sb("scale1", [P, G]), ph.sb("scale2", [P, G])
        back1, back2 = ph.sb("back1", [P, G]), ph.sb("back2", [P, 2, G])
        diag1, diag2 = ph.sb("diag1", [P, G, P]), ph.sb("diag2", [P, G, P])
        xqT = ph.sb("xqT", [P, 2, KC, W], BF16)
        back_b = ph.sb("back_b", [P, 2, W])
        scale_b = ph.sb("scale_b", [P, 2, W])
        tap = ph.sb("tap", [P, 2, FC, P])
        h = ph.sb("h", [P, 4, W // T, T + 2])
        y = ph.sb("y", [P, 2, FC, W])
        peak = ph.sb("peak", [P, 2, W])
        hq = ph.sb("hq", [P, 2, FC, W], BF16)
        ps_h = [ph.ps(f"h{i}") for i in range(2)]
        ps_y = [ph.ps(f"y{i}") for i in range(2)]
        ps_x, ps_b = ph.ps("x"), ph.ps("b")
        ps_o = [ph.ps(f"o{i}") for i in range(2)]
        loaded, n_loads = ph.sem("loaded"), 4
        consts_set, w_summed, w_totalled = ph.sem("consts_set"), ph.sem("w_summed"), ph.sem("w_totalled")
        prepared, w_ready = ph.sem("prepared"), ph.sem("w_ready")
        stats_done, var_ready, eps_added = ph.sem("stats_done"), ph.sem("var_ready"), ph.sem("eps_added")
        rstd_ready, xn_ready = ph.sem("rstd_ready"), ph.sem("xn_ready")
        top1_ready, scale1_ready = ph.sem("top1_ready"), ph.sem("scale1_ready")
        xr_ready, diag1_ready = ph.sem("xr_ready"), ph.sem("diag1_ready")
        xT_done, xqT_ready = ph.sem("xT_done"), ph.sem("xqT_ready")
        back_done, back_ready = ph.sem("back_done"), ph.sem("back_ready")
        h_done, h_ready = ph.sem("h_done"), ph.sem("h_ready")
        tap_set, taps_done, y_ready = ph.sem("tap_set"), ph.sem("taps_done"), ph.sem("y_ready")
        silu_ready, peak_ready, peak_done = ph.sem("silu_ready"), ph.sem("peak_ready"), ph.sem("peak_done")
        top2_ready, scale2_ready = ph.sem("top2_ready"), ph.sem("scale2_ready")
        diag2_ready, scale_done, scale_ready = ph.sem("diag2_ready"), ph.sem("scale_done"), ph.sem("scale_ready")
        scaled, rounded, hq_ready = ph.sem("scaled"), ph.sem("rounded"), ph.sem("hq_ready")
        o_done, x_updated = ph.sem("o_done"), ph.sem("x_updated")

        def unit(s, f, ahead):
            g = s - 1 - (1 if f < ahead else 0)
            return g, (f - ahead) % FC
        block = ph.block()

        @block.sync
        def _(sp):
            sp.dma_start(w_raw[0][:, :], d["ff_w1T"].rearrange("p k n -> p (k n)")).then_inc(loaded, 16)
            sp.dma_start(w_raw[1][:, :], d["ff_w2T"].rearrange("p k n -> p (k n)")).then_inc(loaded, 16)
            sp.dma_start(cw[:, :, :], d["ff_cw"]).then_inc(loaded, 16)
            sp.dma_start(cb[:, :], d["ff_cb"]).then_inc(loaded, 16)

        @block.gpsimd
        def _(pool):
            nc.gpsimd.memset(rounding[:, 0:1], ROUND).then_inc(consts_set, 1)
            nc.gpsimd.memset(rounding[:, 1:2], -ROUND).then_inc(consts_set, 1)
            nc.gpsimd.memset(ones[:, :], 1.0).then_inc(consts_set, 1)
            nc.gpsimd.memset(h[:, :, :, :], 0.0).then_inc(consts_set, 1)

            def step(s, par):
                for f in range(FC):
                    if f == 2 and live(s, n):
                        wait_apart(pool, var_ready, s + 1, c.passed_pool)
                        nc.gpsimd.tensor_scalar(var_eps[:, :], mv[:, :, 1], LN_EPS, None, ALU.add).then_inc(eps_added, 1)
                        pool.wait_ge(eps_added, s + 1)
                        nc.gpsimd.tensor_tensor(rstd[:, :], var_eps[:, :], c.minus_half[:, 0:1].to_broadcast([P, G]),
                                                ALU.pow).then_inc(rstd_ready, 1)
                    g, j = (s - 2 if f >= 6 else s - 3), (f - 6) % FC
                    if live(g, n):
                        gp = (par + (f < 6)) % 2
                        pool.wait_ge(scale_ready, g + 1)
                        nc.gpsimd.tensor_tensor(y[:, gp, j, :], y[:, gp, j, :], scale_b[:, gp, :], ALU.mult)\
                            .then_inc(scaled, 1)
                    g, j = (s - 2 if f >= 7 else s - 3), (f - 7) % FC
                    if live(g, n):
                        gp = (par + (f < 7)) % 2
                        pool.wait_ge(scaled, FC * g + j + 1)
                        nc.gpsimd.tensor_tensor(y[:, gp, j, :], y[:, gp, j, :],
                                                rounding[:, 0:1].to_broadcast([P, W]), ALU.add).then_inc(rounded, 1)
            tile_steps(pool, step, n=n, lag=4)

        @block.vector
        def _(dve):
            V = nc.vector
            ch = Chain(dve, prepared)
            dve.wait_ge(loaded, 16 * n_loads)
            for i in range(2):
                V.tensor_reduce(w_sum[:, i:i + 1], w_raw[i][:, :], AX.X, ALU.add, apply_absolute_value=True)\
                    .then_inc(w_summed, 1)
            dve.wait_ge(w_totalled, 1)
            ch.then(V.tensor_scalar(w_mean[:, :], ps_x[:, 0:2], 1.0 / (F * E), 1e-5, ALU.mult, ALU.max))
            ch.then(V.reciprocal(w_scale[:, :], w_mean[:, :]))
            for i in range(2):
                ch.add(V.tensor_scalar(w_raw[i][:, :], w_raw[i][:, :], w_scale[:, i:i + 1], ROUND, ALU.mult, ALU.add))
            ch.done()
            for i in range(2):
                ch.add(V.tensor_scalar(w_raw[i][:, :], w_raw[i][:, :], ROUND, 1.0, ALU.subtract, ALU.min))
            ch.done()
            for i, w in enumerate((w1, w2)):
                V.tensor_scalar(w[:, :, :].rearrange("p k n -> p (k n)"), w_raw[i][:, :], -1.0, None, ALU.max)\
                    .then_inc(w_ready, 1)
            dve.wait_ge(consts_set, 4)

            def step(s, par):
                q, last = s - 2, s - 4
                for f in range(FC):
                    g = s - 1
                    if live(g, n):
                        if f == 0:
                            dve.wait_ge(back_ready, g + 1)
                        dve.wait_ge(h_done, FC * g + f + 1)
                        wait(dve, taps_done, FC * g + f - 3)
                        V.tensor_tensor(h[:, f % 4, :, 1:T + 1], ps_h[f % 2][:, :].rearrange("p (b t) -> p b t", t=T),
                                        back_b[:, 1 - par, :].rearrange("p (b t) -> p b t", t=T), ALU.mult)\
                            .then_inc(h_ready, 1)
                    g, j = unit(s, f, 2)
                    if live(g, n):
                        yp = (par + 1 + (f < 2)) % 2
                        dve.wait_ge(taps_done, FC * g + j + 1)
                        wait(dve, hq_ready, FC * (g - 2) + j + 1)
                        V.scalar_tensor_tensor(y[:, yp, j, :].rearrange("p (b t) -> p b t", t=T),
                                               h[:, j % 4, :, 1:T + 1], cw[:, j, 1:2],
                                               ps_y[j % 2][:, :].rearrange("p (b t) -> p b t", t=T),
                                               ALU.mult, ALU.add).then_inc(y_ready, 1)
                    g, half = (s - 1, 0) if f == 7 else (q, 1)
                    if f in (3, 7) and live(g, n):
                        dve.wait_ge(silu_ready, FC * g + 4 * half + 4)
                        wait(dve, peak_done, g)
                        V.tensor_reduce(peak[:, half, :],
                                        y[:, (par + 1 + half) % 2, 4 * half:4 * half + 4, :].rearrange("p j t -> p t j"),
                                        AX.X, ALU.max, apply_absolute_value=True).then_inc(peak_ready, 1)
                        if half:
                            dve.wait_ge(peak_ready, 3 * g + 2)
                            V.tensor_tensor(peak[:, 0, :], peak[:, 0, :], peak[:, 1, :], ALU.max).then_inc(peak_ready, 1)
                    if f == 0 and live(s, n):
                        for i in range(G):
                            V.bn_stats(stats[:, i, :], X[:, s * G + i, :]).then_inc(stats_done, 1)
                    if f == 1 and live(s, n):
                        wait_apart(dve, stats_done, G * s + G, c.passed_dve)
                        for i in range(G):
                            ins = V.bn_aggr(mv[:, i, :], stats[:, i, :])
                        ins.then_inc(var_ready, 1)
                    if f == 3 and live(s, n):
                        dve.wait_ge(rstd_ready, s + 1)
                        wait(dve, xr_ready, s)
                        for i in range(G):
                            ins = V.tensor_scalar(xn[:, i, :], X[:, s * G + i, :], mv[:, i, 0:1], rstd[:, i:i + 1],
                                                  ALU.subtract, ALU.mult)
                        ins.then_inc(xn_ready, 1)
                    if f == 4 and live(s, n):
                        dve.wait_ge(xn_ready, s + 1)
                        wait(dve, diag1_ready, s)
                        V.tensor_reduce(top1[:, :], xn[:, :, :], AX.X, ALU.max, apply_absolute_value=True)\
                            .then_inc(top1_ready, 1)
                        dve.wait_ge(top1_ready, 3 * s + 1)
                        V.tensor_scalar(top1[:, :], top1[:, :], 1e-5, None, ALU.max).then_inc(top1_ready, 1)
                        dve.wait_ge(top1_ready, 3 * s + 2)
                        V.reciprocal(scale1[:, :], top1[:, :]).then_inc(top1_ready, 1)
                        dve.wait_ge(top1_ready, 3 * s + 3)
                        V.tensor_scalar(scale1[:, :], scale1[:, :], 127.0, None, ALU.mult)
                        V.tensor_scalar(back1[:, :], top1[:, :], w_mean[:, 0:1], 1.0 / 127, ALU.mult, ALU.mult)\
                            .then_inc(scale1_ready, 1)
                    if f == 4 and live(q, n):
                        dve.wait_ge(peak_done, q + 1)
                        wait(dve, diag2_ready, q)
                        V.tensor_reduce(top2[:, :], ps_x[:, :].rearrange("p (i c) -> p i c", i=G), AX.X, ALU.max)\
                            .then_inc(top2_ready, 1)
                        dve.wait_ge(top2_ready, 3 * q + 1)
                        V.tensor_scalar(top2[:, :], top2[:, :], 1e-5, None, ALU.max).then_inc(top2_ready, 1)
                        dve.wait_ge(top2_ready, 3 * q + 2)
                        V.reciprocal(scale2[:, :], top2[:, :]).then_inc(top2_ready, 1)
                        dve.wait_ge(top2_ready, 3 * q + 3)
                        V.tensor_scalar(scale2[:, :], scale2[:, :], 127.0, None, ALU.mult)
                        V.tensor_scalar(back2[:, par, :], top2[:, :], w_mean[:, 1:2], 1.0 / 127, ALU.mult, ALU.mult)\
                            .then_inc(scale2_ready, 1)
                    if f in (1, 2) and live(last, n):
                        for i in (2 * f - 2, 2 * f - 1):
                            dve.wait_ge(o_done, G * last + i + 1)
                            V.scalar_tensor_tensor(X[:, last * G + i, :], ps_o[i % 2][:, 0:E], back2[:, par, i:i + 1],
                                                   X[:, last * G + i, :], ALU.mult, ALU.add).then_inc(x_updated, 1)
            tile_steps(dve, step, n=n, lag=4)

        @block.scalar
        def _(act):
            act.wait_ge(consts_set, 4)
            act.wait_ge(loaded, 16 * n_loads)
            for i, t in enumerate((0, 2)):
                for j in range(FC):
                    ins = nc.scalar.activation(tap[:, i, j, :], c.ident[:, :], ACT.Copy, scale=cw[:, j, t:t + 1])
            ins.then_inc(tap_set, 1)

            def step(s, par):
                q = s - 2
                for f in range(FC):
                    if f == 6 and live(q, n):
                        act.wait_ge(scale_done, q + 1)
                        wait(act, scaled, FC * (q - 1))
                        nc.scalar.activation(scale_b[:, par, :], ps_b[:, :], ACT.Copy).then_inc(scale_ready, 1)
                    if f == 6 and live(s, n):
                        wait(act, h_done, FC * (s - 1))
                        for k in range(KC):
                            act.wait_ge(xT_done, KC * s + k + 1)
                            nc.scalar.activation(xqT[:, par, k, :], ps_x[:, :], ACT.Identity,
                                                 bias=rounding[:, 1:2]).then_inc(xqT_ready, 1)
                        act.wait_ge(back_done, s + 1)
                        wait(act, h_ready, FC * (s - 1))
                        nc.scalar.activation(back_b[:, par, :], ps_b[:, :], ACT.Copy).then_inc(back_ready, 1)
                    g, j = unit(s, f, 3)
                    if live(g, n):
                        yj = y[:, (par + 1 + (f < 3)) % 2, j, :]
                        act.wait_ge(y_ready, FC * g + j + 1)
                        nc.scalar.activation(yj, yj, ACT.Silu, bias=cb[:, j:j + 1]).then_inc(silu_ready, 1)
                    g, j = s - 3, f
                    if live(g, n):
                        gp = 1 - par
                        act.wait_ge(rounded, FC * g + j + 1)
                        nc.scalar.activation(hq[:, gp, j, :], y[:, gp, j, :], ACT.Identity,
                                             bias=rounding[:, 1:2]).then_inc(hq_ready, 1)
                    if f == 4 and live(q, n):
                        act.wait_ge(scale2_ready, q + 1)
                        wait(act, scale_done, q)
                        for i in range(G):
                            ins = nc.scalar.activation(diag2[:, i, :], c.ident[:, :], ACT.Copy, scale=scale2[:, i:i + 1])
                        ins.then_inc(diag2_ready, 1)
                    if f == 5 and live(s, n):
                        act.wait_ge(scale1_ready, s + 1)
                        wait(act, xT_done, KC * s)
                        for i in range(G):
                            ins = nc.scalar.activation(xr[:, i, :], xn[:, i, :], ACT.Identity, bias=rounding[:, 0:1],
                                                       scale=scale1[:, i:i + 1])
                        ins.then_inc(xr_ready, 1)
                        wait(act, back_done, s)
                        for i in range(G):
                            ins = nc.scalar.activation(diag1[:, i, :], c.ident[:, :], ACT.Copy, scale=back1[:, i:i + 1])
                        ins.then_inc(diag1_ready, 1)
            tile_steps(act, step, n=n, lag=4)

        @block.tensor
        def _(pe):
            pe.wait_ge(consts_set, 4)
            pe.wait_ge(w_summed, 2)
            nc.tensor.matmul(ps_x[:, 0:2], ones[:, :], w_sum[:, :], start=True, stop=True).then_inc(w_totalled, 1)
            pe.wait_ge(w_ready, 2)
            pe.wait_ge(tap_set, 1)

            def step(s, par):
                q, last = s - 2, s - 4
                for f in range(FC):
                    g = s - 1
                    if live(g, n):
                        if f == 0:
                            pe.wait_ge(xqT_ready, KC * g + KC)
                        wait(pe, h_ready, FC * g + f - 1)
                        for k in range(KC):
                            mm = nc.tensor.matmul(ps_h[f % 2][:, :], w1[:, k, f * P:(f + 1) * P],
                                                  xqT[:, 1 - par, k, :], start=(k == 0), stop=(k == KC - 1))
                        mm.then_inc(h_done, 1)
                    g, j = unit(s, f, 1)
                    if live(g, n):
                        pe.wait_ge(h_ready, FC * g + j + 1)
                        wait(pe, y_ready, FC * g + j - 1)
                        for i in range(2):
                            mm = nc.tensor.matmul(ps_y[j % 2][:, :], tap[:, i, j, :],
                                                  h[:, j % 4, :, 2 * i:2 * i + T], start=(i == 0), stop=(i == 1))
                        mm.then_inc(taps_done, 1)
                    if f == 3 and live(q, n):
                        pe.wait_ge(peak_ready, 3 * q + 3)
                        pe.wait_ge(xqT_ready, KC * (q + 2) if not isinstance(q, int) else KC * min(n, q + 2))
                        for i in range(G):
                            mm = nc.tensor.transpose(ps_x[:, i * P:(i + 1) * P], peak[:, 0, i * P:(i + 1) * P],
                                                     c.ident[:, :])
                        mm.then_inc(peak_done, 1)
                    if f == 5 and live(q, n):
                        pe.wait_ge(diag2_ready, q + 1)
                        pe.wait_ge(back_ready, q + 2 if not isinstance(q, int) else min(n, q + 2))
                        nc.tensor.matmul(ps_b[:, :], ones[:, :], diag2[:, :, :].rearrange("p i t -> p (i t)"),
                                         start=True, stop=True).then_inc(scale_done, 1)
                    if f == 6 and live(s, n):
                        pe.wait_ge(xr_ready, s + 1)
                        if live(q, n):
                            pe.wait_ge(top2_ready, 3 * q + 1)
                        for k in range(KC):
                            wait(pe, xqT_ready, KC * s + k)
                            for i in range(G):
                                mm = nc.tensor.transpose(ps_x[:, i * P:(i + 1) * P], xr[:, i, k * P:(k + 1) * P],
                                                         c.ident[:, :])
                            mm.then_inc(xT_done, 1)
                        pe.wait_ge(diag1_ready, s + 1)
                        wait(pe, scale_ready, s - 1)
                        wait(pe, back_ready, s)
                        nc.tensor.matmul(ps_b[:, :], ones[:, :], diag1[:, :, :].rearrange("p i t -> p (i t)"),
                                         start=True, stop=True).then_inc(back_done, 1)
                    if f < 2 and live(last, n):
                        pe.wait_ge(hq_ready, FC * last + FC)
                        for i in (2 * f, 2 * f + 1):
                            if isinstance(s, int) or f == 1:
                                wait(pe, x_updated, G * last + i - 1)
                            for k in range(FC):
                                mm = nc.tensor.matmul(ps_o[i % 2][:, 0:E], hq[:, par, k, i * P:(i + 1) * P],
                                                      w2[:, k, :], start=(k == 0), stop=(k == FC - 1))
                            mm.then_inc(o_done, 1)
            tile_steps(pe, step, n=n, lag=4)


class Constants:
    pass


def kernel_program(nc, d, out):
    with ExitStack() as ctx:
        ph = Phase(nc, ctx, "g")
        X = ph.sb("x", [P, NT, E])
        c = Constants()
        c.ident = ph.sb("ident", [P, P])
        c.head_mask = ph.sb("head_mask", [P, HG])
        c.minus_half = ph.sb("minus_half", [P, 1])
        c.loaded, c.n_loads = ph.sem("const_loaded"), 3
        x_loaded = [ph.sem(f"x_loaded{i}") for i in range(4)]
        stored = ph.sem("stored")
        c.passed_dve, c.passed_pool = ph.sem("passed_dve"), ph.sem("passed_pool")
        with nc.Block() as block:
            @block.sync
            def _(sp):
                q = NT // 4
                for i in range(4):
                    sp.dma_start(X[:, i * q:(i + 1) * q, :],
                                 d["x"].rearrange("t p e -> p t e")[:, i * q:(i + 1) * q, :]).then_inc(x_loaded[i], 16)

            @block.scalar
            def _(act):
                act.dma_start(c.ident[:, :], d["ident"]).then_inc(c.loaded, 16)
                act.dma_start(c.head_mask[:, :], d["head_mask"]).then_inc(c.loaded, 16)
                act.dma_start(c.minus_half[:, :], d["minus_half"]).then_inc(c.loaded, 16)

            @block.gpsimd
            def _(pool):
                pool.wait_ge(c.loaded, 16 * c.n_loads)
        c.xn_dram = nc.dram_tensor("xn_rows", [NT, P, E], F32).ap()
        c.xg_dram = nc.dram_tensor("expert_rows", [NS * P, E], F32).ap()
        c.y_dram = nc.dram_tensor("expert_outs", [NS * P, E], F32).ap()
        c.zeroed = ph.sem("zeroed")
        cross_attention_0(nc, c, X, d, x_loaded)
        causal_attention(nc, c, X, d, 0)
        with ExitStack() as moe:
            mp = Phase(nc, moe, "moe")
            c.slot = mp.sb("slot", [P, NT, TOP], I32)
            c.weight = mp.sb("weight", [P, NT, TOP])
            c.owner = mp.sb("owner", [1, NS], I32)
            c.moe_loaded = mp.sem("loaded")
            route(nc, c, X, d)
            with ExitStack() as weights:
                wp = Phase(nc, weights, "moew")
                c.w1 = wp.sb("w1", [P, NE, KC, 2 * E])
                c.w2 = wp.sb("w2", [P, NE, KC, E])
                shared_expert(nc, c, X, d)
                experts(nc, c, d)
            cross_attention_1(nc, c, X, d)
        causal_attention(nc, c, X, d, 1)
        feed_forward(nc, c, X, d)
        with nc.Block() as block:
            @block.sync
            def _(sp):
                sp.dma_start(out.rearrange("t p e -> p t e"), X[:, :, :]).then_inc(stored, 16)
                sp.wait_ge(stored, 16)


def laid_out(i):
    f = {k: np.asarray(v) for k, v in i.items()}
    c = np.ascontiguousarray

    def rows(w):
        return c(w.reshape(w.shape[0] // P, P, -1).transpose(1, 0, 2))

    pair = lambda w: c(w.reshape(H // 2, 2, D, -1).transpose(0, 2, 1, 3).reshape(P, 2, -1))
    q, k = np.arange(P)[:, None], np.arange(P)[None, :]
    in_order = (q // T == k // T) & (k <= q)
    pad = f["mask_BxS2_bf0"]
    return {
        "x": c(f["x"].reshape(NT, P, E)),
        "ctxT": c(f["ctx_1024"].reshape(NT, 2 * S, KC, P).transpose(0, 3, 2, 1)),
        "ctx_rows": c(f["ctx_1024"].reshape(NT, SC, P, E).transpose(0, 2, 1, 3)),
        "attn_mask": f["fside_SxS2_0"],
        "pad": c(pad.reshape(1, B, S)),
        "padT": c(pad.reshape(NT, SC, P).transpose(2, 0, 1)),
        "xa_wqT": rows(f["L0_xattn_Wq"].T), "xa_wkT": rows(f["L0_xattn_Wk"].T), "xa_wvT": rows(f["L0_xattn_Wv"].T),
        "xa_woP": pair(f["L0_xattn_Wo"].T),
        "xa_bq": c(f["L0_xattn_bq"].reshape(KC, P).T), "xa_bk": c(f["L0_xattn_bk"].reshape(KC, P).T),
        "xa_bvP": c(pair(f["L0_xattn_bv"][:, None])[:, :, 0]),
        "xa_bo": c(f["L0_xattn_bo"].reshape(1, E)),
        "sa0_wqkvT": rows(np.concatenate([f["L0_attn_Wq"].T, f["L0_attn_Wk"].T, f["L0_attn_Wv"].T], 1)),
        "sa0_woT": rows(f["L0_attn_Wo"].T),
        "sa0_mask": c(np.where(in_order.T, 0.5, 0.0).astype(np.float32)),
        "sa1_wqkvT": rows(f["L1_attn_Wqkv"].T), "sa1_woT": rows(f["L1_attn_Wout"].T),
        "sa1_mask": np.where(in_order, 0.0, MASKED).astype(np.float32),
        "sa1_bo": c(f["L1_attn_bout"].reshape(1, E)),
        "rt_w": rows(f["L0_ffn_router_w"].T), "rt_bias": c(f["L0_ffn_bias"].reshape(1, NE)),
        "rt_before": np.tile((np.arange(NG)[None, :] < np.arange(NG)[:, None]).reshape(1, -1), (P, 1)).astype(np.float32),
        "rt_upper": (q < k).astype(np.float32), "rt_ones": np.ones((P, P), np.float32),
        "rt_count16": np.tile(np.arange(NE, dtype=np.float32), (P, 1)),
        "rt_count_tiles": np.arange(NS, dtype=np.float32)[None],
        "rt_carry": np.tile((np.arange(NT) > 0).astype(np.float32), (P, NE, 1)),
        "sh_wg": rows(f["L0_ffn_sh_gate_w"]), "sh_wu": rows(f["L0_ffn_sh_up_w"]), "sh_wd": rows(f["L0_ffn_sh_down_w"]),
        "moe_w1": c(np.concatenate([f["L0_ffn_gate_w"], f["L0_ffn_up_w"]], 2)
                    .reshape(NE, KC, P, 2 * E).transpose(2, 0, 1, 3)),
        "moe_w2": c(f["L0_ffn_down_w"].reshape(NE, KC, P, E).transpose(2, 0, 1, 3)),
        "ff_w1T": rows(f["L1_ffn_w1"].T), "ff_w2T": rows(f["L1_ffn_w2"].T),
        "ff_cw": rows(f["L1_ffn_conv_w"].reshape(-1, 3)), "ff_cb": rows(f["L1_ffn_conv_b"].reshape(-1, 1))[:, :, 0],
        "ident": np.eye(P, dtype=np.float32),
        "head_mask": (np.arange(P)[:, None] // D == np.arange(HG)[None, :]).astype(np.float32),
        "minus_half": np.full((P, 1), -0.5, np.float32),
    }


def kernel(**inputs):
    import concourse.bacc as bacc
    from concourse.bass_utils import run_bass_kernel_spmd

    nc = bacc.Bacc("TRN2", target_bir_lowering=False, num_devices=1)
    arrays = {f"in_{name}_dram": a for name, a in laid_out(inputs).items()}
    d = {name[3:-5]: nc.dram_tensor(name, a.shape, mybir.dt.from_np(a.dtype), kind="ExternalInput").ap()
         for name, a in arrays.items()}
    out = nc.dram_tensor("out_dram", (NT, P, E), F32, kind="ExternalOutput").ap()
    kernel_program(nc, d, out)
    result = run_bass_kernel_spmd(nc, [arrays], core_ids=[0])
    return result.results[0]["out_dram"].reshape(B, T, E)
```
